# Optimizing a Trainium2 kernel written in Bass

```python
import numpy as np
import jax
import jax.numpy as jnp

def _softmax(x, axis=-1):
    return jax.nn.softmax(x, axis=axis)

def _gelu(x):
    return jax.nn.gelu(x, approximate=True)

def _silu(x):
    return jax.nn.silu(x)

def _sigmoid(x):
    return jax.nn.sigmoid(x)

def _layernorm(x, axis=-1, eps=1e-05):
    m = jnp.mean(x, axis=axis, keepdims=True)
    v = jnp.var(x, axis=axis, keepdims=True)
    return (x - m) / jnp.sqrt(v + eps)

def _scatter_add(tgt, idx, src, axis=0):
    return tgt.at[idx].add(src)

def _segment_sum(src, seg, n):
    return jax.ops.segment_sum(src, seg, n)
kernel_name = 'mk_flamingo_gated_d4_seqx_r8_61ed3b'

def setup_inputs(seed: int=0):
    np.random.seed(seed)
    _w = jnp.asarray

    def _rec_inputs():
        import jax
        import jax.numpy as jnp
        _rk = jax.random.key(seed)
        x = 7.22e-05 + 1 * jax.random.normal(jax.random.fold_in(_rk, 1), (32, 64, 512), jnp.float32)
        _lenS = 64 - jax.random.randint(jax.random.fold_in(_rk, 7), (32,), 0, max(1, 64 // 4) + 1, jnp.int32)
        _lenS2 = 64 - jax.random.randint(jax.random.fold_in(_rk, 8), (32,), 0, max(1, 64 // 4) + 1, jnp.int32)
        _ctx_4096P = jax.random.normal(jax.random.fold_in(_rk, 11), (32, 16, 512), jnp.float32)
        _ctx_4096c = jax.random.dirichlet(jax.random.fold_in(_rk, 511), 0.3 * jnp.ones((16,), jnp.float32), (32, 64))
        _ctx_4096t = jnp.einsum('bsk,bkd->bsd', _ctx_4096c, _ctx_4096P)
        _ctx_4096t = _ctx_4096t * jax.lax.rsqrt(jnp.mean(jnp.square(_ctx_4096t)) + 1e-12) * 0.953939
        ctx_4096 = 4.13588e-05 + 0.999923 * (_ctx_4096t + 0.3 * jax.random.normal(jax.random.fold_in(_rk, 611), (32, 64, 512), jnp.float32))
        pos_BxS2 = jnp.broadcast_to(jnp.arange(64, dtype=jnp.int32), (32, 64))
        _validS = jnp.arange(64)[None, :] < _lenS[:, None]
        _validS2 = jnp.arange(64)[None, :] < _lenS2[:, None]
        _causal = jnp.tril(jnp.ones((64, 64), dtype=bool))
        mask_BxSxS2_ik0 = jnp.where(jnp.broadcast_to(_validS2[:, None, :], (32, 64, 64)), 0, 1).astype(jnp.int32)
        _g = jax.random.normal(jax.random.fold_in(_rk, 9001), (2, 4), jnp.float32)
        _g = jnp.sign(_g) * jnp.maximum(jnp.abs(_g), 1.0) + (_g == 0) * 1.0
        g_xattn = _g[0]
        g_ffn = _g[1]
        return (x, ctx_4096, pos_BxS2, mask_BxSxS2_ik0, g_xattn, g_ffn)
    x, ctx_4096, pos_BxS2, mask_BxSxS2_ik0, g_xattn, g_ffn = _rec_inputs()

    def _L0_xattn_setup():
        import jax, jax.numpy as jnp
        import numpy as np
        HEADS = 8
        WINDOW = 16

        def _pointwise(W, b, t):
            return jnp.einsum('oc,bct->bot', W, t) + b[None, :, None]
        key = jax.random.key(seed)
        ks = jax.random.split(key, 10)
        B, C, T = (4, 64, 512)
        s = 0.02
        return {'x': jax.random.normal(ks[0], (B, C, T), jnp.float32), 'cond': jax.random.normal(ks[1], (B, C, T), jnp.float32), 'Wq': jax.random.normal(ks[2], (C, C), jnp.float32) * s, 'bq': jnp.zeros((C,), jnp.float32), 'Wk': jax.random.normal(ks[3], (C, C), jnp.float32) * s, 'bk': jnp.zeros((C,), jnp.float32), 'Wv': jax.random.normal(ks[4], (C, C), jnp.float32) * s, 'bv': jnp.zeros((C,), jnp.float32), 'Wo': jax.random.normal(ks[5], (C, C), jnp.float32) * s, 'bo': jnp.zeros((C,), jnp.float32)}
    _L0_xattn_all = _L0_xattn_setup()
    _L0_xattn_in = {k: v for k, v in _L0_xattn_all.items() if k in ('Wq', 'bq', 'Wk', 'bk', 'Wv', 'bv', 'Wo', 'bo')}
    del _L0_xattn_all

    def _L0_ffn_setup():
        import jax, jax.numpy as jnp
        import numpy as np
        B_, S, D = (4, 512, 512)
        E, R, O = (8, 16, 512)
        TOP_K = 2
        SCALING = 8.0 / R
        key = jax.random.key(seed)
        ks = jax.random.split(key, 5)
        x = jax.random.normal(ks[0], (B_, S, D), dtype=jnp.float32)
        router_w = jax.random.normal(ks[1], (E, D), dtype=jnp.float32) * (1.0 / np.sqrt(D))
        router_b = jax.random.normal(ks[2], (E,), dtype=jnp.float32) * 0.01
        A = jax.random.normal(ks[3], (E, R, D), dtype=jnp.float32) * (1.0 / np.sqrt(D))
        Bm = jax.random.normal(ks[4], (E, O, R), dtype=jnp.float32) * 0.02
        return {'x': x, 'router_w': router_w, 'router_b': router_b, 'A': A, 'Bm': Bm}
    _L0_ffn_all = _L0_ffn_setup()
    _L0_ffn_in = {k: v for k, v in _L0_ffn_all.items() if k in ('router_w', 'router_b', 'A', 'Bm')}
    del _L0_ffn_all

    def _L1_xattn_setup():
        import jax, jax.numpy as jnp
        import numpy as np
        B, S, E = (2, 256, 512)
        H, KVH, D = (32, 8, 128)
        GROUPS = H // KVH
        MAX_POS = 512
        ROPE_THETA = 10000.0

        def _rope_tables(max_pos, dim, theta):
            inv_freq = 1.0 / theta ** (jnp.arange(0, dim, 2, dtype=jnp.float32) / dim)
            t = jnp.arange(max_pos, dtype=jnp.float32)
            freqs = jnp.einsum('i,j->ij', t, inv_freq)
            emb = jnp.concatenate([freqs, freqs], axis=-1)
            return (jnp.cos(emb), jnp.sin(emb))

        def _rotate_half(x):
            x1, x2 = (x[..., :x.shape[-1] // 2], x[..., x.shape[-1] // 2:])
            return jnp.concatenate([-x2, x1], axis=-1)
        key = jax.random.key(seed)
        ks = jax.random.split(key, 8)
        scale_w = 1.0 / np.sqrt(E)
        query = jax.random.normal(ks[0], (B, S, E), dtype=jnp.float32)
        k_in = jax.random.normal(ks[1], (B, S, E), dtype=jnp.float32)
        v_in = jax.random.normal(ks[2], (B, S, E), dtype=jnp.float32)
        position_ids = jnp.broadcast_to(jnp.arange(S, dtype=jnp.int64), (B, S))
        src_mask = jnp.tril(jnp.ones((S, S), dtype=jnp.int32))
        src_mask = jnp.broadcast_to(src_mask, (B, S, S))
        Wq = jax.random.normal(ks[3], (E, H * D), dtype=jnp.float32) * scale_w
        Wk = jax.random.normal(ks[4], (E, KVH * D), dtype=jnp.float32) * scale_w
        Wv = jax.random.normal(ks[5], (E, KVH * D), dtype=jnp.float32) * scale_w
        Wo = jax.random.normal(ks[6], (H * D, E), dtype=jnp.float32) * scale_w
        return {'query': query, 'key': k_in, 'value': v_in, 'position_ids': position_ids, 'src_mask': src_mask, 'Wq': Wq, 'Wk': Wk, 'Wv': Wv, 'Wo': Wo}
    _L1_xattn_all = _L1_xattn_setup()
    _L1_xattn_in = {k: v for k, v in _L1_xattn_all.items() if k in ('Wq', 'Wk', 'Wv', 'Wo')}
    del _L1_xattn_all

    def _L1_ffn_setup():
        import jax, jax.numpy as jnp
        import numpy as np
        B, T, D_IN, D_OUT = (8, 256, 512, 512)
        N_LORAS, RANK = (16, 32)
        SCALING = 1.0
        key = jax.random.key(seed)
        ks = jax.random.split(key, 8)
        std = 1.0 / D_IN ** 0.5
        x = jax.random.normal(ks[0], (B, T, D_IN), dtype=jnp.float32)
        idx = jax.random.randint(ks[1], (B,), 0, N_LORAS)
        gate = jax.nn.one_hot(idx, N_LORAS, dtype=jnp.float32)
        kernel = jax.random.normal(ks[2], (D_IN, D_OUT), dtype=jnp.float32) * std
        bias = jnp.zeros((D_OUT,), dtype=jnp.float32)
        lora_A = jax.random.normal(ks[3], (N_LORAS, RANK, D_IN), dtype=jnp.float32) * std
        lora_B = jax.random.normal(ks[4], (N_LORAS, D_OUT, RANK), dtype=jnp.float32) * 0.01
        lora_A_shared = jax.random.normal(ks[5], (RANK, D_IN), dtype=jnp.float32) * std
        lora_B_shared = jax.random.normal(ks[6], (D_OUT, RANK), dtype=jnp.float32) * 0.01
        return {'x': x, 'gate': gate, 'kernel': kernel, 'bias': bias, 'lora_A': lora_A, 'lora_B': lora_B, 'lora_A_shared': lora_A_shared, 'lora_B_shared': lora_B_shared}
    _L1_ffn_all = _L1_ffn_setup()
    _L1_ffn_in = {k: v for k, v in _L1_ffn_all.items() if k in ('gate', 'kernel', 'bias', 'lora_A', 'lora_B', 'lora_A_shared', 'lora_B_shared')}
    del _L1_ffn_all

    def _L2_xattn_setup():
        import jax, jax.numpy as jnp
        import numpy as np
        H = 8
        C = 2

        def _autocorrelation(Q, K, V):
            B, L, D = Q.shape
            d = D // H
            q = Q.reshape(B, L, H, d).transpose(0, 2, 1, 3)
            k = K.reshape(B, L, H, d).transpose(0, 2, 1, 3)
            v = V.reshape(B, L, H, d).transpose(0, 2, 1, 3)
            qf = jnp.fft.fft(q, axis=2)
            kf = jnp.fft.fft(k, axis=2)
            corr = jnp.fft.ifft(qf * jnp.conj(kf), axis=2).real
            topk = int(C * np.log(L))
            w, idx = jax.lax.top_k(corr.transpose(0, 1, 3, 2), topk)
            w = jax.nn.softmax(w, axis=-1)
            pos = jnp.arange(L)[:, None]
            out = jnp.zeros_like(v)
            for i in range(topk):
                g = jnp.minimum(idx[:, :, None, :, i] + pos, L - 1)
                out = out + w[:, :, None, :, i] * jnp.take_along_axis(v, g, axis=2)
            return out.transpose(0, 2, 1, 3).reshape(B, L, D)
        key = jax.random.key(seed)
        k1, k2, k3 = jax.random.split(key, 3)
        B, L, D = (16, 64, 512)
        Q = jax.random.normal(k1, (B, L, D), dtype=jnp.float32)
        K = jax.random.normal(k2, (B, L, D), dtype=jnp.float32)
        V = jax.random.normal(k3, (B, L, D), dtype=jnp.float32)
        return {'Q': Q, 'K': K, 'V': V}
    _L2_xattn_all = _L2_xattn_setup()
    _L2_xattn_in = {k: v for k, v in _L2_xattn_all.items() if k in ()}
    del _L2_xattn_all

    def _L2_ffn_setup():
        import jax, jax.numpy as jnp
        import numpy as np
        FP8_MAX = 448.0
        IN_F, OUT_F = (512, 512)
        key = jax.random.key(seed)
        kx, kw, kb = jax.random.split(key, 3)
        x = jax.random.normal(kx, (4, 256, IN_F), dtype=jnp.float32)
        w = jax.random.normal(kw, (OUT_F, IN_F), dtype=jnp.float32) * 0.02
        amax = jnp.max(jnp.abs(w))
        weight_scale = jnp.where(amax > 0, amax / FP8_MAX, 1.0).astype(jnp.float32)
        weight_fp8 = jnp.clip(w / weight_scale, -FP8_MAX, FP8_MAX).astype(jnp.float8_e4m3fn)
        bias = (jax.random.normal(kb, (OUT_F,), dtype=jnp.float32) * 0.01).astype(jnp.bfloat16)
        return {'x': x, 'weight_fp8': weight_fp8, 'weight_scale': weight_scale, 'bias': bias}
    _L2_ffn_all = _L2_ffn_setup()
    _L2_ffn_in = {k: v for k, v in _L2_ffn_all.items() if k in ('weight_fp8', 'weight_scale', 'bias')}
    del _L2_ffn_all

    def _L3_xattn_setup():
        import jax, jax.numpy as jnp
        import numpy as np
        B, N, NKV = (2, 256, 256)
        E = 512
        H = 16
        HD = E // H
        LQ = E // 8
        LKV = E // 16
        key = jax.random.key(seed)
        ks = jax.random.split(key, 6)
        Q = jax.random.normal(ks[0], (B, N, E), dtype=jnp.float32)
        K = jax.random.normal(ks[1], (B, NKV, E), dtype=jnp.float32)
        Wq_d = jax.random.normal(ks[2], (E, LQ), dtype=jnp.float32) / np.sqrt(E)
        W_qk = jax.random.normal(ks[3], (LQ, H * LKV), dtype=jnp.float32) / np.sqrt(LQ)
        Wkv_d = jax.random.normal(ks[4], (E, LKV), dtype=jnp.float32) / np.sqrt(E)
        Wv_u = jax.random.normal(ks[5], (LKV, H * HD), dtype=jnp.float32) / np.sqrt(LKV)
        return {'Q': Q, 'K': K, 'Wq_d': Wq_d, 'W_qk': W_qk, 'Wkv_d': Wkv_d, 'Wv_u': Wv_u}
    _L3_xattn_all = _L3_xattn_setup()
    _L3_xattn_in = {k: v for k, v in _L3_xattn_all.items() if k in ('Wq_d', 'W_qk', 'Wkv_d', 'Wv_u')}
    del _L3_xattn_all

    def _L3_ffn_setup():
        import jax, jax.numpy as jnp
        import numpy as np
        D_MODEL = 512
        D_HIDDEN = 1376
        RANK = 16
        BATCH, SEQ = (2, 256)

        def _matmul_lora(x, w, a, b, scale=1.0):
            out = jnp.einsum('bsd,hd->bsh', x, w)
            out = out + jnp.einsum('bsr,hr->bsh', jnp.einsum('bsd,rd->bsr', x, a), b) * scale
            return out
        key = jax.random.key(seed)
        ks = jax.random.split(key, 10)
        s = 0.02
        return {'x': jax.random.normal(ks[0], (BATCH, SEQ, D_MODEL), jnp.float32), 'gate_w': jax.random.normal(ks[1], (D_HIDDEN, D_MODEL), jnp.float32) * s, 'up_w': jax.random.normal(ks[2], (D_HIDDEN, D_MODEL), jnp.float32) * s, 'down_w': jax.random.normal(ks[3], (D_MODEL, D_HIDDEN), jnp.float32) * s, 'gate_a': jax.random.normal(ks[4], (RANK, D_MODEL), jnp.float32) * s, 'gate_b': jax.random.normal(ks[5], (D_HIDDEN, RANK), jnp.float32) * s, 'up_a': jax.random.normal(ks[6], (RANK, D_MODEL), jnp.float32) * s, 'up_b': jax.random.normal(ks[7], (D_HIDDEN, RANK), jnp.float32) * s, 'down_a': jax.random.normal(ks[8], (RANK, D_HIDDEN), jnp.float32) * s, 'down_b': jax.random.normal(ks[9], (D_MODEL, RANK), jnp.float32) * s}
    _L3_ffn_all = _L3_ffn_setup()
    _L3_ffn_in = {k: v for k, v in _L3_ffn_all.items() if k in ('gate_w', 'up_w', 'down_w', 'gate_a', 'gate_b', 'up_a', 'up_b', 'down_a', 'down_b')}
    del _L3_ffn_all
    return {'x': x, 'ctx_4096': ctx_4096, 'pos_BxS2': pos_BxS2, 'mask_BxSxS2_ik0': mask_BxSxS2_ik0, 'g_xattn': g_xattn, 'g_ffn': g_ffn, 'L0_xattn_Wq': _L0_xattn_in['Wq'], 'L0_xattn_bq': _L0_xattn_in['bq'], 'L0_xattn_Wk': _L0_xattn_in['Wk'], 'L0_xattn_bk': _L0_xattn_in['bk'], 'L0_xattn_Wv': _L0_xattn_in['Wv'], 'L0_xattn_bv': _L0_xattn_in['bv'], 'L0_xattn_Wo': _L0_xattn_in['Wo'], 'L0_xattn_bo': _L0_xattn_in['bo'], 'L0_ffn_router_w': _L0_ffn_in['router_w'], 'L0_ffn_router_b': _L0_ffn_in['router_b'], 'L0_ffn_A': _L0_ffn_in['A'], 'L0_ffn_Bm': _L0_ffn_in['Bm'], 'L1_xattn_Wq': _L1_xattn_in['Wq'], 'L1_xattn_Wk': _L1_xattn_in['Wk'], 'L1_xattn_Wv': _L1_xattn_in['Wv'], 'L1_xattn_Wo': _L1_xattn_in['Wo'], 'L1_ffn_gate': _L1_ffn_in['gate'], 'L1_ffn_kernel': _L1_ffn_in['kernel'], 'L1_ffn_bias': _L1_ffn_in['bias'], 'L1_ffn_lora_A': _L1_ffn_in['lora_A'], 'L1_ffn_lora_B': _L1_ffn_in['lora_B'], 'L1_ffn_lora_A_shared': _L1_ffn_in['lora_A_shared'], 'L1_ffn_lora_B_shared': _L1_ffn_in['lora_B_shared'], 'L2_ffn_weight_fp8': _L2_ffn_in['weight_fp8'], 'L2_ffn_weight_scale': _L2_ffn_in['weight_scale'], 'L2_ffn_bias': _L2_ffn_in['bias'], 'L3_xattn_Wq_d': _L3_xattn_in['Wq_d'], 'L3_xattn_W_qk': _L3_xattn_in['W_qk'], 'L3_xattn_Wkv_d': _L3_xattn_in['Wkv_d'], 'L3_xattn_Wv_u': _L3_xattn_in['Wv_u'], 'L3_ffn_gate_w': _L3_ffn_in['gate_w'], 'L3_ffn_up_w': _L3_ffn_in['up_w'], 'L3_ffn_down_w': _L3_ffn_in['down_w'], 'L3_ffn_gate_a': _L3_ffn_in['gate_a'], 'L3_ffn_gate_b': _L3_ffn_in['gate_b'], 'L3_ffn_up_a': _L3_ffn_in['up_a'], 'L3_ffn_up_b': _L3_ffn_in['up_b'], 'L3_ffn_down_a': _L3_ffn_in['down_a'], 'L3_ffn_down_b': _L3_ffn_in['down_b']}

def reference(x, ctx_4096, pos_BxS2, mask_BxSxS2_ik0, g_xattn, g_ffn, L0_xattn_Wq, L0_xattn_bq, L0_xattn_Wk, L0_xattn_bk, L0_xattn_Wv, L0_xattn_bv, L0_xattn_Wo, L0_xattn_bo, L0_ffn_router_w, L0_ffn_router_b, L0_ffn_A, L0_ffn_Bm, L1_xattn_Wq, L1_xattn_Wk, L1_xattn_Wv, L1_xattn_Wo, L1_ffn_gate, L1_ffn_kernel, L1_ffn_bias, L1_ffn_lora_A, L1_ffn_lora_B, L1_ffn_lora_A_shared, L1_ffn_lora_B_shared, L2_ffn_weight_fp8, L2_ffn_weight_scale, L2_ffn_bias, L3_xattn_Wq_d, L3_xattn_W_qk, L3_xattn_Wkv_d, L3_xattn_Wv_u, L3_ffn_gate_w, L3_ffn_up_w, L3_ffn_down_w, L3_ffn_gate_a, L3_ffn_gate_b, L3_ffn_up_a, L3_ffn_up_b, L3_ffn_down_a, L3_ffn_down_b):
    import jax
    import jax.numpy as jnp

    def _L0_xattn_ref(x, cond, Wq, bq, Wk, bk, Wv, bv, Wo, bo):
        import jax, jax.numpy as jnp
        import numpy as np
        HEADS = 8
        WINDOW = 16

        def _pointwise(W, b, t):
            return jnp.einsum('oc,bct->bot', W, t) + b[None, :, None]
        B, C, T = x.shape
        H, W = (HEADS, WINDOW)
        hd = C // H
        scale = hd ** (-0.5)
        pad_left = W // 2
        pad_right = W - pad_left - 1
        q = _pointwise(Wq, bq, x)
        k = _pointwise(Wk, bk, cond)
        v = _pointwise(Wv, bv, cond)
        k = jnp.pad(k, ((0, 0), (0, 0), (pad_left, pad_right)))
        v = jnp.pad(v, ((0, 0), (0, 0), (pad_left, pad_right)))
        idx = jnp.arange(T)[:, None] + jnp.arange(W)[None, :]
        k_win = k[:, :, idx].reshape(B, H, hd, T, W)
        v_win = v[:, :, idx].reshape(B, H, hd, T, W)
        qh = q.reshape(B, H, hd, T)
        dots = jnp.einsum('bhdt,bhdtw->bhtw', qh, k_win) * scale
        attn = jax.nn.softmax(dots, axis=-1)
        out = jnp.einsum('bhtw,bhdtw->bhdt', attn, v_win)
        out = out.reshape(B, C, T)
        return _pointwise(Wo, bo, out)

    def _L0_ffn_ref(x, router_w, router_b, A, Bm):
        import jax, jax.numpy as jnp
        import numpy as np
        B_, S, D = (4, 512, 512)
        E, R, O = (8, 16, 512)
        TOP_K = 2
        SCALING = 8.0 / R
        flat = x.reshape(-1, x.shape[-1])
        N = flat.shape[0]
        logits = flat @ router_w.T + router_b
        probs = jax.nn.softmax(logits, axis=-1)
        topv, topi = jax.lax.top_k(probs, TOP_K)
        gates = topv / jnp.sum(topv, axis=-1, keepdims=True)
        w = jnp.zeros((N, E), dtype=flat.dtype).at[jnp.arange(N)[:, None], topi].add(gates)
        h = jnp.einsum('nd,erd->ner', flat, A)
        hw = h * w[:, :, None]
        out = jnp.einsum('ner,eor->no', hw, Bm) * SCALING
        return out.reshape(*x.shape[:-1], O)

    def _L1_xattn_ref(query, key, value, position_ids, src_mask, Wq, Wk, Wv, Wo):
        import jax, jax.numpy as jnp
        import numpy as np
        B, S, E = (2, 256, 512)
        H, KVH, D = (32, 8, 128)
        GROUPS = H // KVH
        MAX_POS = 512
        ROPE_THETA = 10000.0

        def _rope_tables(max_pos, dim, theta):
            inv_freq = 1.0 / theta ** (jnp.arange(0, dim, 2, dtype=jnp.float32) / dim)
            t = jnp.arange(max_pos, dtype=jnp.float32)
            freqs = jnp.einsum('i,j->ij', t, inv_freq)
            emb = jnp.concatenate([freqs, freqs], axis=-1)
            return (jnp.cos(emb), jnp.sin(emb))

        def _rotate_half(x):
            x1, x2 = (x[..., :x.shape[-1] // 2], x[..., x.shape[-1] // 2:])
            return jnp.concatenate([-x2, x1], axis=-1)
        nb, q_len, _ = query.shape
        q = (query @ Wq).reshape(nb, q_len, H, D).transpose(0, 2, 1, 3)
        k = (key @ Wk).reshape(nb, q_len, KVH, D).transpose(0, 2, 1, 3)
        v = (value @ Wv).reshape(nb, q_len, KVH, D).transpose(0, 2, 1, 3)
        cos_t, sin_t = _rope_tables(MAX_POS, D, ROPE_THETA)
        cos = cos_t[position_ids][:, None]
        sin = sin_t[position_ids][:, None]
        q = q * cos + _rotate_half(q) * sin
        k = k * cos + _rotate_half(k) * sin
        k = jnp.repeat(k, GROUPS, axis=1)
        v = jnp.repeat(v, GROUPS, axis=1)
        scores = jnp.einsum('bhqd,bhkd->bhqk', q, k) / jnp.sqrt(jnp.float32(D))
        mask = src_mask[:, None]
        scores = jnp.where(mask == 0, jnp.float32(-1000000000.0), scores)
        attn = jax.nn.softmax(scores, axis=-1)
        x = jnp.einsum('bhqk,bhkd->bhqd', attn, v)
        x = x.transpose(0, 2, 1, 3).reshape(nb, q_len, H * D)
        return x @ Wo

    def _L1_ffn_ref(x, gate, kernel, bias, lora_A, lora_B, lora_A_shared, lora_B_shared):
        import jax, jax.numpy as jnp
        import numpy as np
        B, T, D_IN, D_OUT = (8, 256, 512, 512)
        N_LORAS, RANK = (16, 32)
        SCALING = 1.0
        base_out = jnp.matmul(x, kernel) + bias
        b = gate.shape[0]
        x_flat = x.reshape(b, -1, x.shape[-1])
        A_eff = jnp.einsum('bn,nri->bri', gate, lora_A)
        B_eff = jnp.einsum('bn,nor->bor', gate, lora_B)
        Ax = jnp.einsum('bri,bti->btr', A_eff, x_flat)
        delta_flat = jnp.einsum('bor,btr->bto', B_eff, Ax)
        Ax_s = jnp.einsum('ri,bti->btr', lora_A_shared, x_flat)
        delta_flat = delta_flat + jnp.einsum('or,btr->bto', lora_B_shared, Ax_s)
        delta = delta_flat.reshape(x.shape[:-1] + (kernel.shape[-1],))
        return base_out + (SCALING * delta).astype(base_out.dtype)

    def _L2_xattn_ref(Q, K, V):
        import jax, jax.numpy as jnp
        import numpy as np
        H = 8
        C = 2

        def _autocorrelation(Q, K, V):
            B, L, D = Q.shape
            d = D // H
            q = Q.reshape(B, L, H, d).transpose(0, 2, 1, 3)
            k = K.reshape(B, L, H, d).transpose(0, 2, 1, 3)
            v = V.reshape(B, L, H, d).transpose(0, 2, 1, 3)
            qf = jnp.fft.fft(q, axis=2)
            kf = jnp.fft.fft(k, axis=2)
            corr = jnp.fft.ifft(qf * jnp.conj(kf), axis=2).real
            topk = int(C * np.log(L))
            w, idx = jax.lax.top_k(corr.transpose(0, 1, 3, 2), topk)
            w = jax.nn.softmax(w, axis=-1)
            pos = jnp.arange(L)[:, None]
            out = jnp.zeros_like(v)
            for i in range(topk):
                g = jnp.minimum(idx[:, :, None, :, i] + pos, L - 1)
                out = out + w[:, :, None, :, i] * jnp.take_along_axis(v, g, axis=2)
            return out.transpose(0, 2, 1, 3).reshape(B, L, D)
        return _autocorrelation(Q, K, V)

    def _L2_ffn_ref(x, weight_fp8, weight_scale, bias):
        import jax, jax.numpy as jnp
        import numpy as np
        FP8_MAX = 448.0
        IN_F, OUT_F = (512, 512)
        orig_shape = x.shape
        x2d = x.reshape(-1, orig_shape[-1])
        amax = jnp.max(jnp.abs(x2d))
        x_scale = jnp.maximum(amax.astype(jnp.float32) / FP8_MAX, 1e-12)
        x_fp8 = jnp.clip(x2d.astype(jnp.float32) / x_scale, -FP8_MAX, FP8_MAX).astype(jnp.float8_e4m3fn)
        acc = jnp.einsum('mk,nk->mn', x_fp8.astype(jnp.float32), weight_fp8.astype(jnp.float32))
        out = (acc * (x_scale * weight_scale)).astype(jnp.bfloat16)
        out = out + bias
        return out.reshape(*orig_shape[:-1], bias.shape[0])

    def _L3_xattn_ref(Q, K, Wq_d, W_qk, Wkv_d, Wv_u):
        import jax, jax.numpy as jnp
        import numpy as np
        B, N, NKV = (2, 256, 256)
        E = 512
        H = 16
        HD = E // H
        LQ = E // 8
        LKV = E // 16
        b, n, _ = Q.shape
        nkv = K.shape[1]
        C_q = Q @ Wq_d
        C_kv = K @ Wkv_d
        CqWqk = (C_q @ W_qk).reshape(b, n, H, LKV)
        scores = jnp.einsum('bnhl,bkl->bhnk', CqWqk, C_kv) / jnp.sqrt(jnp.asarray(LKV, dtype=Q.dtype))
        attn = jax.nn.softmax(scores, axis=-1)
        V_up = (C_kv @ Wv_u).reshape(b, nkv, H, HD)
        out = jnp.einsum('bhnk,bkhd->bnhd', attn, V_up)
        return out.reshape(b, n, H * HD)

    def _L3_ffn_ref(x, gate_w, up_w, down_w, gate_a, gate_b, up_a, up_b, down_a, down_b):
        import jax, jax.numpy as jnp
        import numpy as np
        D_MODEL = 512
        D_HIDDEN = 1376
        RANK = 16
        BATCH, SEQ = (2, 256)

        def _matmul_lora(x, w, a, b, scale=1.0):
            out = jnp.einsum('bsd,hd->bsh', x, w)
            out = out + jnp.einsum('bsr,hr->bsh', jnp.einsum('bsd,rd->bsr', x, a), b) * scale
            return out
        gate = _matmul_lora(x, gate_w, gate_a, gate_b)
        up = _matmul_lora(x, up_w, up_a, up_b)
        hidden = jax.nn.silu(gate) * up
        out = _matmul_lora(hidden, down_w, down_a, down_b)
        return out
    x = x + jnp.tanh(g_xattn[0]) * _L0_xattn_ref(_layernorm(x, axis=-1), ctx_4096, L0_xattn_Wq, L0_xattn_bq, L0_xattn_Wk, L0_xattn_bk, L0_xattn_Wv, L0_xattn_bv, L0_xattn_Wo, L0_xattn_bo)
    x = x + jnp.tanh(g_ffn[0]) * _L0_ffn_ref(_layernorm(x, axis=-1), L0_ffn_router_w, L0_ffn_router_b, L0_ffn_A, L0_ffn_Bm)
    x = x + jnp.tanh(g_xattn[1]) * _L1_xattn_ref(_layernorm(x, axis=-1), ctx_4096, ctx_4096, pos_BxS2, mask_BxSxS2_ik0, L1_xattn_Wq, L1_xattn_Wk, L1_xattn_Wv, L1_xattn_Wo)
    x = x + jnp.tanh(g_ffn[1]) * _L1_ffn_ref(_layernorm(x, axis=-1), L1_ffn_gate, L1_ffn_kernel, L1_ffn_bias, L1_ffn_lora_A, L1_ffn_lora_B, L1_ffn_lora_A_shared, L1_ffn_lora_B_shared)
    x = x + jnp.tanh(g_xattn[2]) * _L2_xattn_ref(_layernorm(x, axis=-1), ctx_4096, ctx_4096)
    x = x + jnp.tanh(g_ffn[2]) * _L2_ffn_ref(_layernorm(x, axis=-1), L2_ffn_weight_fp8, L2_ffn_weight_scale, L2_ffn_bias)
    x = x + jnp.tanh(g_xattn[3]) * _L3_xattn_ref(_layernorm(x, axis=-1), ctx_4096, L3_xattn_Wq_d, L3_xattn_W_qk, L3_xattn_Wkv_d, L3_xattn_Wv_u)
    x = x + jnp.tanh(g_ffn[3]) * _L3_ffn_ref(_layernorm(x, axis=-1), L3_ffn_gate_w, L3_ffn_up_w, L3_ffn_down_w, L3_ffn_gate_a, L3_ffn_gate_b, L3_ffn_up_a, L3_ffn_up_b, L3_ffn_down_a, L3_ffn_down_b)
    return x

_drawn_inputs = setup_inputs


def setup_inputs(seed=0):
    import zlib

    import numpy as np

    out = dict(_drawn_inputs(seed))
    spreads = {'L0_xattn_bq': (0.0, 0.8),
     'L0_xattn_bk': (0.0, 2.0),
     'L0_xattn_bv': (0.0, 0.8),
     'L0_xattn_bo': (0.0, 0.8),
     'L1_ffn_bias': (0.0, 0.1)}
    factors = {'g_ffn': 28.312,
     'L0_xattn_Wq': 8.0,
     'L0_xattn_Wk': 8.0,
     'L0_xattn_Wv': 8.0,
     'L0_xattn_Wo': 8.0,
     'L0_ffn_router_w': 4.285,
     'L0_ffn_router_b': 28.957,
     'L0_ffn_A': 3.69,
     'L0_ffn_Bm': 3.723,
     'L2_ffn_bias': 8.0,
     'L3_ffn_gate_a': 8.0,
     'L3_ffn_gate_b': 8.0,
     'L3_ffn_up_a': 8.0,
     'L3_ffn_up_b': 8.0,
     'L3_ffn_down_a': 8.0,
     'L3_ffn_down_b': 8.0}
    for name, (base, spread) in spreads.items():
        noise = np.random.default_rng([zlib.crc32(name.encode()), seed]).standard_normal(out[name].shape)
        drawn = base * np.exp(spread * noise) if base else spread * noise
        out[name] = jnp.asarray(drawn.astype(out[name].dtype))
    for name, factor in factors.items():
        out[name] = (out[name] * factor).astype(out[name].dtype)
    return out
```

```python
from contextlib import ExitStack

import concourse.bass as bass
import numpy as np
from concourse import mybir

F32 = mybir.dt.float32
BF16 = mybir.dt.bfloat16
I32 = mybir.dt.int32
U32 = mybir.dt.uint32
U8 = mybir.dt.uint8
ALU = mybir.AluOpType
ACT = mybir.ActivationFunctionType
X = mybir.AxisListType.X
RMAX = bass.bass_isa.ReduceOp.max

B, S, D = 32, 64, 512
P = 128
PAIRS = B * S // P
KT = D // P
EPS = 1e-5
TURNS = PAIRS // 2


def at(j, per, k):
    return j * per + k


def overlapped(ap, step, count, width):
    part = ap.ap[0]
    return bass.AP(tensor=ap.tensor, offset=ap.offset, ap=[list(part), [step, count], [1, width]])


def spread(ap, count):
    return ap.unsqueeze(len(ap.shape)).to_broadcast([*ap.shape, count])


class Stage:

    def __init__(self, nc, name):
        self.nc, self.name, self.ctx, self.used = nc, name, ExitStack(), []

    def __enter__(self):
        self.ctx.__enter__()
        return self

    def __exit__(self, *e):
        self.nc.clear_and_free_semaphores(self.used)
        self.nc.all_engine_barrier()
        return self.ctx.__exit__(*e)

    def sb(self, name, shape, dt=F32):
        return self.ctx.enter_context(self.nc.sbuf_tensor(f"{self.name}_{name}", shape, dt))

    def ps(self, name, shape, dt=F32):
        return self.ctx.enter_context(self.nc.psum_tensor(f"{self.name}_{name}", shape, dt))

    def sem(self, name):
        self.used.append(self.nc.alloc_semaphore(f"{self.name}_{name}"))
        return self.used[-1]

    def sems(self, name, n=2):
        return [self.sem(f"{name}{u}") for u in range(n)]


class Chain:

    def __init__(self, eng, sem, turn=0, per=0):
        self.eng, self.sem, self.base, self.per, self.n = eng, sem, turn * per, per, 0

    def step(self, ins):
        self.n += 1
        ins.then_inc(self.sem, 1)
        self.eng.wait_ge(self.sem, self.base + self.n)

    def end(self):
        assert self.n == self.per, (self.n, self.per)


class Core:

    def __init__(self, nc, ctx):
        def sb(name, shape, dt=F32):
            return ctx.enter_context(nc.sbuf_tensor(name, shape, dt))

        self.nc = nc
        self.x = sb("x_sb", [P, PAIRS, D])
        self.stats = sb("ln_stats", [P, PAIRS, 6])
        self.mv = sb("ln_mean_var", [P, PAIRS, 2])
        self.rstd = sb("ln_rstd", [P, PAIRS])
        self.shift = sb("ln_shift", [P, PAIRS])
        self.t1 = sb("ln_t1", [P, PAIRS])
        self.gate = sb("tanh_gates", [P, 8])
        self.ident = sb("ident", [P, P])
        self.identb = sb("ident_bf", [P, P], BF16)


def rows_of(ap):
    return ap.rearrange("(i b) s d -> (b s) i d", b=2)


def load_stage(c, x, g_xattn, g_ffn):
    nc = c.nc
    with Stage(nc, "load") as s:
        x_in, g_in, id_set, ids, stats = s.sem("x_in"), s.sem("g_in"), s.sem("id_set"), s.sem("ids"), s.sem("stats")
        g_raw = s.sb("g_raw", [P, 8])
        tanh_done = s.sem("tanh")
        with nc.Block() as block:
            @block.sync
            def _(sp):
                sp.dma_start(g_raw[:, 0:4], g_xattn.rearrange("(o n) -> o n", o=1).to_broadcast([P, 4])).then_inc(g_in, 16)
                sp.dma_start(g_raw[:, 4:8], g_ffn.rearrange("(o n) -> o n", o=1).to_broadcast([P, 4])).then_inc(g_in, 16)
                for q in range(4):
                    sp.dma_start(c.x[:, 4 * q:4 * q + 4, :], rows_of(x)[:, 4 * q:4 * q + 4, :]).then_inc(x_in, 16)

            @block.gpsimd
            def _(pool):
                pool.memset(c.ident[:, :], 0.0).then_inc(id_set, 1)
                pool.memset(c.identb[:, :], 0.0).then_inc(id_set, 1)
                pool.wait_ge(id_set, 2)
                for m in (c.ident, c.identb):
                    pool.affine_select(out=m[:, :], in_=m[:, :], compare_op=ALU.not_equal, fill=1.0,
                                       base=0, pattern=[[-1, P]], channel_multiplier=1).then_inc(ids, 1)

            @block.scalar
            def _(act):
                act.wait_ge(g_in, 32)
                act.activation(c.gate[:, :], g_raw[:, :], ACT.Tanh).then_inc(tanh_done, 1)

            @block.vector
            def _(dve):
                for i in range(PAIRS):
                    if i == 0:
                        dve.wait_ge(x_in, 64)
                    dve.bn_stats(c.stats[:, i, :], c.x[:, i, :]).then_inc(stats, 1)


def norm_stage(c, name):
    nc = c.nc
    with Stage(nc, name) as s:
        aggr, var_ready, root_ready, chain = s.sem("aggr"), s.sem("var"), s.sem("root"), s.sem("chain")
        var, root, t = s.sb("var", [P, PAIRS]), s.sb("root", [P, PAIRS]), s.sb("t", [P, PAIRS])
        with nc.Block() as block:
            @block.vector
            def _(dve):
                for i in range(PAIRS):
                    dve.bn_aggr(c.mv[:, i, :], c.stats[:, i, :]).then_inc(aggr, 1)
                dve.wait_ge(aggr, PAIRS)
                dve.tensor_scalar(var[:, :], c.mv[:, :, 1], EPS, None, ALU.add).then_inc(var_ready, 1)
                dve.wait_ge(root_ready, 1)
                dve.wait_ge(var_ready, 1)
                ch = Chain(dve, chain)
                ch.step(dve.reciprocal(c.rstd[:, :], root[:, :]))
                ch.step(dve.tensor_tensor(t[:, :], c.rstd[:, :], c.rstd[:, :], ALU.mult))
                ch.step(dve.tensor_tensor(t[:, :], t[:, :], var[:, :], ALU.mult))
                ch.step(dve.tensor_scalar(t[:, :], t[:, :], -0.5, 1.5, ALU.mult, ALU.add))
                ch.step(dve.tensor_tensor(c.rstd[:, :], c.rstd[:, :], t[:, :], ALU.mult))
                ch.step(dve.scalar_tensor_tensor(out=c.shift[:, :], in0=c.mv[:, :, 0], scalar=-1.0,
                                                 in1=c.rstd[:, :], op0=ALU.mult, op1=ALU.mult))

            @block.scalar
            def _(act):
                act.wait_ge(var_ready, 1)
                act.activation(root[:, :], var[:, :], ACT.Sqrt).then_inc(root_ready, 1)


def normalised(c, dve, out, t):
    t = bass.ds(t, 1)
    return dve.tensor_scalar(out, c.x[:, t, :].rearrange("p o d -> p (o d)"), c.rstd[:, t], c.shift[:, t], ALU.mult, ALU.add)


def need(eng, sem, value):
    if not isinstance(value, int) or value > 0:
        eng.wait_ge(sem, value)


def pipelined(eng, step, first, last, count=PAIRS):
    lo = -first + (-first) % 2
    hi = count - last
    hi -= (hi - lo) % 2

    def alone(v):
        step(v, v % 2, lambda off: 0 <= v + off < count)

    for v in range(-last, lo):
        alone(v)
    with eng.Fori(0, (hi - lo) // 2) as j:
        for par in range(2):
            step(2 * j + (lo + par), par, lambda off: True)
    for v in range(hi, count - first):
        alone(v)


WINDOW, HEADS0, HD0 = 16, 8, 8
PAD_L, PAD_R = WINDOW // 2, WINDOW - WINDOW // 2 - 1
BH = 2 * HEADS0
PARTS = 3


def window_attention_stage(c, ctx_in, wqT, wkT, wvT, woT, bq, bk, bv, bo, head_sums, head_spread):
    nc = c.nc
    with Stage(nc, "win") as s:
        TB = D // P
        w4 = s.sb("w4", [P, 4, P])
        bias4 = s.sb("bias4", [P, 4])
        sumw = s.sb("sumw", [P, 2, 32])
        expw = s.sb("expw", [2 * PARTS * BH, 2, P], BF16)
        expw_in = s.sb("expw_in", [2 * PARTS * BH, 2, P])
        cin = s.sb("cin", [P, 2, D])
        xn = s.sb("xn", [P, 2, D])
        q = s.sb("q", [P, 2, D])
        kp = s.sb("kp", [P, 2, D + WINDOW])
        vp = s.sb("vp", [P, 2, D + WINDOW])
        WS = 4
        prod = s.sb("prod", [P, 2, WS, D])
        dots = s.sb("dots", [P, 2, D])
        e = s.sb("e", [P, TB, WINDOW, BH])
        pr = s.sb("pr", [P, TB, WINDOW, BH])
        mx = s.sb("mx", [P, TB, BH])
        sm = s.sb("sm", [P, TB, BH])
        parts = s.sb("parts", [P, TB, WINDOW, PARTS, BH], BF16)
        pT = s.sb("pT", [2 * PARTS * BH, WINDOW // 2, D], BF16)
        pv = s.sb("pv", [P, WINDOW // 2, 2, D])
        acc = s.sb("acc", [P, 2, D])
        acc1 = s.sb("acc1", [P, D])
        upd = s.sb("upd", [P, D])
        mm = s.ps("mm", [P, D])
        dps = s.ps("dps", [P, D])
        tps = s.ps("tps", [P, TB, WINDOW, BH])
        eps_ = s.ps("eps", [P, 2, 2, D])

        w_in, w_zero, b_ready = s.sem("w_in"), s.sem("w_zero"), s.sem("b_ready")
        ctx_loaded = s.sems("ctx_loaded")
        xn_ready = s.sem("xn_ready")
        proj, outp = s.sem("proj"), s.sem("outp")
        proj_read = s.sem("proj_read")
        prod_ready, prod_used = s.sem("prod_ready"), s.sem("prod_used")
        dots_out, dotsT = s.sem("dots_out"), s.sem("dotsT")
        shifted, exped, probs, dve_chain = s.sem("shifted"), s.sem("exped"), s.sem("probs"), s.sem("dve_chain")
        hi, mid, lo, rest, rest2 = s.sem("hi"), s.sem("mid"), s.sem("lo"), s.sem("rest"), s.sem("rest2")
        pT_ps, pT_read = s.sem("pT_ps"), s.sem("pT_read")
        spread_ready, pv_ready, added, acc_ready = s.sem("spread_ready"), s.sem("pv_ready"), s.sem("added"), s.sem("acc_ready")
        upd_ready, x_new, stats = s.sem("upd_ready"), s.sem("x_new"), s.sem("stats")
        NP = WINDOW // WS
        def tpb(n):
            flat = tps[:, :, :, :].rearrange("p a b c -> p (a b c)").bitcast(BF16)
            return flat[0:2 * PARTS * BH, (n % 2) * 1024:(n % 2) * 1024 + 1024].rearrange("p (w t) -> p w t", w=2)

        with nc.Block() as block:
            @block.sync
            def _(sp):
                sp.wait_ge(w_zero, 1)
                for n, w in enumerate((wqT, wkT, wvT, woT)):
                    for b in range(2):
                        sp.dma_start(w4[64 * b:64 * b + 64, n, 64 * b:64 * b + 64], w).then_inc(w_in, 16)
                for n, w in enumerate((bq, bk, bv, bo)):
                    for b in range(2):
                        sp.dma_start(bias4[64 * b:64 * b + 64, n:n + 1], w.rearrange("(n o) -> n o", o=1)).then_inc(w_in, 16)
                sp.dma_start(sumw[:, :, :], head_sums).then_inc(w_in, 16)
                sp.dma_start(expw_in[:, :, :], head_spread).then_inc(w_in, 16)
                rows = rows_of(ctx_in)
                for u in range(2):
                    sp.dma_start(cin[:, u, :], rows[:, u, :]).then_inc(ctx_loaded[u], 16)
                with sp.Fori(0, TURNS - 1) as j:
                    for u in range(2):
                        sp.wait_ge(proj, j * 6 + 3 * u + 3)
                        sp.dma_start(cin[:, u, :], rows[:, 2 * j + u + 2, :]).then_inc(ctx_loaded[u], 16)


            @block.gpsimd
            def _(pool):
                def add(p, n):
                    need(pool, pv_ready, 8 * p + n + 1)
                    if n == 1:
                        need(pool, acc_ready, p)
                        pool.tensor_tensor(acc[:, :, :], pv[:, 0, :, :], pv[:, 1, :, :], ALU.add).then_inc(added, 2)
                    else:
                        need(pool, added, 8 * p + n)
                        pool.tensor_tensor(acc[:, :, :], acc[:, :, :], pv[:, n, :, :], ALU.add).then_inc(added, 1)

                def step(v, par, has):
                    for n in range(1, 7):
                        if has(0):
                            add(v, n)
                        if n == 3 and has(-1):
                            need(pool, upd_ready, v)
                            pool.tensor_tensor(c.x[:, v - 1, :], c.x[:, v - 1, :], upd[:, :], ALU.add).then_inc(x_new, 1)
                    if has(1):
                        need(pool, hi, v + 2)
                        pool.tensor_tensor(pr[:, :, :, :], pr[:, :, :, :], parts[:, :, :, 0, :], ALU.subtract).then_inc(rest, 1)
                    if has(0):
                        add(v, 7)
                    if has(1):
                        need(pool, mid, v + 2)
                        pool.tensor_tensor(parts[:, :, :, 2, :], pr[:, :, :, :], parts[:, :, :, 1, :], ALU.subtract).then_inc(lo, 1)
                    if has(0):
                        need(pool, added, 8 * v + 8)
                        need(pool, outp, v)
                        pool.tensor_tensor(acc1[:, :], acc[:, 0, :], acc[:, 1, :], ALU.add).then_inc(acc_ready, 1)

                pipelined(pool, step, -1, 2)

            @block.scalar
            def _(act):
                act.wait_ge(b_ready, 3)
                act.wait_ge(w_zero, 3)

                def dots_half(p, h):
                    need(act, prod_used, NP * p + (h + 1) * NP // 2)
                    need(act, dotsT, p)
                    act.copy(dots[:, h, :], dps[:, :]).then_inc(dots_out, 1)

                def step(v, par, has):
                    if has(1):
                        dots_half(v + 1, 0)
                    if has(0):
                        for n in range(4):
                            need(act, pT_ps, v * 4 + n + 1)
                            if n == 0:
                                need(act, spread_ready, v * 8)
                            act.copy(pT[:, 2 * n:2 * n + 2, :], tpb(n)).then_inc(pT_read, 1)
                    if has(1):
                        dots_half(v + 1, 1)
                    if has(-1):
                        need(act, outp, v)
                        need(act, x_new, v - 1)
                        act.activation(upd[:, :], mm[:, :], ACT.Identity, bias=bias4[:, 3:4], scale=c.gate[:, 0:1]).then_inc(upd_ready, 1)
                    if has(1):
                        need(act, shifted, v + 2)
                        act.activation(e[:, :, :, :], e[:, :, :, :], ACT.Exp).then_inc(exped, 1)
                    if has(2):
                        p = v + 2
                        need(act, proj, p * 3 + 1)
                        need(act, prod_ready, (p - 1) * NP)
                        act.activation(q[:, par, :], mm[:, :], ACT.Identity, bias=bias4[:, 0:1], scale=HD0 ** -0.5).then_inc(proj_read, 1)
                        need(act, proj, p * 3 + 2)
                        act.activation(kp[:, par, PAD_L:PAD_L + D], mm[:, :], ACT.Identity, bias=bias4[:, 1:2]).then_inc(proj_read, 1)
                        need(act, proj, p * 3 + 3)
                        need(act, pv_ready, (p - 1) * 8)
                        act.activation(vp[:, par, PAD_L:PAD_L + D], mm[:, :], ACT.Identity, bias=bias4[:, 2:3]).then_inc(proj_read, 1)
                    if has(1):
                        need(act, probs, v + 2)
                        need(act, pT_ps, (v + 1) * 4)
                        act.copy(parts[:, :, :, 0, :], pr[:, :, :, :]).then_inc(hi, 1)
                        need(act, rest, v + 2)
                        act.copy(parts[:, :, :, 1, :], pr[:, :, :, :]).then_inc(mid, 1)

                pipelined(act, step, -1, 2)

            @block.tensor
            def _(pe):
                pe.wait_ge(w_in, 16 * 18)
                pe.wait_ge(b_ready, 1)

                def reduce(p, n):
                    need(pe, prod_ready, p * NP + n + 1)
                    need(pe, dots_out, 2 * p + n // 2)
                    for wl in range(WS):
                        w = n * WS + wl
                        g, par = w % 8 // 2, w % 2
                        ins = pe.matmul(dps[32 * g:32 * g + 32, :], sumw[:, par, :], prod[:, n % 2, wl, :],
                                        start=(par == 0), stop=(par == 1))
                    ins.then_inc(prod_used, 1)

                def spread_probs(p, n):
                    if n % 2 == 0:
                        need(pe, pT_read, p * 4 + n // 2 + 1)
                    need(pe, pv_ready, p * 8 + n - 1)
                    for par in range(2):
                        ins = pe.matmul(eps_[:, n % 2, par, :], expw[:, par, :], pT[:, n, :], start=True, stop=True)
                    ins.then_inc(spread_ready, 1)

                def step(v, par, has):
                    if has(1):
                        for n in range(3):
                            reduce(v + 1, n)
                    if has(0):
                        need(pe, lo, v + 1)
                        for n in range(4):
                            need(pe, pT_read, v * 4 + max(0, n - 1))
                            for wp in range(2):
                                for tb in range(TB):
                                    ins = pe.transpose(tpb(n)[:, wp, P * tb:P * tb + P],
                                                       parts[:, tb, 4 * n + 2 * wp:4 * n + 2 * wp + 2, :, :].rearrange("p a b c -> p (a b c)"),
                                                       c.identb[:, :])
                            ins.then_inc(pT_ps, 1)
                        spread_probs(v, 0)
                        spread_probs(v, 1)
                    if has(1):
                        reduce(v + 1, 3)
                    if has(0):
                        spread_probs(v, 2)
                        spread_probs(v, 3)
                    if has(-1):
                        need(pe, acc_ready, v)
                        need(pe, proj_read, min(3 * v + 6, 3 * PAIRS) if isinstance(v, int) else 3 * v + 6)
                        pe.matmul(mm[:, :], w4[:, 3, :], acc1[:, :], start=True, stop=True).then_inc(outp, 1)
                    if has(1):
                        need(pe, dots_out, 2 * v + 4)
                        need(pe, pT_read, 4 * v + 4)
                        for tb in range(TB):
                            for half in range(2):
                                ins = pe.transpose(tps[:, tb, 8 * half:8 * half + 8, :].rearrange("p a b -> p (a b)"),
                                                   dots[:, half, P * tb:P * tb + P], c.ident[:, :])
                        ins.then_inc(dotsT, 1)
                    if has(0):
                        for n in range(4, 8):
                            spread_probs(v, n)
                    if has(2):
                        p = v + 2
                        need(pe, xn_ready, p + 1)
                        need(pe, upd_ready, p - 2)
                        pe.matmul(mm[:, :], w4[:, 0, :], xn[:, par, :], start=True, stop=True).then_inc(proj, 1)
                        need(pe, ctx_loaded[par], 16 * (p // 2 + 1) if isinstance(p, int) else (p - par) * 8 + 16)
                        need(pe, proj_read, p * 3 + 1)
                        pe.matmul(mm[:, :], w4[:, 1, :], cin[:, par, :], start=True, stop=True).then_inc(proj, 1)
                        need(pe, proj_read, p * 3 + 2)
                        pe.matmul(mm[:, :], w4[:, 2, :], cin[:, par, :], start=True, stop=True).then_inc(proj, 1)

                pipelined(pe, step, -1, 2)

            @block.vector
            def _(dve):
                dve.memset(w4[:, :, :], 0.0).then_inc(w_zero, 1)
                dve.memset(kp[:, :, :], 0.0).then_inc(w_zero, 1)
                dve.memset(vp[:, :, :], 0.0).then_inc(w_zero, 1)
                dve.wait_ge(w_in, 16 * 18)
                dve.tensor_copy(expw[:, :, :], expw_in[:, :, :]).then_inc(b_ready, 1)
                dve.tensor_scalar(bias4[:, 0:1], bias4[:, 0:1], HD0 ** -0.5, None, ALU.mult).then_inc(b_ready, 1)
                dve.tensor_scalar(bias4[:, 3:4], bias4[:, 3:4], c.gate[:, 0:1], None, ALU.mult).then_inc(b_ready, 1)

                def weigh(p, par, n):
                    need(dve, spread_ready, p * 8 + n + 1)
                    need(dve, added, 8 * (p - 1) + max(2, n + 1))
                    dve.tensor_tensor(pv[:, n, :, :], eps_[:, n % 2, :, :], overlapped(vp[:, par, 2 * n:2 * n + D], 1, 2, D),
                                      ALU.mult).then_inc(pv_ready, 1)

                def step(v, par, has):
                    if has(1):
                        p, other = v + 1, 1 - par
                        need(dve, proj_read, p * 3 + 2)
                        for n in range(NP):
                            need(dve, prod_used, p * NP + n - 1)
                            dve.tensor_tensor(prod[:, n % 2, :, :],
                                              q[:, other:other + 1, :].to_broadcast([P, WS, D]),
                                              overlapped(kp[:, other, WS * n:WS * n + D], 1, WS, D), ALU.mult).then_inc(prod_ready, 1)
                    if has(0):
                        need(dve, proj_read, v * 3 + 3)
                        for n in range(4):
                            weigh(v, par, n)
                    if has(1):
                        need(dve, dotsT, p + 1)
                        ch = Chain(dve, dve_chain, p, 3)
                        ch.step(dve.tensor_reduce(mx[:, :, :], tps[:, :, :, :].rearrange("p a w b -> p a b w"), X, ALU.max))
                        dve.tensor_tensor(e[:, :, :, :], tps[:, :, :, :], mx[:, :, :].unsqueeze(2).to_broadcast([P, TB, WINDOW, BH]),
                                          ALU.subtract).then_inc(shifted, 1)
                    if has(0):
                        for n in range(4, 8):
                            weigh(v, par, n)
                    if has(2):
                        need(dve, proj, 3 * v + 1)
                        normalised(c, dve, xn[:, par, :], v + 2).then_inc(xn_ready, 1)
                    if has(1):
                        need(dve, exped, p + 1)
                        ch.step(dve.tensor_reduce(sm[:, :, :], e[:, :, :, :].rearrange("p a w b -> p a b w"), X, ALU.add))
                        ch.step(dve.reciprocal(sm[:, :, :], sm[:, :, :]))
                        need(dve, lo, p)
                        dve.tensor_tensor(pr[:, :, :, :], e[:, :, :, :], sm[:, :, :].unsqueeze(2).to_broadcast([P, TB, WINDOW, BH]),
                                          ALU.mult).then_inc(probs, 1)
                        ch.end()
                    if has(-1):
                        need(dve, x_new, v)
                        dve.bn_stats(c.stats[:, v - 1, :], c.x[:, v - 1, :]).then_inc(stats, 1)

                pipelined(dve, step, -1, 2)


EXPERTS, RANK0 = 8, 16
SCALING0 = 8.0 / RANK0
ER = EXPERTS * RANK0


def lora_mixture_stage(c, aT, bT, router_b):
    nc = c.nc
    with Stage(nc, "moe") as s:
        a_sb = s.sb("a", [P, KT, ER + EXPERTS])
        b_sb = s.sb("b", [P, D])
        rb = s.sb("rb", [P, EXPERTS])
        g = s.sb("g", [P, 1])
        iota = s.sb("iota", [P, EXPERTS])
        xn = s.sb("xn", [P, 2, D])
        xT = s.sb("xT", [P, 2, KT, P])
        lg = s.sb("lg", [P, EXPERTS])
        top = s.sb("top", [P, 8])
        at_top = s.sb("at_top", [P, 8], U32)
        at_topf = s.sb("at_topf", [P, 8])
        diff = s.sb("diff", [P, 2])
        ex = s.sb("ex", [P, 2])
        wt = s.sb("wt", [P, 2, EXPERTS])
        hw = s.sb("hw", [P, 2, ER])
        hT = s.sb("hT", [P, 2, P])
        xT_ps = s.ps("xT_ps", [P, 2, KT, P])
        h_ps = s.ps("h_ps", [P, 2, 512])
        hT_ps = s.ps("hT_ps", [P, 512])
        out_ps = s.ps("out_ps", [P, 2, D])
        w_in, iota_set, g_set = s.sem("w_in"), s.sem("iota"), s.sem("g_set")
        xn_ready, xT_made, xT_ready, h_ready = s.sem("xn"), s.sem("xT_made"), s.sem("xT_ready"), s.sem("h_ready")
        diffs, exps, hw_ready, hT_made, hT_ready = s.sem("diffs"), s.sem("exps"), s.sem("hw"), s.sem("hT_made"), s.sem("hT_ready")
        out_ready, x_new, chain, stats = s.sem("out_ready"), s.sem("x_new"), s.sem("chain"), s.sem("stats")
        with nc.Block() as block:
            @block.sync
            def _(sp):
                sp.dma_start(a_sb[:, :, :], aT.rearrange("(k p) n -> p k n", p=P)).then_inc(w_in, 16)
                sp.dma_start(b_sb[:, :], bT).then_inc(w_in, 16)
                sp.dma_start(rb[:, :], router_b.rearrange("(o n) -> o n", o=1).to_broadcast([P, EXPERTS])).then_inc(w_in, 16)

            @block.gpsimd
            def _(pool):
                pool.iota(iota[:, :], [[1, EXPERTS]], base=0, channel_multiplier=0, allow_small_or_imprecise_dtypes=True).then_inc(iota_set, 1)


            @block.tensor
            def _(pe):
                pe.wait_ge(w_in, 48)

                def step(v, par, has):
                    if has(2):
                        need(pe, xn_ready, v + 3)
                        need(pe, xT_ready, v + 1)
                        for k in range(KT):
                            ins = pe.transpose(xT_ps[:, par, k, :], xn[:, par, P * k:P * k + P], c.ident[:, :])
                        ins.then_inc(xT_made, 1)
                    if has(0):
                        need(pe, hT_ready, v + 1)
                        need(pe, x_new, v)
                        pe.matmul(out_ps[:, par, :], hT[:, par, :], b_sb[:, :], start=True, stop=True).then_inc(out_ready, 1)
                    if has(2):
                        need(pe, xT_ready, v + 3)
                        need(pe, hw_ready, v + 1)
                        for k in range(KT):
                            ins = pe.matmul(h_ps[:, par, 0:ER + EXPERTS], xT[:, par, k, :], a_sb[:, k, :], start=(k == 0), stop=(k == KT - 1))
                        ins.then_inc(h_ready, 1)
                    if has(1):
                        need(pe, hw_ready, v + 2)
                        need(pe, hT_ready, v + 1)
                        pe.transpose(hT_ps[:, 0:P], hw[:, 1 - par, :], c.ident[:, :]).then_inc(hT_made, 1)

                pipelined(pe, step, 0, 3)

            @block.scalar
            def _(act):
                def step(v, par, has):
                    if has(2):
                        need(act, xT_made, v + 3)
                        need(act, h_ready, v + 1)
                        act.copy(xT[:, par, :, :], xT_ps[:, par, :, :]).then_inc(xT_ready, 1)
                    if has(1):
                        need(act, diffs, v + 2)
                        act.activation(ex[:, :], diff[:, :], ACT.Exp).then_inc(exps, 1)
                        need(act, hT_made, v + 2)
                        need(act, out_ready, v)
                        act.copy(hT[:, 1 - par, :], hT_ps[:, 0:P]).then_inc(hT_ready, 1)

                pipelined(act, step, 0, 3)

            @block.vector
            def _(dve):
                dve.wait_ge(w_in, 48)
                dve.wait_ge(iota_set, 1)
                dve.tensor_scalar(g[:, :], c.gate[:, 4:5], SCALING0, None, ALU.mult).then_inc(g_set, 1)
                dve.wait_ge(g_set, 1)

                def step(v, par, has):
                    u = 1 - par
                    if has(1):
                        need(dve, h_ready, v + 2)
                        ch = Chain(dve, chain, v + 1, 8)
                        ch.step(dve.tensor_tensor(lg[:, :], h_ps[:, u, ER:ER + EXPERTS], rb[:, :], ALU.add))
                        dve.tensor_copy(diff[:, 0:1], lg[:, 0:1])
                        ch.step(dve.max(out=top[:, :], in_=lg[:, :]))
                        dve.tensor_tensor(diff[:, 0:1], top[:, 1:2], top[:, 0:1], ALU.subtract)
                        dve.tensor_tensor(diff[:, 1:2], top[:, 0:1], top[:, 1:2], ALU.subtract).then_inc(diffs, 1)
                        ch.step(dve.max_index(out=at_top[:, :], in_max=top[:, :], in_values=lg[:, :]))
                        ch.step(dve.tensor_copy(at_topf[:, :], at_top[:, :]))
                    if has(3):
                        need(dve, xT_made, v + 2)
                        normalised(c, dve, xn[:, u, :], v + 3).then_inc(xn_ready, 1)
                    if has(1):
                        need(dve, exps, v + 2)
                        ch.step(dve.tensor_scalar(ex[:, :], ex[:, :], 1.0, None, ALU.add))
                        ch.step(dve.reciprocal(ex[:, :], ex[:, :]))
                        dve.tensor_scalar(wt[:, 0, :], iota[:, :], at_topf[:, 0:1], ex[:, 0:1], ALU.is_equal, ALU.mult)
                        ch.step(dve.tensor_scalar(wt[:, 1, :], iota[:, :], at_topf[:, 1:2], ex[:, 1:2], ALU.is_equal, ALU.mult))
                        ch.step(dve.tensor_tensor(wt[:, 0, :], wt[:, 0, :], wt[:, 1, :], ALU.add))
                        need(dve, hT_made, v)
                        dve.tensor_tensor(hw[:, u, :].rearrange("p (e r) -> p e r", e=EXPERTS),
                                          h_ps[:, u, 0:ER].rearrange("p (e r) -> p e r", e=EXPERTS),
                                          spread(wt[:, 0, :], RANK0), ALU.mult).then_inc(hw_ready, 1)
                        ch.end()
                    if has(0):
                        need(dve, out_ready, v + 1)
                        dve.scalar_tensor_tensor(out=c.x[:, v, :], in0=out_ps[:, par, :], scalar=g[:, 0:1], in1=c.x[:, v, :],
                                                 op0=ALU.mult, op1=ALU.add).then_inc(x_new, 1)
                        need(dve, x_new, v + 1)
                        dve.bn_stats(c.stats[:, v, :], c.x[:, v, :]).then_inc(stats, 1)

                pipelined(dve, step, 0, 3)


def transposed_norm_stage(c, xT_all, name):
    nc = c.nc
    with Stage(nc, name) as s:
        xn = s.sb("xn", [P, 2, D])
        xT_ps = s.ps("xT_ps", [P, 2, KT, P])
        xn_ready, xT_made, xT_out = s.sem("xn"), s.sem("xT_made"), s.sem("xT_out")
        with nc.Block() as block:
            @block.vector
            def _(dve):
                with dve.Fori(0, TURNS) as j:
                    for u in range(2):
                        t = 2 * j + u
                        dve.wait_ge(xT_made, t)
                        normalised(c, dve, xn[:, u, :], t).then_inc(xn_ready, 1)

            @block.tensor
            def _(pe):
                with pe.Fori(0, TURNS) as j:
                    for u in range(2):
                        t = 2 * j + u
                        pe.wait_ge(xn_ready, t + 1)
                        pe.wait_ge(xT_out, t)
                        for k in range(KT):
                            ins = pe.transpose(xT_ps[:, u, k, :], xn[:, u, P * k:P * k + P], c.ident[:, :])
                        ins.then_inc(xT_made, 1)

            @block.scalar
            def _(act):
                with act.Fori(0, TURNS) as j:
                    for u in range(2):
                        t = 2 * j + u
                        act.wait_ge(xT_made, t + 1)
                        act.copy(xT_all[:, :, bass.ds(t * P, P)], xT_ps[:, u, :, :]).then_inc(xT_out, 1)


def stats_stage(c, name):
    nc = c.nc
    with Stage(nc, name) as s:
        stats = s.sem("stats")
        with nc.Block() as block:
            @block.vector
            def _(dve):
                for i in range(PAIRS):
                    dve.bn_stats(c.stats[:, i, :], c.x[:, i, :]).then_inc(stats, 1)


KV, GROUP, HD1, MAX_POS, THETA = 8, 4, 128, 512, 10000.0
STEP = 4 * P
STEPS = B * S // STEP
KEEP, MASKED = 3.0e38, -1.0e9 * HD1 ** 0.5


def rope_stage(c, pos, mask, tables, cosT, sinT, limit):
    nc = c.nc
    with Stage(nc, "rope") as s:
        pos_i = s.sb("pos_i", [P, PAIRS], I32)
        pos_f = s.sb("pos_f", [P, PAIRS])
        wrap = s.sb("wrap", [P, PAIRS])
        idx = s.sb("idx", [P, PAIRS], U32)
        rows = s.sb("rows", [P, 2, 2 * HD1])
        m_i = s.sb("m_i", [P, PAIRS, S], I32)
        masked = s.sb("masked", [P, PAIRS, S])
        t_ps = s.ps("t_ps", [P, 2, 4, P])
        p_in, m_in, chain, idx_ready = s.sem("p_in"), s.sem("m_in"), s.sem("chain"), s.sem("idx_ready")
        gathered, turned, out = s.sems("gathered"), s.sem("turned"), s.sem("out")
        with nc.Block() as block:
            @block.sync
            def _(sp):
                with nc.allow_non_contiguous_dma(reason="2048 positions, once"):
                    sp.dma_start(pos_i[:, :], pos.rearrange("(i b) s -> (b s) i", b=2)).then_inc(p_in, 16)
                sp.dma_start(m_i[:, :, :], mask.rearrange("(i b) q k -> (b q) i k", b=2)).then_inc(m_in, 16)

            @block.vector
            def _(dve):
                dve.wait_ge(p_in, 16)
                ch = Chain(dve, chain)
                ch.step(dve.tensor_copy(pos_f[:, :], pos_i[:, :]))
                ch.step(dve.tensor_scalar(wrap[:, :], pos_f[:, :], 0.0, float(MAX_POS), ALU.is_lt, ALU.mult))
                ch.step(dve.tensor_tensor(pos_f[:, :], pos_f[:, :], wrap[:, :], ALU.add))
                ch.step(dve.tensor_scalar(pos_f[:, :], pos_f[:, :], 0.0, float(MAX_POS - 1), ALU.max, ALU.min))
                dve.tensor_copy(idx[:, :], pos_f[:, :]).then_inc(idx_ready, 1)
                dve.wait_ge(m_in, 16)
                ch.step(dve.tensor_scalar(masked[:, :, :], m_i[:, :, :], 0.0, MASKED, ALU.is_equal, ALU.mult))
                ch.step(dve.tensor_scalar(limit[:, :, :], m_i[:, :, :], 0.0, KEEP, ALU.not_equal, ALU.mult))
                ch.step(dve.tensor_tensor(limit[:, :, :], limit[:, :, :], masked[:, :, :], ALU.add))

            @block.gpsimd
            def _(pool):
                pool.wait_ge(idx_ready, 1)
                for i in range(PAIRS):
                    if i >= 2:
                        pool.wait_ge(turned, i - 1)
                    pool.indirect_dma_start(out=rows[:, i % 2, :], out_offset=None, in_=tables,
                                            in_offset=bass.IndirectOffsetOnAxis(ap=idx[:, i:i + 1], axis=0)).then_inc(gathered[i % 2], 16)

            @block.tensor
            def _(pe):
                for i in range(PAIRS):
                    pe.wait_ge(gathered[i % 2], 16 * (i // 2 + 1))
                    if i >= 2:
                        pe.wait_ge(out, i - 1)
                    for n in range(2):
                        ins = pe.transpose(t_ps[:, i % 2, n, :], rows[:, i % 2, HD1 * n:HD1 * n + HD1], c.ident[:, :])
                    ins.then_inc(turned, 1)

            @block.scalar
            def _(act):
                for i in range(PAIRS):
                    act.wait_ge(turned, i + 1)
                    act.copy(cosT[:, P * i:P * i + P], t_ps[:, i % 2, 0, :])
                    act.copy(sinT[:, P * i:P * i + P], t_ps[:, i % 2, 1, :]).then_inc(out, 1)


def rope_tables():
    inv = (1.0 / np.float32(THETA) ** (np.arange(0, HD1, 2, dtype=np.float32) / np.float32(HD1))).astype(np.float32)
    f = np.arange(MAX_POS, dtype=np.float32)[:, None] * inv[None]
    cos, sin = np.cos(f).astype(np.float32), np.sin(f).astype(np.float32)
    return np.concatenate([cos, cos, -sin, sin], axis=1)


def grouped_attention_stage(c, ctxT, wq, wk, wv, wo, cosT, sinT, limit, xT, cT):
    nc = c.nc
    with Stage(nc, "gqa") as s:
        w_q = s.sb("wq", [P, 2, KT, GROUP * HD1])
        w_k = s.sb("wk", [P, 2, KT, HD1])
        w_v = s.sb("wv", [P, 2, KT, HD1])
        w_o = s.sb("wo", [P, 2, GROUP, D])
        qk = s.sb("qk", [P, 2, 1 + GROUP, STEP])
        v = s.sb("v", [P, 2, 4, HD1])
        sw = s.sb("sw", [P, 2, STEP])
        e = s.sb("e", [P, 4 * GROUP, S])
        mx = s.sb("mx", [P, 4 * GROUP])
        sm = s.sb("sm", [P, 4 * GROUP])
        probs = s.sb("probs", [P, 4 * GROUP, P])
        pT = s.sb("pT", [P, 2, GROUP * P])
        oT = s.sb("oT", [P, 2, GROUP, P])
        proj_ps = s.ps("proj", [P, 2, STEP])
        s_ps = s.ps("scores", [P, 4, GROUP, S])
        t_ps = s.ps("pT_ps", [P, GROUP, P])
        o_ps = s.ps("o_ps", [P, GROUP, P])
        y_ps = s.ps("y_ps", [P, 2, D])
        w_loaded = s.sems("w_loaded")
        c_loaded, probs_zero = s.sem("c_loaded"), s.sem("probs_zero")
        filled, swapped, cosed, sined, roped = s.sem("filled"), s.sem("swapped"), s.sem("cosed"), s.sem("sined"), s.sem("roped")
        scored, bounded, shifted, exped, normed = s.sem("scored"), s.sem("bounded"), s.sem("shifted"), s.sem("exped"), s.sem("normed")
        turned, turned_out, headed, headed_out = s.sem("turned"), s.sem("turned_out"), s.sem("headed"), s.sem("headed_out")
        summed, added, chain = s.sem("summed"), s.sem("added"), s.sem("chain")
        GT = KV // 2
        R = 2 * STEPS
        FILLS, ROPES = 6, 5
        with nc.Block() as block:
            @block.sync
            def _(sp):
                with sp.Fori(0, GT) as j:
                    for gb in range(2):
                        sp.wait_ge(summed, j * (4 * R))
                        gh = 2 * j + gb
                        sp.dma_start(w_k[:, gb, :, :], wk.rearrange("(k p) n -> p k n", p=P)[:, :, bass.ts(gh, HD1)]).then_inc(w_loaded[gb], 16)
                        sp.dma_start(w_q[:, gb, :, :], wq.rearrange("(k p) n -> p k n", p=P)[:, :, bass.ts(gh, GROUP * HD1)]).then_inc(w_loaded[gb], 16)
                        sp.dma_start(w_v[:, gb, :, :], wv.rearrange("(k p) n -> p k n", p=P)[:, :, bass.ts(gh, HD1)]).then_inc(w_loaded[gb], 16)
                        sp.dma_start(w_o[:, gb, :, :], wo.rearrange("(g h p) n -> p g h n", h=GROUP, p=P)[:, gh, :, :]).then_inc(w_loaded[gb], 16)

            @block.tensor
            def _(pe):
                pe.wait_ge(probs_zero, 1)

                def project(j, r):
                    par, gb, step = r % 2, r // STEPS, r % STEPS
                    cols = slice(STEP * step, STEP * step + STEP)
                    for n in range(FILLS):
                        pe.wait_ge(swapped, j * FILLS * R + FILLS * r + max(0, n - 1))
                        pe.wait_ge(cosed, j * ROPES * R + ROPES * r + max(0, n - 1))
                        for k in range(KT):
                            if n == 0:
                                ins = pe.matmul(proj_ps[:, 0, :], w_k[:, gb, k, :], cT[:, k, cols], start=(k == 0), stop=(k == KT - 1))
                            elif n < 5:
                                ins = pe.matmul(proj_ps[:, n % 2, :], w_q[:, gb, k, HD1 * (n - 1):HD1 * n], xT[:, k, cols], start=(k == 0), stop=(k == KT - 1))
                        if n == 5:
                            for i in range(4):
                                for k in range(KT):
                                    ins = pe.matmul(proj_ps[:, 1, HD1 * i:HD1 * i + HD1], cT[:, k, STEP * step + P * i:STEP * step + P * i + P],
                                                    w_v[:, gb, k, :], start=(k == 0), stop=(k == KT - 1))
                        ins.then_inc(filled, 1)

                def scores(j, r):
                    par = r % 2
                    pe.wait_ge(roped, j * ROPES * R + ROPES * (r + 1))
                    pe.wait_ge(bounded, j * R + r)
                    for i in range(4):
                        for h in range(GROUP):
                            for b in range(2):
                                rows = slice(P * i + S * b, P * i + S * b + S)
                                ins = pe.matmul(s_ps[S * b:S * b + S, i, h, :], qk[:, par, 1 + h, rows], qk[:, par, 0, rows], start=True, stop=True)
                    ins.then_inc(scored, 1)

                def turn(j, r, i):
                    if i == 0:
                        pe.wait_ge(normed, j * R + r + 1)
                    pe.wait_ge(turned_out, j * 4 * R + 4 * r + i)
                    for h in range(GROUP):
                        ins = pe.transpose(t_ps[:, h, :], probs[:, GROUP * i + h, :], c.ident[:, :])
                    ins.then_inc(turned, 1)

                def attend(j, r, i):
                    pe.wait_ge(turned_out, j * 4 * R + 4 * r + i + 1)
                    pe.wait_ge(headed_out, j * 4 * R + 4 * r + i)
                    pe.matmul(o_ps[:, :, :], v[:, r % 2, i, :], pT[:, i % 2, :], start=True, stop=True).then_inc(headed, 1)

                def project_out(j, r, i):
                    pe.wait_ge(headed_out, j * 4 * R + 4 * r + i + 1)
                    pe.wait_ge(added, j * 4 * R + 4 * r + max(0, i - 1))
                    for h in range(GROUP):
                        ins = pe.matmul(y_ps[:, i % 2, :], oT[:, i % 2, h, :], w_o[:, r // STEPS, h, :], start=(h == 0), stop=(h == GROUP - 1))
                    ins.then_inc(summed, 1)

                pe.wait_ge(c_loaded, 16)
                with pe.Fori(0, GT) as j:
                    for r in range(R + 1):
                        if r < R and r % STEPS == 0:
                            pe.wait_ge(w_loaded[r // STEPS], j * 64 + 64)
                        if r > 0:
                            scores(j, r - 1)
                        if r < R:
                            project(j, r)
                        if r > 0:
                            for i in range(4 + 2):
                                if i < 4:
                                    turn(j, r - 1, i)
                                if 1 <= i < 5:
                                    attend(j, r - 1, i - 1)
                                if i >= 2:
                                    project_out(j, r - 1, i - 2)

            @block.scalar
            def _(act):
                act.dma_start(cT[:, :, :], ctxT.rearrange("(k p) n -> p k n", p=P)).then_inc(c_loaded, 16)

                def exps(j, r):
                    act.wait_ge(shifted, j * R + r + 1)
                    act.activation(e[:, :, :], e[:, :, :], ACT.Exp, scale=HD1 ** -0.5).then_inc(exped, 1)

                def read(j, r, n):
                    act.wait_ge(filled, j * FILLS * R + FILLS * r + n + 1)
                    if n < ROPES:
                        par = (ROPES * r + n) % 2
                        act.wait_ge(roped, j * ROPES * R + max(0, ROPES * r + n - 1))
                        act.copy(sw[0:64, par, :], proj_ps[64:128, n % 2, :])
                        act.copy(sw[64:128, par, :], proj_ps[0:64, n % 2, :]).then_inc(swapped, 1)
                    else:
                        act.wait_ge(headed, j * 4 * R + max(0, 4 * (r - 1)))
                        act.copy(v[:, r % 2, :, :], proj_ps[:, 1, :].rearrange("p (i d) -> p i d", i=4)).then_inc(swapped, 1)

                with act.Fori(0, GT) as j:
                    for r in range(R + 1):
                        for n in range(FILLS):
                            if r < R:
                                read(j, r, n)
                            if r > 0 and n == 1:
                                exps(j, r - 1)
                        if r > 0:
                            q = r - 1
                            for i in range(5):
                                if i < 4:
                                    act.wait_ge(turned, j * 4 * R + 4 * q + i + 1)
                                    act.wait_ge(headed, j * 4 * R + max(0, 4 * q + i - 1))
                                    act.copy(pT[:, i % 2, :], t_ps[:, :, :].rearrange("p h q -> p (h q)")).then_inc(turned_out, 1)
                                if i > 0:
                                    act.wait_ge(headed, j * 4 * R + 4 * q + i)
                                    act.wait_ge(summed, j * 4 * R + max(0, 4 * q + i - 2))
                                    act.copy(oT[:, (i - 1) % 2, :, :], o_ps[:, :, :]).then_inc(headed_out, 1)

            @block.gpsimd
            def _(pool):
                with pool.Fori(0, GT) as j:
                    for r in range(R):
                        for n in range(ROPES):
                            par, k = (ROPES * r + n) % 2, ROPES * r + n
                            pool.wait_ge(swapped, j * FILLS * R + FILLS * r + n + 1)
                            pool.tensor_tensor(sw[:, par, :], sw[:, par, :], sinT[:, STEP * (r % STEPS):STEP * (r % STEPS) + STEP],
                                               ALU.mult).then_inc(sined, 1)

            @block.vector
            def _(dve):
                dve.memset(probs[:, :, :], 0.0).then_inc(probs_zero, 1)

                def rope(j, r, n):
                    cols = slice(STEP * (r % STEPS), STEP * (r % STEPS) + STEP)
                    k = j * ROPES * R + ROPES * r + n
                    dve.wait_ge(swapped, j * FILLS * R + FILLS * r + n + 1)
                    if n == 0:
                        dve.wait_ge(scored, j * R + max(0, r - 1))
                    dve.tensor_tensor(qk[:, r % 2, n, :], proj_ps[:, n % 2, :], cosT[:, cols], ALU.mult).then_inc(cosed, 1)
                    dve.wait_ge(sined, k + 1)
                    dve.wait_ge(cosed, k + 1)
                    dve.tensor_tensor(qk[:, r % 2, n, :], qk[:, r % 2, n, :], sw[:, (ROPES * r + n) % 2, :], ALU.add).then_inc(roped, 1)

                CH = 4
                def bound(j, r):
                    dve.wait_ge(scored, j * R + r + 1)
                    lim = limit[:, 4 * (r % STEPS):4 * (r % STEPS) + 4, :].unsqueeze(2).to_broadcast([P, 4, GROUP, S])
                    dve.tensor_tensor(e[:, :, :].rearrange("p (i h) k -> p i h k", h=GROUP), s_ps[:, :, :, :], lim, ALU.min).then_inc(bounded, 1)
                    dve.wait_ge(bounded, j * R + r + 1)
                    ch = Chain(dve, chain)
                    ch.base, ch.per = (j * R + r) * CH, CH
                    ch.step(dve.tensor_reduce(mx[:, :], e[:, :, :], X, ALU.max))
                    dve.tensor_tensor(e[:, :, :], e[:, :, :], spread(mx[:, :], S), ALU.subtract).then_inc(shifted, 1)
                    return ch

                def norm(j, r, ch):
                    dve.wait_ge(exped, j * R + r + 1)
                    ch.step(dve.tensor_reduce(sm[:, :], e[:, :, :], X, ALU.add))
                    ch.step(dve.reciprocal(sm[:, :], sm[:, :]))
                    dve.wait_ge(turned, j * 4 * R + 4 * r)
                    for b in range(2):
                        rows = slice(S * b, S * b + S)
                        ins = dve.tensor_tensor(probs[rows, :, rows], e[rows, :, :], spread(sm[rows, :], S), ALU.mult)
                        if b == 0:
                            ins.then_inc(chain, 1)
                            ch.n += 1
                    ins.then_inc(normed, 1)
                    ch.end()

                with dve.Fori(0, GT) as j:
                    for r in range(R + 1):
                        if r > 0:
                            ch = bound(j, r - 1)
                        if r < R:
                            rope(j, r, 0)
                            rope(j, r, 1)
                        if r > 0:
                            norm(j, r - 1, ch)
                        if r < R:
                            for n in range(2, ROPES):
                                rope(j, r, n)
                        if r > 0:
                            q = r - 1
                            for i in range(4):
                                row = 4 * (q % STEPS) + i
                                dve.wait_ge(summed, j * 4 * R + 4 * q + i + 1)
                                dve.scalar_tensor_tensor(out=c.x[:, row, :], in0=y_ps[:, i % 2, :], scalar=c.gate[:, 1:2], in1=c.x[:, row, :],
                                                         op0=ALU.mult, op1=ALU.add).then_inc(added, 1)


LORAS, RANK1, GROUPS1 = 16, 32, 8
NR = LORAS * RANK1
ROWS1 = B * S // GROUPS1
LR = 2 * RANK1


def lora_linear_stage(c, kernel, bias, gateT, pick, a_all, b_allT, a_sharedT, b_sharedT):
    nc = c.nc
    with Stage(nc, "lora") as s:
        NT, G = NR // P, GROUPS1
        w = s.sb("w", [P, KT, D])
        a_n = s.sb("a_n", [P, NT, D])
        b_n = s.sb("b_n", [P, NT, D])
        gate = s.sb("gate", [P, NT, G])
        eye = s.sb("eye", [P, RANK1])
        mix = s.sb("mix", [P, NT, G, RANK1])
        a_all_g = s.sb("a_all_g", [P, KT, G * RANK1])
        a_s = s.sb("a_s", [P, KT, RANK1])
        a_g = s.sb("a_g", [P, 2, KT, LR])
        b_g = s.sb("b_g", [LR + 1, G, D])
        xn = s.sb("xn", [P, 2, D])
        xT = s.sb("xT", [P, 2, KT, ROWS1])
        ax = s.sb("ax", [LR + 1, 2, ROWS1])
        mix_ps = s.ps("mix_ps", [P, 2, 512])
        xT_ps = s.ps("xT_ps", [P, 2, KT, P])
        ax_ps = s.ps("ax_ps", [P, 512])
        y_ps = s.ps("y_ps", [P, 2, D])
        gate_in, ab_in, shared_in, w_in = s.sem("gate_in"), s.sem("ab_in"), s.sem("shared_in"), s.sem("w_in")
        mixed, ones, shared_set = s.sem("mixed"), s.sem("ones"), s.sem("shared_set")
        a_made, a_out, b_made, b_out = s.sem("a_made"), s.sem("a_out"), s.sem("b_made"), s.sem("b_out")
        xn_ready, xT_made, xT_out = s.sem("xn"), s.sem("xT_made"), s.sem("xT_out")
        picked, ax_made, ax_out = s.sem("picked"), s.sem("ax_made"), s.sem("ax_out")
        summed, x_new, stats = s.sem("summed"), s.sem("x_new"), s.sem("stats")
        with nc.Block() as block:
            @block.sync
            def _(sp):
                sp.dma_start(gate[:, :, :], gateT).then_inc(gate_in, 16)
                sp.dma_start(eye[:, :], pick).then_inc(gate_in, 16)
                sp.dma_start(a_n[:, :, :], a_all.rearrange("(k p) n -> p k n", p=P)).then_inc(ab_in, 16)
                sp.dma_start(b_n[:, :, :], b_allT.rearrange("(k p) n -> p k n", p=P)).then_inc(ab_in, 16)
                sp.dma_start(a_s[:, :, :], a_sharedT.rearrange("(k p) n -> p k n", p=P)).then_inc(shared_in, 16)
                sp.dma_start(b_g[RANK1:LR, :, :], b_sharedT.unsqueeze(1).to_broadcast([RANK1, G, D])).then_inc(shared_in, 16)
                sp.dma_start(b_g[LR:LR + 1, :, :], bias.rearrange("(o g n) -> o g n", o=1, g=1).to_broadcast([1, G, D])).then_inc(shared_in, 16)
                sp.dma_start(w[:, :, :], kernel.rearrange("(k p) n -> p k n", p=P)).then_inc(w_in, 16)


            @block.tensor
            def _(pe):
                pe.wait_ge(ab_in, 32)
                pe.wait_ge(mixed, 1)
                for k in range(KT):
                    for n in range(NT):
                        ins = pe.matmul(mix_ps[:, k // 2, G * RANK1 * (k % 2):G * RANK1 * (k % 2 + 1)], a_n[:, n, P * k:P * k + P],
                                        mix[:, n, :, :].rearrange("p g r -> p (g r)"), start=(n == 0), stop=(n == NT - 1))
                    ins.then_inc(a_made, 1)
                for half in range(2):
                    pe.wait_ge(a_out, half + 1)
                    for n in range(NT):
                        ins = pe.matmul(mix_ps[:, half, :], mix[:, n, 4 * half:4 * half + 4, :].rearrange("p g r -> p (g r)"), b_n[:, n, :],
                                        start=(n == 0), stop=(n == NT - 1))
                    ins.then_inc(b_made, 1)
                pe.wait_ge(w_in, 16)
                pe.wait_ge(shared_in, 48)
                pe.wait_ge(ones, 1)
                pe.wait_ge(b_out, G)

                def turn(g, u, i):
                    need(pe, xn_ready, 2 * g + i + 1)
                    need(pe, xT_out, 2 * g + i - 1)
                    for k in range(KT):
                        ins = pe.transpose(xT_ps[:, i, k, :], xn[:, i, P * k:P * k + P], c.ident[:, :])
                    ins.then_inc(xT_made, 1)

                def step(v, par, has):
                    if has(0):
                        need(pe, xT_out, 2 * v + 2)
                        need(pe, picked, v + 1)
                        need(pe, ax_out, v)
                        for k in range(KT):
                            ins = pe.matmul(ax_ps[0:LR, 0:ROWS1], a_g[:, par, k, :], xT[:, par, k, :], start=(k == 0), stop=(k == KT - 1))
                        ins.then_inc(ax_made, 1)
                    for i in range(2):
                        if has(1):
                            turn(v + 1, 1 - par, i)
                        if has(0):
                            need(pe, x_new, 2 * v + max(0, i - 1))
                            for k in range(KT):
                                pe.matmul(y_ps[:, i, :], xT[:, par, k, P * i:P * i + P], w[:, k, :], start=(k == 0), stop=False)
                            if i == 0:
                                need(pe, ax_out, v + 1)
                            pe.matmul(y_ps[:, i, :], ax[:, par, P * i:P * i + P], b_g[:, v, :], start=False, stop=True).then_inc(summed, 1)

                pipelined(pe, step, 0, 2, G)

            @block.gpsimd
            def _(pool):
                pool.wait_ge(shared_set, 2)
                pool.wait_ge(a_out, 2)

                def step(v, par, has):
                    if has(1):
                        need(pool, ax_made, v)
                        pool.tensor_copy(a_g[:, 1 - par, :, 0:RANK1], a_all_g[:, :, bass.ds((v + 1) * RANK1, RANK1)]).then_inc(picked, 1)

                pipelined(pool, step, 0, 2, G)

            @block.scalar
            def _(act):
                act.wait_ge(a_made, 2)
                act.copy(a_all_g[:, 0:2, :], mix_ps[:, 0, :].rearrange("p (k n) -> p k n", k=2)).then_inc(a_out, 1)
                act.wait_ge(a_made, 4)
                act.copy(a_all_g[:, 2:4, :], mix_ps[:, 1, :].rearrange("p (k n) -> p k n", k=2)).then_inc(a_out, 1)
                act.wait_ge(shared_in, 48)
                for u in range(2):
                    act.copy(a_g[:, u, :, RANK1:LR], a_s[:, :, :]).then_inc(shared_set, 1)
                for g in range(G):
                    act.wait_ge(b_made, g // 4 + 1)
                    act.copy(b_g[0:RANK1, g, :], mix_ps[RANK1 * (g % 4):RANK1 * (g % 4 + 1), g // 4, :]).then_inc(b_out, 1)

                def step(v, par, has):
                    if has(0):
                        need(act, ax_made, v + 1)
                        need(act, summed, 2 * v)
                        act.copy(ax[0:LR, par, :], ax_ps[0:LR, 0:ROWS1]).then_inc(ax_out, 1)
                    if has(1):
                        for i in range(2):
                            need(act, xT_made, 2 * (v + 1) + i + 1)
                            need(act, summed, 2 * v)
                            act.copy(xT[:, 1 - par, :, P * i:P * i + P], xT_ps[:, i, :, :]).then_inc(xT_out, 1)

                pipelined(act, step, 0, 2, G)

            @block.vector
            def _(dve):
                dve.memset(ax[LR:LR + 1, :, :], 1.0).then_inc(ones, 1)
                dve.wait_ge(gate_in, 32)
                dve.tensor_tensor(mix[:, :, :, :].rearrange("p n g r -> p (n g) r"), spread(gate[:, :, :].rearrange("p n g -> p (n g)"), RANK1),
                                  eye[:, :].unsqueeze(1).to_broadcast([P, NT * G, RANK1]), ALU.mult).then_inc(mixed, 1)

                def step(v, par, has):
                    for i in range(2):
                        if has(2):
                            need(dve, xT_made, 2 * (v + 1) + i + 1)
                            normalised(c, dve, xn[:, i, :], 2 * (v + 2) + i).then_inc(xn_ready, 1)
                        if has(0):
                            t = 2 * v + i
                            need(dve, summed, t + 1)
                            dve.scalar_tensor_tensor(out=c.x[:, t, :], in0=y_ps[:, i, :], scalar=c.gate[:, 5:6], in1=c.x[:, t, :],
                                                     op0=ALU.mult, op1=ALU.add).then_inc(x_new, 1)
                            need(dve, x_new, t + 1)
                            dve.bn_stats(c.stats[:, t, :], c.x[:, t, :]).then_inc(stats, 1)

                pipelined(dve, step, 0, 2, G)


TOP = 8
LOW = -3.0e38


def dft(n, rows):
    j, h = np.arange(rows)[:, None], n // 2
    return np.concatenate([np.cos(2 * np.pi * j * np.arange(h + 1) / n), -np.sin(2 * np.pi * j * np.arange(1, h) / n)], axis=1)


def swap_parts(m, n):
    h, out = n // 2, np.zeros_like(m)
    out[:, 1:h] = m[:, h + 1:]
    out[:, h + 1:] = m[:, 1:h]
    return out


def inverse_parts(n, cols):
    h = n // 2
    t, f = np.arange(cols)[None, :], np.arange(1, h)[:, None]
    cos, sin = 2 * np.cos(2 * np.pi * f * t / n), 2 * np.sin(2 * np.pi * f * t / n)
    one, alt = np.ones((1, cols)), np.cos(np.pi * np.arange(cols))[None]
    a = np.concatenate([one, cos, alt, cos]) / n
    b = np.concatenate([0 * one, -sin, 0 * alt, sin]) / n
    return a, b


def correlation_tables():
    two = lambda m: np.kron(np.eye(2), m)
    q = dft(S, S)
    ia, ib = inverse_parts(S, S)
    w = dft(2 * S, S)
    ends = dft(2 * S, 2 * S)
    v = np.concatenate([ends[:S - 1], ends[S - 1:].sum(0, keepdims=True)])
    va, vb = inverse_parts(2 * S, S)
    both = lambda m: np.concatenate([m, m])
    t = {"dft_q": two(q), "dft_qs": two(swap_parts(q, S)), "inv_a": two(ia), "inv_b": two(ib),
         "dft_w": both(w), "dft_v": both(v), "dft_vs": both(swap_parts(v, 2 * S)),
         "inv_v": np.concatenate([va, vb], axis=1)}
    return np.concatenate([t[k] for k in ("dft_q", "dft_qs", "inv_a", "inv_b", "dft_w", "dft_v", "dft_vs", "inv_v")], axis=1).astype(np.float32)


def correlation_stage(c, ctx_in, tables):
    nc = c.nc
    with Stage(nc, "corr") as s:
        m = s.sb("m", [P, 8, P])
        cin = s.sb("cin", [P, 2, 2, D])
        xn = s.sb("xn", [P, 2, D])
        kf = s.sb("kf", [P, D])
        pa = s.sb("pa", [P, 2, 2, D])
        top = s.sb("top", [P, 8, TOP])
        z = s.sb("z", [P, 8, S])
        cor = s.sb("cor", [P, 8, S])
        e = s.sb("e", [P, 8, S])
        te = s.sb("te", [P, 8, TOP])
        sm = s.sb("sm", [P, 8])
        wT = s.sb("wT", [P, D])
        wf = s.sb("wf", [P, 2, D])
        pv = s.sb("pv", [P, 2, 2, D])
        qf_ps = s.ps("qf", [P, 2, D])
        kf_ps = s.ps("kf_ps", [P, D])
        cor_ps = s.ps("cor_ps", [P, 8, S])
        wT_ps = s.ps("wT_ps", [P, D])
        vf_ps = s.ps("vf_ps", [P, 2, D])
        y_ps = s.ps("y_ps", [P, D])
        m_in, k_in, v_in, xn_ready = s.sem("m_in"), s.sems("k_in"), s.sems("v_in"), s.sem("xn")
        kf_made, kf_out, qf_made, qf_used = s.sem("kf_made"), s.sem("kf_out"), s.sem("qf_made"), s.sem("qf_used")
        cor_made, cor_out, chain, shifted, exped = s.sem("cor_made"), s.sem("cor_out"), s.sem("chain"), s.sem("shifted"), s.sem("exped")
        w_ready, wT_made, wT_out = s.sem("w_ready"), s.sem("wT_made"), s.sem("wT_out")
        wf_made, wf_out, vf_made, vf_used, summed, x_new, stats = (s.sem(n) for n in ("wf_made", "wf_out", "vf_made", "vf_used", "summed", "x_new", "stats"))
        with nc.Block() as block:
            @block.sync
            def _(sp):
                sp.dma_start(m[:, :, :], tables.rearrange("p (n f) -> p n f", n=8)).then_inc(m_in, 16)
                rows = rows_of(ctx_in)
                for u in range(2):
                    sp.dma_start(cin[:, 0, u, :], rows[:, u, :]).then_inc(k_in[u], 16)
                for u in range(2):
                    sp.dma_start(cin[:, 1, u, :], rows[:, u, :]).then_inc(v_in[u], 16)
                with sp.Fori(0, TURNS - 1) as j:
                    for u in range(2):
                        sp.wait_ge(kf_made, j * 2 + (u + 1))
                        sp.dma_start(cin[:, 0, u, :], rows[:, 2 * j + u + 2, :]).then_inc(k_in[u], 16)
                        sp.wait_ge(vf_made, j * 4 + (2 * u + 2))
                        sp.dma_start(cin[:, 1, u, :], rows[:, 2 * j + u + 2, :]).then_inc(v_in[u], 16)


            @block.tensor
            def _(pe):
                pe.wait_ge(m_in, 16)

                def values(p, par, b):
                    half = slice(S * b, S * b + S)
                    need(pe, v_in[par], (p - par) * 8 + 16)
                    need(pe, vf_used, p * 2 + b)
                    for n in range(2):
                        ins = pe.matmul(vf_ps[:, n, :], m[half, 5 + n, :], cin[half, 1, par, :], start=True, stop=True)
                    ins.then_inc(vf_made, 1)

                def weights(p, b, keys):
                    half = slice(S * b, S * b + S)
                    need(pe, wT_out, p + 1)
                    need(pe, kf_out, keys)
                    need(pe, wf_out, p * 2 + b)
                    pe.matmul(kf_ps[:, :], m[half, 4, :], wT[half, :], start=True, stop=True).then_inc(wf_made, 1)

                def step(i, par, has):
                    if has(0):
                        need(pe, w_ready, i + 1)
                        need(pe, wT_out, i)
                        for k in range(KT):
                            ins = pe.transpose(wT_ps[:, P * k:P * k + P], e[:, 2 * k:2 * k + 2, :].rearrange("p a b -> p (a b)"), c.ident[:, :])
                        ins.then_inc(wT_made, 1)
                    if has(1):
                        need(pe, qf_used, i * 2 + 4)
                        need(pe, cor_out, i + 1)
                        for k in range(KT):
                            for n in range(2):
                                ins = pe.matmul(cor_ps[:, 2 * k:2 * k + 2, :].rearrange("p a b -> p (a b)"), pa[:, 1 - par, n, P * k:P * k + P], m[:, 2 + n, :],
                                                start=(n == 0), stop=(n == 1))
                        ins.then_inc(cor_made, 1)
                    if has(0):
                        weights(i, 0, i + 2 if not isinstance(i, int) else min(i + 2, PAIRS))
                        values(i, par, 0)
                    if has(2):
                        p = i + 2
                        need(pe, k_in[par], (p - par) * 8 + 16)
                        need(pe, kf_out, p)
                        need(pe, wf_out, 2 * i + 1)
                        pe.matmul(kf_ps[:, :], m[:, 0, :], cin[:, 0, par, :], start=True, stop=True).then_inc(kf_made, 1)
                        need(pe, xn_ready, p + 1)
                        need(pe, qf_used, p * 2)
                        for n in range(2):
                            ins = pe.matmul(qf_ps[:, n, :], m[:, n, :], xn[:, par, :], start=True, stop=True)
                        ins.then_inc(qf_made, 1)
                    if has(0):
                        weights(i, 1, i + 3 if not isinstance(i, int) else min(i + 3, PAIRS))
                        values(i, par, 1)
                        for b in range(2):
                            need(pe, vf_used, i * 2 + b + 1)
                            need(pe, x_new, i)
                            for n in range(2):
                                ins = pe.matmul(y_ps[S * b:S * b + S, :], m[:, 7, S * n:S * n + S], pv[:, b, n, :], start=(n == 0), stop=(n == 1))
                        ins.then_inc(summed, 1)

                pipelined(pe, step, 0, 2)

            @block.scalar
            def _(act):
                def weights(p, b):
                    need(act, wf_made, p * 2 + b + 1)
                    need(act, vf_used, p * 2)
                    act.copy(wf[:, b, :], kf_ps[:, :]).then_inc(wf_out, 1)

                def step(i, par, has):
                    if has(0):
                        need(act, wT_made, i + 1)
                        need(act, wf_made, i * 2)
                        act.copy(wT[:, :], wT_ps[:, :]).then_inc(wT_out, 1)
                    if has(1):
                        need(act, cor_made, i + 2)
                        need(act, w_ready, i + 1)
                        act.copy(cor[:, :, :], cor_ps[:, :, :]).then_inc(cor_out, 1)
                    if has(0):
                        weights(i, 0)
                    if has(2):
                        need(act, kf_made, i + 3)
                        need(act, qf_used, i * 2 + 4)
                        act.copy(kf[:, :], kf_ps[:, :]).then_inc(kf_out, 1)
                    if has(1):
                        need(act, shifted, i + 2)
                        act.activation(te[:, :, :], te[:, :, :], ACT.Exp).then_inc(exped, 1)
                        act.activation(e[:, :, :], e[:, :, :], ACT.Exp).then_inc(exped, 1)
                    if has(0):
                        weights(i, 1)

                pipelined(act, step, 0, 2)

            @block.vector
            def _(dve):
                def values(p, b):
                    need(dve, vf_made, p * 2 + b + 1)
                    need(dve, wf_out, p * 2 + b + 1)
                    need(dve, summed, p)
                    dve.tensor_tensor(pv[:, b, :, :], vf_ps[:, :, :], wf[:, b:b + 1, :].to_broadcast([P, 2, D]), ALU.mult).then_inc(vf_used, 1)

                def step(i, par, has):
                    if has(2):
                        need(dve, qf_made, i + 1)
                        normalised(c, dve, xn[:, par, :], i + 2).then_inc(xn_ready, 1)
                    if has(1):
                        ch = Chain(dve, chain, i + 1, 6)
                        need(dve, cor_out, i + 2)
                        need(dve, wT_made, i + 1)
                        dve.tensor_copy(sm[:, 0:1], cor[:, 0, 0:1])
                        for g in range(8):
                            ins = dve.max(out=top[:, g, :], in_=cor[:, g, :])
                        ch.step(ins)
                        dve.tensor_tensor(te[:, :, :], top[:, :, :], spread(top[:, :, 0], TOP), ALU.subtract)
                        dve.tensor_tensor(e[:, :, :], cor[:, :, :], spread(top[:, :, 0], S), ALU.subtract).then_inc(shifted, 1)
                        for g in range(8):
                            ins = dve.match_replace(out=z[:, g, :], in_to_replace=top[:, g, :], in_values=cor[:, g, :], imm_value=LOW)
                        ch.step(ins)
                        ch.step(dve.tensor_tensor(z[:, :, :], cor[:, :, :], z[:, :, :], ALU.not_equal))
                    if has(0):
                        values(i, 0)
                    if has(2):
                        need(dve, qf_made, i + 3)
                        need(dve, kf_out, i + 3)
                        need(dve, cor_made, i + 1)
                        for n in range(2):
                            dve.tensor_tensor(pa[:, par, n, :], qf_ps[:, n, :], kf[:, :], ALU.mult).then_inc(qf_used, 1)
                    if has(1):
                        need(dve, exped, i * 2 + 4)
                        ch.step(dve.tensor_reduce(sm[:, :], te[:, :, :], X, ALU.add))
                        ch.step(dve.reciprocal(sm[:, :], sm[:, :]))
                        ch.step(dve.tensor_tensor(e[:, :, :], e[:, :, :], z[:, :, :], ALU.mult))
                        dve.tensor_tensor(e[:, :, :], e[:, :, :], spread(sm[:, :], S), ALU.mult).then_inc(w_ready, 1)
                        ch.end()
                    if has(0):
                        values(i, 1)
                        need(dve, summed, i + 1)
                        dve.scalar_tensor_tensor(out=c.x[:, i, :], in0=y_ps[:, :], scalar=c.gate[:, 2:3], in1=c.x[:, i, :],
                                                 op0=ALU.mult, op1=ALU.add).then_inc(x_new, 1)
                        need(dve, x_new, i + 1)
                        dve.bn_stats(c.stats[:, i, :], c.x[:, i, :]).then_inc(stats, 1)

                pipelined(dve, step, 0, 2)


FP8_MAX = 448.0
EXP_BITS = 0x7F800000


def fp8_linear_stage(c, w8T, w_scale, bias16):
    nc = c.nc
    with Stage(nc, "fp8") as s:
        xn = s.sb("xn", [P, PAIRS, D])
        mags = s.sb("mags", [P, PAIRS])
        amax, amax_all, sc = s.sb("amax", [P, 1]), s.sb("amax_all", [P, 1]), s.sb("sc", [P, 4])
        w_raw = s.sb("w_raw", [P, KT, D], U8)
        w_int = s.sb("w_int", [P, KT, D], I32)
        w_t = s.sb("w_t", [P, KT, D], I32)
        w_a = s.sb("w_a", [P, KT, D])
        w = s.sb("w", [P, KT, D], BF16)
        bias = s.sb("bias", [P, D], BF16)
        ws = s.sb("ws", [P, 1])
        y = s.sb("y", [P, 2, D])
        unit = s.sb("unit", [P, 2, D])
        q = s.sb("q", [P, 2, D], BF16)
        xT = s.sb("xT", [P, 2, KT, P], BF16)
        o16 = s.sb("o16", [P, 2, D], BF16)
        xT_ps = s.ps("xT_ps", [P, 2, 2 * KT, P], BF16)
        y_ps = s.ps("y_ps", [P, 2, D])
        w_in, b_in, chain, maxed, scaled = s.sem("w_in"), s.sem("b_in"), s.sem("chain"), s.sem("maxed"), s.sem("scaled")
        xn_made, w_made, reduced = s.sem("xn_made"), s.sem("w_made"), s.sem("reduced")
        x_scaled, stats = s.sem("x_scaled"), s.sem("stats")
        bounded, united, q_ready, lchain = s.sem("bounded"), s.sem("united"), s.sem("q_ready"), s.sem("lchain")
        xT_made, xT_out, summed, out_ready, x_new = (s.sem(n) for n in ("xT_made", "xT_out", "summed", "out_ready", "x_new"))
        with nc.Block() as block:
            @block.sync
            def _(sp):
                sp.dma_start(w_raw[:, :, :], w8T.rearrange("(k p) n -> p k n", p=P)).then_inc(w_in, 16)
                sp.dma_start(bias[:, :], bias16.rearrange("(o n) -> o n", o=1).to_broadcast([P, D])).then_inc(b_in, 16)
                sp.dma_start(ws[:, :], w_scale.rearrange("(o n) -> o n", o=1).to_broadcast([P, 1])).then_inc(b_in, 16)

            @block.gpsimd
            def _(pool):
                pool.wait_ge(maxed, 1)
                pool.partition_all_reduce(amax_all[:, :], amax[:, :], P, RMAX).then_inc(reduced, 1)
                pool.wait_ge(scaled, 1)

                def step(v, par, has):
                    if has(0):
                        need(pool, out_ready, v + 1)
                        pool.tensor_tensor(o16[:, par, :], o16[:, par, :], bias[:, :], ALU.add).then_inc(bounded, 1)

                pipelined(pool, step, 0, 2)

            @block.vector
            def _(dve):
                for t in range(PAIRS):
                    dve.wait_ge(xn_made, t + 1)
                    ins = dve.tensor_reduce(mags[:, t:t + 1], xn[:, t, :], X, ALU.max, apply_absolute_value=True)
                ch = Chain(dve, chain)
                ch.step(ins)
                dve.tensor_reduce(amax[:, :], mags[:, :], X, ALU.max).then_inc(maxed, 1)
                dve.wait_ge(w_in, 16)
                ch.step(dve.tensor_copy(w_int[:, :, :], w_raw[:, :, :]))
                ch.step(dve.tensor_scalar(w_t[:, :, :], w_int[:, :, :], 0x7F, 20, ALU.bitwise_and, ALU.logical_shift_left))
                ch.step(dve.tensor_scalar(w_t[:, :, :], w_t[:, :, :], 0x40000000, None, ALU.bitwise_or))
                ch.step(dve.tensor_scalar(w_a[:, :, :], w_t[:, :, :].bitcast(F32), 2.0 ** -7, -2.0 ** -6, ALU.mult, ALU.add))
                ch.step(dve.scalar_tensor_tensor(out=w_a[:, :, :], in0=w_t[:, :, :].bitcast(F32), scalar=2.0 ** -8, in1=w_a[:, :, :],
                                                 op0=ALU.mult, op1=ALU.min))
                ch.step(dve.tensor_scalar(w_int[:, :, :], w_int[:, :, :], 0x80, 24, ALU.bitwise_and, ALU.logical_shift_left))
                ch.step(dve.tensor_tensor(w_int[:, :, :], w_int[:, :, :], w_a[:, :, :].bitcast(I32), ALU.bitwise_or))
                ch.step(dve.tensor_copy(w[:, :, :], w_int[:, :, :].bitcast(F32)))
                dve.sem_inc(w_made, 1)
                dve.wait_ge(reduced, 1)
                dve.wait_ge(b_in, 32)
                ch.step(dve.tensor_scalar(sc[:, 0:1], amax_all[:, :], 1.0 / FP8_MAX, 1e-12, ALU.mult, ALU.max))
                ch.step(dve.reciprocal(sc[:, 1:2], sc[:, 0:1]))
                dve.tensor_tensor(sc[:, 2:3], sc[:, 0:1], ws[:, :], ALU.mult).then_inc(scaled, 1)
                dve.wait_ge(scaled, 1)

                def step(v, par, has):
                    if has(1):
                        u = 1 - par
                        need(dve, x_scaled, v + 2)
                        lc = Chain(dve, lchain, v + 1, 3)
                        lc.step(dve.tensor_scalar(y[:, u, :], y[:, u, :], FP8_MAX, -FP8_MAX, ALU.min, ALU.max))
                        lc.step(dve.tensor_scalar(unit[:, u, :].bitcast(I32), y[:, u, :].bitcast(I32), EXP_BITS, None, ALU.bitwise_and))
                        lc.step(dve.tensor_scalar(unit[:, u, :], unit[:, u, :], 2.0 ** -6, 1.5 * 2.0 ** 20, ALU.max, ALU.mult))
                        dve.tensor_tensor(y[:, u, :], y[:, u, :], unit[:, u, :], ALU.add).then_inc(united, 1)
                        need(dve, united, v + 2)
                        need(dve, xT_made, v)
                        dve.tensor_tensor(q[:, u, :], y[:, u, :], unit[:, u, :], ALU.subtract).then_inc(q_ready, 1)
                        lc.end()
                    if has(0):
                        need(dve, bounded, v + 1)
                        dve.scalar_tensor_tensor(out=c.x[:, v, :], in0=o16[:, par, :], scalar=c.gate[:, 6:7], in1=c.x[:, v, :],
                                                 op0=ALU.mult, op1=ALU.add).then_inc(x_new, 1)
                        need(dve, x_new, v + 1)
                        dve.bn_stats(c.stats[:, v, :], c.x[:, v, :]).then_inc(stats, 1)

                pipelined(dve, step, 0, 2)

            @block.tensor
            def _(pe):
                pe.wait_ge(w_made, 1)

                def step(v, par, has):
                    if has(1):
                        u = 1 - par
                        need(pe, q_ready, v + 2)
                        need(pe, xT_out, v)
                        for k in range(KT):
                            ins = pe.transpose(xT_ps[:, u, k, :], q[:, u, P * k:P * k + P], c.identb[:, :])
                        ins.then_inc(xT_made, 1)
                        need(pe, xT_out, v + 2)
                        need(pe, out_ready, v)
                        for k in range(KT):
                            ins = pe.matmul(y_ps[:, u, :], xT[:, u, k, :], w[:, k, :], start=(k == 0), stop=(k == KT - 1))
                        ins.then_inc(summed, 1)

                pipelined(pe, step, 0, 2)

            @block.scalar
            def _(act):
                for t in range(PAIRS):
                    act.activation(xn[:, t, :], c.x[:, t, :], ACT.Identity, bias=c.shift[:, t:t + 1], scale=c.rstd[:, t:t + 1]).then_inc(xn_made, 1)
                act.wait_ge(scaled, 1)

                def step(v, par, has):
                    if has(2):
                        need(act, q_ready, v + 1)
                        act.activation(y[:, par, :], xn[:, v + 2, :], ACT.Copy, scale=sc[:, 1:2]).then_inc(x_scaled, 1)
                    if has(1):
                        u = 1 - par
                        need(act, xT_made, v + 2)
                        need(act, summed, v)
                        act.copy(xT[:, u, :, :], xT_ps[:, u, 0:KT, :]).then_inc(xT_out, 1)
                        need(act, summed, v + 2)
                        need(act, x_new, v)
                        act.activation(o16[:, u, :], y_ps[:, u, :], ACT.Copy, scale=sc[:, 2:3]).then_inc(out_ready, 1)

                pipelined(act, step, 0, 2)


HEADS3, HD3, LQ, LKV = 16, 32, 64, 32


def latent_attention_stage(c, ctxT, wq_dT, w_qk, wkv_d4, wv_u):
    nc = c.nc
    with Stage(nc, "mla") as s:
        HT = HEADS3 * LKV // P
        wq = s.sb("wq", [P, KT, LQ])
        wqk = s.sb("wqk", [LQ, HEADS3 * LKV])
        wkv = s.sb("wkv", [P, KT, P])
        wv = s.sb("wv", [LKV, D])
        xn = s.sb("xn", [P, 2, D])
        xT = s.sb("xT", [P, 2, KT, P])
        cT = s.sb("cT", [P, 2, KT, P])
        cq = s.sb("cq", [LQ, 2, P])
        ql = s.sb("ql", [P, 2, HT, P])
        kl = s.sb("kl", [LKV, 2, P])
        kbd = s.sb("kbd", [P, 2, 2, 4, S])
        v = s.sb("v", [P, 2, D])
        d = s.sb("d", [P, HEADS3, S])
        mx = s.sb("mx", [P, HEADS3])
        e = s.sb("e", [P, 2, HEADS3, P])
        sm = s.sb("sm", [P, 2, HEADS3])
        eT = s.sb("eT", [P, 2, 4, P])
        o = s.sb("o", [P, D])
        a_ps = s.ps("a_ps", [P, KT, P])
        b_ps = s.ps("b_ps", [P, 4, P])
        v_ps = s.ps("v_ps", [P, D])
        s_ps = s.ps("s_ps", [P, HEADS3, S])
        t_ps = s.ps("t_ps", [P, 2, 4, P])
        o_ps = s.ps("o_ps", [P, D])
        w_in, c_in, zeros = s.sem("w_in"), s.sems("c_in"), s.sem("zeros")
        xn_ready, xT_made, xT_out, lat_made, lat_out = (s.sem(n) for n in ("xn", "xT_made", "xT_out", "lat_made", "lat_out"))
        ql_made, ql_out, v_made, v_out = (s.sem(n) for n in ("ql_made", "ql_out", "v_made", "v_out"))
        scored, maxed, shifted, exped, sums, chain = (s.sem(n) for n in ("scored", "maxed", "shifted", "exped", "sums", "chain"))
        turned, turned_out, summed, divided, x_new = (s.sem(n) for n in ("turned", "turned_out", "summed", "divided", "x_new"))
        with nc.Block() as block:
            @block.sync
            def _(sp):
                sp.dma_start(wq[:, :, :], wq_dT.rearrange("(k p) n -> p k n", p=P)).then_inc(w_in, 16)
                sp.dma_start(wqk[:, :], w_qk).then_inc(w_in, 16)
                sp.dma_start(wkv[:, :, :], wkv_d4.rearrange("(k p) n -> p k n", p=P)).then_inc(w_in, 16)
                sp.dma_start(wv[:, :], wv_u).then_inc(w_in, 16)
                cols = ctxT.rearrange("(k p) n -> p k n", p=P)
                for u in range(2):
                    sp.dma_start(cT[:, u, :, :], cols[:, :, P * u:P * u + P]).then_inc(c_in[u], 16)
                with sp.Fori(0, TURNS - 1) as j:
                    for u in range(2):
                        sp.wait_ge(lat_made, j * 2 + (u + 1))
                        sp.dma_start(cT[:, u, :, :], cols[:, :, bass.ds((2 * j + u + 2) * P, P)]).then_inc(c_in[u], 16)


            @block.tensor
            def _(pe):
                pe.wait_ge(w_in, 64)
                pe.wait_ge(zeros, 2)

                def turn(p, par, n):
                    if n == 0:
                        need(pe, exped, p + 1)
                    need(pe, turned_out, p * 4 + max(0, n - 1))
                    for h in range(4):
                        ins = pe.transpose(t_ps[:, n % 2, h, :], e[:, par, 4 * n + h, :], c.ident[:, :])
                    ins.then_inc(turned, 1)

                def weigh(p, par, n):
                    need(pe, turned_out, p * 4 + n + 1)
                    if n == 0:
                        need(pe, divided, p)
                        need(pe, v_out, p + 1)
                    for h in range(4):
                        cols = slice(HD3 * (4 * n + h), HD3 * (4 * n + h) + HD3)
                        ins = pe.matmul(o_ps[:, cols], eT[:, n % 2, h, :], v[:, par, cols], start=True, stop=True)
                    ins.then_inc(summed, 1)

                def step(i, par, has):
                    p = i + 2
                    if has(1):
                        u = 1 - par
                        need(pe, ql_out, i + 2)
                        need(pe, shifted, i + 1)
                        for b in range(2):
                            for n in range(HT):
                                ins = pe.matmul(s_ps[S * b:S * b + S, 4 * n:4 * n + 4, :].rearrange("p h k -> p (h k)"), ql[:, u, n, S * b:S * b + S],
                                                kbd[:, u, b, :, :].rearrange("p h k -> p (h k)"), start=True, stop=True)
                        ins.then_inc(scored, 1)
                    if has(0):
                        turn(i, par, 0)
                    if has(2):
                        need(pe, xn_ready, p + 1)
                        need(pe, ql_out, p)
                        for k in range(KT):
                            ins = pe.transpose(a_ps[:, k, :], xn[:, par, P * k:P * k + P], c.ident[:, :])
                        ins.then_inc(xT_made, 1)
                    if has(0):
                        turn(i, par, 1)
                        weigh(i, par, 0)
                    if has(2):
                        need(pe, xT_out, p + 1)
                        need(pe, c_in[par], (p - par) * 8 + 16)
                        need(pe, lat_out, p)
                        for k in range(KT):
                            pe.matmul(b_ps[0:LQ, 0, :], wq[:, k, :], xT[:, par, k, :], start=(k == 0), stop=(k == KT - 1))
                        for k in range(KT):
                            ins = pe.matmul(b_ps[:, 1, :], wkv[:, k, :], cT[:, par, k, :], start=(k == 0), stop=(k == KT - 1))
                        ins.then_inc(lat_made, 1)
                    if has(0):
                        turn(i, par, 2)
                        weigh(i, par, 1)
                    if has(2):
                        need(pe, lat_out, p + 1)
                        for n in range(HT):
                            ins = pe.matmul(a_ps[:, n, :], wqk[:, P * n:P * n + P], cq[:, par, :], start=True, stop=True)
                        ins.then_inc(ql_made, 1)
                        need(pe, v_out, p)
                        pe.matmul(v_ps[:, :], kl[:, par, :], wv[:, :], start=True, stop=True).then_inc(v_made, 1)
                    if has(0):
                        turn(i, par, 3)
                        weigh(i, par, 2)
                        weigh(i, par, 3)

                pipelined(pe, step, 0, 2)

            @block.scalar
            def _(act):
                act.wait_ge(zeros, 2)

                def turned_copy(p, n):
                    need(act, turned, p * 4 + n + 1)
                    need(act, summed, p * 4 + max(0, n - 1))
                    act.copy(eT[:, n % 2, :, :], t_ps[:, n % 2, :, :]).then_inc(turned_out, 1)

                def step(i, par, has):
                    p = i + 2
                    if has(0):
                        turned_copy(i, 0)
                    if has(2):
                        need(act, xT_made, p + 1)
                        act.copy(xT[:, par, :, :], a_ps[:, :, :]).then_inc(xT_out, 1)
                    if has(0):
                        turned_copy(i, 1)
                    if has(1):
                        u = 1 - par
                        need(act, shifted, i + 2)
                        need(act, sums, i)
                        need(act, turned, 4 * i)
                        for b in range(2):
                            half = slice(S * b, S * b + S)
                            ins = act.activation(e[half, u, :, half], d[half, :, :], ACT.Exp, scale=LKV ** -0.5)
                        ins.then_inc(exped, 1)
                    if has(2):
                        need(act, lat_made, p + 1)
                        need(act, v_made, p - 1)
                        need(act, scored, p - 1)
                        act.copy(cq[:, par, :], b_ps[0:LQ, 0, :])
                        act.copy(kl[:, par, :], b_ps[0:LKV, 1, :])
                        for h in range(4):
                            part = slice(LKV * h, LKV * h + LKV)
                            ins = act.copy(kbd[part, par, :, h, :], b_ps[part, 1, :].rearrange("p (b k) -> p b k", b=2))
                        ins.then_inc(lat_out, 1)
                    if has(0):
                        turned_copy(i, 2)
                    if has(2):
                        need(act, ql_made, p + 1)
                        act.copy(ql[:, par, :, :], a_ps[:, :, :]).then_inc(ql_out, 1)
                    if has(0):
                        turned_copy(i, 3)
                    if has(2):
                        need(act, v_made, p + 1)
                        need(act, summed, 4 * (p - 1))
                        act.copy(v[:, par, :], v_ps[:, :]).then_inc(v_out, 1)

                pipelined(act, step, 0, 2)

            @block.vector
            def _(dve):
                dve.memset(kbd[:, :, :, :, :], 0.0).then_inc(zeros, 1)
                dve.memset(e[:, :, :, :], 0.0).then_inc(zeros, 1)

                def step(i, par, has):
                    if has(2):
                        need(dve, xT_made, i + 1)
                        normalised(c, dve, xn[:, par, :], i + 2).then_inc(xn_ready, 1)
                    if has(1):
                        need(dve, scored, i + 2)
                        dve.tensor_reduce(mx[:, :], s_ps[:, :, :], X, ALU.max).then_inc(maxed, 1)
                        need(dve, maxed, i + 2)
                        need(dve, exped, i + 1)
                        dve.tensor_tensor(d[:, :, :], s_ps[:, :, :], spread(mx[:, :], S), ALU.subtract).then_inc(shifted, 1)
                    if has(0):
                        ch = Chain(dve, chain, i, 2)
                        need(dve, exped, i + 1)
                        for b in range(2):
                            half = slice(S * b, S * b + S)
                            ins = dve.tensor_reduce(sm[half, 0, :], e[half, par, :, half], X, ALU.add)
                        ins.then_inc(sums, 1)
                        need(dve, sums, i + 1)
                        ch.step(dve.reciprocal(sm[:, 1, :], sm[:, 0, :]))
                        need(dve, summed, i * 4 + 4)
                        dve.tensor_tensor(o[:, :].rearrange("p (h d) -> p h d", h=HEADS3), o_ps[:, :].rearrange("p (h d) -> p h d", h=HEADS3),
                                          spread(sm[:, 1, :], HD3), ALU.mult).then_inc(divided, 1)
                        need(dve, divided, i + 1)
                        dve.scalar_tensor_tensor(out=c.x[:, i, :], in0=o[:, :], scalar=c.gate[:, 3:4], in1=c.x[:, i, :],
                                                 op0=ALU.mult, op1=ALU.add).then_inc(x_new, 1)
                        need(dve, x_new, i + 1)
                        ch.step(dve.bn_stats(c.stats[:, i, :], c.x[:, i, :]))
                        ch.end()

                pipelined(dve, step, 0, 2)


HIDDEN, RANK3 = 1376, 16
H_TILES = [(P * n, min(P, HIDDEN - P * n)) for n in range(-(-HIDDEN // P))]


def swiglu_stage(c, gate_wT, up_wT, down_wT, gate_a, gate_bT, up_a, up_bT, down_a, down_bT, out):
    nc = c.nc
    with Stage(nc, "glu") as s:
        NH = len(H_TILES)
        w = s.sb("w", [P, 2, KT, HIDDEN])
        wd = s.sb("wd", [P, NH, D])
        a = s.sb("a", [RANK3, 2, D])
        b = s.sb("b", [RANK3, 2, HIDDEN])
        da = s.sb("da", [RANK3, HIDDEN])
        db = s.sb("db", [RANK3, D])
        xn = s.sb("xn", [P, 2, D])
        xT = s.sb("xT", [P, 2, KT, STEP])
        g = s.sb("g", [P, 2, STEP])
        h = s.sb("h", [P, 2, STEP])
        p_ps = s.ps("p_ps", [P, 4, STEP])
        y_ps = s.ps("y_ps", [P, 4, D])
        w_in, lora_in = s.sems("w_in", 3), s.sem("lora_in")
        fold_made, folded = s.sem("fold_made"), s.sem("folded")
        xn_ready, xT_made, xT_out = (s.sem(n) for n in ("xn", "xT_made", "xT_out"))
        projected, silued, h_ready, downed, x_new, stored = (s.sem(n) for n in ("projected", "silued", "h_ready", "downed", "x_new", "stored"))
        used = s.sem("used")
        pieces = [(n, k, c0, min(512, HIDDEN - c0)) for n in range(2) for k in range(KT) for c0 in range(0, HIDDEN, 512)]
        FOLDS = len(pieces) + NH
        with nc.Block() as block:
            @block.sync
            def _(sp):
                for n, (x_a, x_b) in enumerate(((gate_a, gate_bT), (up_a, up_bT))):
                    sp.dma_start(a[:, n, :], x_a).then_inc(lora_in, 16)
                    sp.dma_start(b[:, n, :], x_b).then_inc(lora_in, 16)
                sp.dma_start(da[:, :], down_a).then_inc(lora_in, 16)
                sp.dma_start(db[:, :], down_bT).then_inc(lora_in, 16)
                for n, m in enumerate((gate_wT, up_wT)):
                    sp.dma_start(w[:, n, :, :], m.rearrange("(k p) n -> p k n", p=P)).then_inc(w_in[n], 16)
                full = (NH - 1) * P
                sp.dma_start(wd[:, 0:NH - 1, :], down_wT[0:full, :].rearrange("(n p) d -> p n d", p=P)).then_inc(w_in[2], 16)
                sp.dma_start(wd[0:HIDDEN - full, NH - 1, :], down_wT[full:HIDDEN, :]).then_inc(w_in[2], 16)
                rows = rows_of(out)
                with sp.Fori(0, STEPS) as j:
                    for i in range(4):
                        sp.wait_ge(x_new, j * 4 + i + 1)
                        sp.dma_start(rows[:, 4 * j + i, :], c.x[:, 4 * j + i, :]).then_inc(stored, 16)
                sp.wait_ge(stored, 16 * PAIRS)

            @block.vector
            def _(dve):
                for f in range(FOLDS):
                    dve.wait_ge(fold_made, f + 1)
                    if f < len(pieces):
                        n, k, c0, wid = pieces[f]
                        dve.wait_ge(w_in[n], 16)
                        dst, rows = w[:, n, k, c0:c0 + wid], P
                    else:
                        t = f - len(pieces)
                        dve.wait_ge(w_in[2], 32)
                        rows, wid = H_TILES[t][1], D
                        dst = wd[0:rows, t, :]
                    dve.tensor_tensor(dst, dst, p_ps[0:rows, f % 2, 0:wid], ALU.add).then_inc(folded, 1)
                with dve.Fori(0, STEPS) as j:
                    for i in range(4):
                        t = 4 * j + i
                        dve.wait_ge(xT_made, t)
                        normalised(c, dve, xn[:, i % 2, :], t).then_inc(xn_ready, 1)
                    for n in range(NH):
                        rows = H_TILES[n][1]
                        dve.wait_ge(silued, j * NH + n + 1)
                        dve.wait_ge(downed, j * NH + max(0, n - 1))
                        dve.tensor_tensor(h[0:rows, n % 2, :], g[0:rows, n % 2, :], p_ps[0:rows, 2 * (n % 2) + 1, :], ALU.mult).then_inc(h_ready, 1)
                    for i in range(4):
                        t = 4 * j + i
                        dve.wait_ge(downed, j * NH + NH)
                        dve.scalar_tensor_tensor(out=c.x[:, t, :], in0=y_ps[:, i, :], scalar=c.gate[:, 7:8], in1=c.x[:, t, :],
                                                 op0=ALU.mult, op1=ALU.add).then_inc(x_new, 1)

            @block.scalar
            def _(act):
                with act.Fori(0, STEPS) as j:
                    for i in range(4):
                        act.wait_ge(xT_made, j * 4 + i + 1)
                        act.copy(xT[:, 0, :, P * i:P * i + P], p_ps[:, i % 2, :].rearrange("p (k r) -> p k r", k=KT)).then_inc(xT_out, 1)
                    for n in range(NH):
                        rows = H_TILES[n][1]
                        act.wait_ge(projected, j * NH + n + 1)
                        act.wait_ge(h_ready, j * NH + max(0, n - 1))
                        act.activation(g[0:rows, n % 2, :], p_ps[0:rows, 2 * (n % 2), :], ACT.Silu).then_inc(silued, 1)

            @block.tensor
            def _(pe):
                pe.wait_ge(lora_in, 96)
                for f in range(FOLDS):
                    pe.wait_ge(folded, f - 1) if f >= 2 else None
                    if f < len(pieces):
                        n, k, c0, wid = pieces[f]
                        ins = pe.matmul(p_ps[:, f % 2, 0:wid], a[:, n, P * k:P * k + P], b[:, n, c0:c0 + wid], start=True, stop=True)
                    else:
                        c0, rows = H_TILES[f - len(pieces)]
                        ins = pe.matmul(p_ps[0:rows, f % 2, :], da[:, c0:c0 + rows], db[:, :], start=True, stop=True)
                    ins.then_inc(fold_made, 1)
                pe.wait_ge(folded, FOLDS)
                with pe.Fori(0, STEPS) as j:
                    for i in range(4):
                        pe.wait_ge(xn_ready, j * 4 + i + 1)
                        pe.wait_ge(xT_out, j * 4 + max(0, i - 1))
                        if i == 0:
                            pe.wait_ge(h_ready, j * NH)
                        for k in range(KT):
                            ins = pe.transpose(p_ps[:, i % 2, P * k:P * k + P], xn[:, i % 2, P * k:P * k + P], c.ident[:, :])
                        ins.then_inc(xT_made, 1)
                    pe.wait_ge(xT_out, j * 4 + 4)
                    for n in range(NH + 1):
                        if n < NH:
                            c0, rows = H_TILES[n]
                            pe.wait_ge(h_ready, j * NH + max(0, n - 1))
                            for m in range(2):
                                for k in range(KT):
                                    ins = pe.matmul(p_ps[0:rows, 2 * (n % 2) + m, :], w[:, m, k, c0:c0 + rows], xT[:, 0, k, :], start=(k == 0), stop=(k == KT - 1))
                            ins.then_inc(projected, 1)
                        if n > 0:
                            q, rows = n - 1, H_TILES[n - 1][1]
                            pe.wait_ge(h_ready, j * NH + q + 1)
                            if q == 0:
                                pe.wait_ge(x_new, j * 4)
                            for i in range(4):
                                ins = pe.matmul(y_ps[:, i, :], h[0:rows, q % 2, P * i:P * i + P], wd[0:rows, q, :], start=(q == 0), stop=(q == NH - 1))
                            ins.then_inc(downed, 1)


def store_stage(c, out):
    nc = c.nc
    with Stage(nc, "store") as s:
        stored = s.sem("stored")
        with nc.Block() as block:
            @block.sync
            def _(sp):
                for q in range(4):
                    sp.dma_start(rows_of(out)[:, 4 * q:4 * q + 4, :], c.x[:, 4 * q:4 * q + 4, :]).then_inc(stored, 16)
                sp.wait_ge(stored, 64)


def program(nc, a, out, first=0, last=7):
    with ExitStack() as ctx:
        c = Core(nc, ctx)
        load_stage(c, a["x"], a["g_xattn"], a["g_ffn"])
        for n in range(first, last + 1):
            norm_stage(c, f"norm{n}")
            STAGES[n](c, {**a, "out": out})
        if last < 7:
            store_stage(c, out)


def _window(c, a):
    window_attention_stage(c, a["ctx"], *[a[f"w0{k}T"] for k in "qkvo"], *[a[f"b0{k}"] for k in "qkvo"], a["sum_heads"], a["expand_heads"])


def _moe(c, a):
    lora_mixture_stage(c, a["a0T"], a["b0T"], a["router_b"])


def _gqa(c, a):
    with Stage(c.nc, "gqa_in") as s:
        cosT, sinT = s.sb("cosT", [P, B * S]), s.sb("sinT", [P, B * S])
        limit = s.sb("limit", [P, PAIRS, S])
        xT, cT = s.sb("xT", [P, KT, B * S]), s.sb("cT", [P, KT, B * S])
        rope_stage(c, a["pos"], a["mask"], a["rope"], cosT, sinT, limit)
        transposed_norm_stage(c, xT, "xT")
        grouped_attention_stage(c, a["ctxT"], a["w1q"], a["w1k"], a["w1v"], a["w1o"], cosT, sinT, limit, xT, cT)
    stats_stage(c, "gqa_stats")


def _lora(c, a):
    lora_linear_stage(c, a["w1"], a["b1"], a["gate1"], a["eye32"], a["a1"], a["b1T"], a["a1sT"], a["b1sT"])


def _corr(c, a):
    correlation_stage(c, a["ctx"], a["dfts"])


def _fp8(c, a):
    fp8_linear_stage(c, a["w8T"], a["w8_scale"], a["b8"])


def _mla(c, a):
    latent_attention_stage(c, a["ctxT"], a["wq_d"], a["w_qk"], a["wkv_d4"], a["wv_u"])


def _glu(c, a):
    swiglu_stage(c, *[a[k] for k in ("gate_wT", "up_wT", "down_wT", "gate_a", "gate_bT", "up_a", "up_bT", "down_a", "down_bT")], a["out"])


STAGES = (_window, _moe, _gqa, _lora, _corr, _fp8, _mla, _glu)


def layouts(i):
    t = lambda w: np.ascontiguousarray(np.asarray(w).T)
    m = {"x": np.asarray(i["x"]), "ctx": np.asarray(i["ctx_4096"]), "g_xattn": np.asarray(i["g_xattn"]), "g_ffn": np.asarray(i["g_ffn"])}
    for k in "qkvo":
        m[f"w0{k}T"] = t(i[f"L0_xattn_W{k}"])
        m[f"b0{k}"] = np.asarray(i[f"L0_xattn_b{k}"])
    m["a0T"] = t(np.concatenate([np.asarray(i["L0_ffn_A"]).reshape(ER, D), np.asarray(i["L0_ffn_router_w"])]))
    m["b0T"] = np.ascontiguousarray(np.asarray(i["L0_ffn_Bm"]).transpose(0, 2, 1).reshape(ER, D))
    m["pos"], m["mask"] = np.asarray(i["pos_BxS2"]), np.asarray(i["mask_BxSxS2_ik0"])
    m["rope"] = rope_tables()
    m["ctxT"] = t(np.asarray(i["ctx_4096"]).reshape(B * S, D))
    for k in "qkvo":
        m[f"w1{k}"] = np.asarray(i[f"L1_xattn_W{k}"])
    m["w1"], m["b1"] = np.asarray(i["L1_ffn_kernel"]), np.asarray(i["L1_ffn_bias"])
    m["gate1"] = np.ascontiguousarray(np.repeat(np.asarray(i["L1_ffn_gate"]).T, RANK1, axis=0).reshape(4, P, GROUPS1).transpose(1, 0, 2))
    m["eye32"] = np.tile(np.eye(RANK1, dtype=np.float32), (4, 1))
    m["a1"] = np.asarray(i["L1_ffn_lora_A"]).reshape(NR, D)
    m["b1T"] = np.ascontiguousarray(np.asarray(i["L1_ffn_lora_B"]).transpose(0, 2, 1).reshape(NR, D))
    m["a1sT"], m["b1sT"] = t(i["L1_ffn_lora_A_shared"]), t(i["L1_ffn_lora_B_shared"])
    m["dfts"] = correlation_tables()
    m["w8T"] = t(np.asarray(i["L2_ffn_weight_fp8"]).view(np.uint8))
    m["w8_scale"] = np.asarray(i["L2_ffn_weight_scale"]).reshape(1)
    m["b8"] = np.asarray(i["L2_ffn_bias"])
    m["wq_d"], m["w_qk"], m["wv_u"] = (np.asarray(i[f"L3_xattn_{k}"]) for k in ("Wq_d", "W_qk", "Wv_u"))
    m["wkv_d4"] = np.tile(np.asarray(i["L3_xattn_Wkv_d"]), (1, 4))
    for k in ("gate_w", "up_w", "down_w", "gate_b", "up_b", "down_b"):
        m[f"{k}T"] = t(i[f"L3_ffn_{k}"])
    for k in ("gate_a", "up_a", "down_a"):
        m[k] = np.asarray(i[f"L3_ffn_{k}"])
    m["router_b"] = np.asarray(i["L0_ffn_router_b"])
    m.update(window_tables())
    return m


def window_tables():
    p = np.arange(P)
    head = p // HD0
    sums = np.zeros((P, 2, 32), np.float32)
    expand = np.zeros((2, PARTS, BH, 2, P), np.float32)
    for par in range(2):
        sums[p, par, BH * par + head] = 1
        for part in range(PARTS):
            expand[par, part, head, par, p] = 1
    return {"sum_heads": sums, "expand_heads": expand.reshape(2 * PARTS * BH, 2, P)}


def kernel(**inputs):
    import concourse.bacc as bacc
    from concourse.bass_utils import run_bass_kernel_spmd

    nc = bacc.Bacc("TRN2", target_bir_lowering=False, num_devices=1)
    arrays = layouts(inputs)
    aps = {name: nc.dram_tensor(name, v.shape, mybir.dt.from_np(v.dtype), kind="ExternalInput").ap() for name, v in arrays.items()}
    out = nc.dram_tensor("y", (B, S, D), F32, kind="ExternalOutput").ap()
    program(nc, aps, out)
    return run_bass_kernel_spmd(nc, [arrays], core_ids=[0]).results[0]["y"]
```

```python
from contextlib import ExitStack

import concourse.bass as bass
import numpy as np
from concourse import mybir

F32 = mybir.dt.float32
BF16 = mybir.dt.bfloat16
I32 = mybir.dt.int32
U32 = mybir.dt.uint32
U8 = mybir.dt.uint8
F16 = mybir.dt.float16
ALU = mybir.AluOpType
ACT = mybir.ActivationFunctionType
X = mybir.AxisListType.X
RMAX = bass.bass_isa.ReduceOp.max

B, S, D = 32, 64, 512
P = 128
PAIRS = B * S // P
KT = D // P
EPS = 1e-5
TURNS = PAIRS // 2


def at(j, per, k):
    return j * per + k


def overlapped(ap, step, count, width):
    part = ap.ap[0]
    return bass.AP(tensor=ap.tensor, offset=ap.offset, ap=[list(part), [step, count], [1, width]])


def spread(ap, count):
    return ap.unsqueeze(len(ap.shape)).to_broadcast([*ap.shape, count])


class Stage:

    def __init__(self, nc, name):
        self.nc, self.name, self.ctx, self.used = nc, name, ExitStack(), []

    def __enter__(self):
        self.ctx.__enter__()
        return self

    def __exit__(self, *e):
        self.nc.clear_and_free_semaphores(self.used)
        self.nc.all_engine_barrier()
        return self.ctx.__exit__(*e)

    def sb(self, name, shape, dt=F32):
        return self.ctx.enter_context(self.nc.sbuf_tensor(f"{self.name}_{name}", shape, dt))

    def ps(self, name, shape, dt=F32):
        return self.ctx.enter_context(self.nc.psum_tensor(f"{self.name}_{name}", shape, dt))

    def sem(self, name):
        self.used.append(self.nc.alloc_semaphore(f"{self.name}_{name}"))
        return self.used[-1]

    def sems(self, name, n=2):
        return [self.sem(f"{name}{u}") for u in range(n)]


class Chain:

    def __init__(self, eng, sem, turn=0, per=0):
        self.eng, self.sem, self.base, self.per, self.n = eng, sem, turn * per, per, 0

    def step(self, ins):
        self.n += 1
        ins.then_inc(self.sem, 1)
        self.eng.wait_ge(self.sem, self.base + self.n)

    def end(self):
        assert self.n == self.per, (self.n, self.per)


class Core:

    def __init__(self, nc, ctx):
        def sb(name, shape, dt=F32):
            return ctx.enter_context(nc.sbuf_tensor(name, shape, dt))

        self.nc = nc
        self.x = sb("x_sb", [P, PAIRS, D])
        self.stats = sb("ln_stats", [P, PAIRS, 6])
        self.mv = sb("ln_mean_var", [P, PAIRS, 2])
        self.rstd = sb("ln_rstd", [P, PAIRS])
        self.shift = sb("ln_shift", [P, PAIRS])
        self.t1 = sb("ln_t1", [P, PAIRS])
        self.gate = sb("tanh_gates", [P, 8])
        self.ident = sb("ident", [P, P])
        self.identb = sb("ident_bf", [P, P], BF16)


def rows_of(ap):
    return ap.rearrange("(i b) s d -> (b s) i d", b=2)


def load_stage(c, x, g_xattn, g_ffn):
    nc = c.nc
    with Stage(nc, "load") as s:
        x_in, g_in, id_set, ids, stats = s.sem("x_in"), s.sem("g_in"), s.sem("id_set"), s.sem("ids"), s.sem("stats")
        g_raw = s.sb("g_raw", [P, 8])
        tanh_done = s.sem("tanh")
        with nc.Block() as block:
            @block.sync
            def _(sp):
                sp.dma_start(g_raw[:, 0:4], g_xattn.rearrange("(o n) -> o n", o=1).to_broadcast([P, 4])).then_inc(g_in, 16)
                sp.dma_start(g_raw[:, 4:8], g_ffn.rearrange("(o n) -> o n", o=1).to_broadcast([P, 4])).then_inc(g_in, 16)
                for q in range(4):
                    sp.dma_start(c.x[:, 4 * q:4 * q + 4, :], rows_of(x)[:, 4 * q:4 * q + 4, :]).then_inc(x_in, 16)

            @block.gpsimd
            def _(pool):
                pool.memset(c.ident[:, :], 0.0).then_inc(id_set, 1)
                pool.memset(c.identb[:, :], 0.0).then_inc(id_set, 1)
                pool.wait_ge(id_set, 2)
                for m in (c.ident, c.identb):
                    pool.affine_select(out=m[:, :], in_=m[:, :], compare_op=ALU.not_equal, fill=1.0,
                                       base=0, pattern=[[-1, P]], channel_multiplier=1).then_inc(ids, 1)

            @block.scalar
            def _(act):
                act.wait_ge(g_in, 32)
                act.activation(c.gate[:, :], g_raw[:, :], ACT.Tanh).then_inc(tanh_done, 1)

            @block.vector
            def _(dve):
                for i in range(PAIRS):
                    if i == 0:
                        dve.wait_ge(x_in, 64)
                    dve.bn_stats(c.stats[:, i, :], c.x[:, i, :]).then_inc(stats, 1)


def norm_stage(c, name):
    nc = c.nc
    with Stage(nc, name) as s:
        aggr, var_ready, root_ready, chain = s.sem("aggr"), s.sem("var"), s.sem("root"), s.sem("chain")
        var, root, t = s.sb("var", [P, PAIRS]), s.sb("root", [P, PAIRS]), s.sb("t", [P, PAIRS])
        with nc.Block() as block:
            @block.vector
            def _(dve):
                for i in range(PAIRS):
                    dve.bn_aggr(c.mv[:, i, :], c.stats[:, i, :]).then_inc(aggr, 1)
                dve.wait_ge(aggr, PAIRS)
                dve.tensor_scalar(var[:, :], c.mv[:, :, 1], EPS, None, ALU.add).then_inc(var_ready, 1)
                dve.wait_ge(root_ready, 1)
                dve.wait_ge(var_ready, 1)
                ch = Chain(dve, chain)
                ch.step(dve.reciprocal(c.rstd[:, :], root[:, :]))
                ch.step(dve.tensor_tensor(t[:, :], c.rstd[:, :], c.rstd[:, :], ALU.mult))
                ch.step(dve.tensor_tensor(t[:, :], t[:, :], var[:, :], ALU.mult))
                ch.step(dve.tensor_scalar(t[:, :], t[:, :], -0.5, 1.5, ALU.mult, ALU.add))
                ch.step(dve.tensor_tensor(c.rstd[:, :], c.rstd[:, :], t[:, :], ALU.mult))
                ch.step(dve.scalar_tensor_tensor(out=c.shift[:, :], in0=c.mv[:, :, 0], scalar=-1.0,
                                                 in1=c.rstd[:, :], op0=ALU.mult, op1=ALU.mult))

            @block.scalar
            def _(act):
                act.wait_ge(var_ready, 1)
                act.activation(root[:, :], var[:, :], ACT.Sqrt).then_inc(root_ready, 1)


def normalised(c, dve, out, t):
    t = bass.ds(t, 1)
    return dve.tensor_scalar(out, c.x[:, t, :].rearrange("p o d -> p (o d)"), c.rstd[:, t], c.shift[:, t], ALU.mult, ALU.add)


SPLIT = ((0, 0), (0, 1), (1, 0))
TOP16 = 2.0 ** 12
TINY = 1e-30


def need(eng, sem, value):
    if not isinstance(value, int) or value > 0:
        eng.wait_ge(sem, value)


def pipelined(eng, step, first, last, count=PAIRS):
    lo = -first + (-first) % 2
    hi = count - last
    hi -= (hi - lo) % 2

    def alone(v):
        step(v, v % 2, lambda off: 0 <= v + off < count)

    for v in range(-last, lo):
        alone(v)
    with eng.Fori(0, (hi - lo) // 2) as j:
        for par in range(2):
            step(2 * j + (lo + par), par, lambda off: True)
    for v in range(hi, count - first):
        alone(v)


WINDOW, HEADS0, HD0 = 16, 8, 8
PAD_L, PAD_R = WINDOW // 2, WINDOW - WINDOW // 2 - 1
BH = 2 * HEADS0
PARTS = 3


def window_attention_stage(c, ctx_in, wqT, wkT, wvT, woT, bq, bk, bv, bo, head_sums, head_spread):
    nc = c.nc
    with Stage(nc, "win") as s:
        TB = D // P
        w4 = s.sb("w4", [P, 4, P])
        bias4 = s.sb("bias4", [P, 4])
        sumw = s.sb("sumw", [P, 2, 32])
        expw = s.sb("expw", [2 * PARTS * BH, 2, P], BF16)
        expw_in = s.sb("expw_in", [2 * PARTS * BH, 2, P])
        cin = s.sb("cin", [P, 2, D])
        xn = s.sb("xn", [P, 2, D])
        q = s.sb("q", [P, 2, D])
        kp = s.sb("kp", [P, 2, D + WINDOW])
        vp = s.sb("vp", [P, 2, D + WINDOW])
        WS = 4
        prod = s.sb("prod", [P, 2, WS, D])
        dots = s.sb("dots", [P, 2, D])
        e = s.sb("e", [P, TB, WINDOW, BH])
        pr = s.sb("pr", [P, TB, WINDOW, BH])
        mx = s.sb("mx", [P, TB, BH])
        sm = s.sb("sm", [P, TB, BH])
        parts = s.sb("parts", [P, TB, WINDOW, PARTS, BH], BF16)
        pT = s.sb("pT", [2 * PARTS * BH, WINDOW // 2, D], BF16)
        pv = s.sb("pv", [P, WINDOW // 2, 2, D])
        acc = s.sb("acc", [P, 2, D])
        acc1 = s.sb("acc1", [P, D])
        upd = s.sb("upd", [P, D])
        mm = s.ps("mm", [P, D])
        dps = s.ps("dps", [P, D])
        tps = s.ps("tps", [P, TB, WINDOW, BH])
        eps_ = s.ps("eps", [P, 2, 2, D])

        w_in, w_zero, b_ready = s.sem("w_in"), s.sem("w_zero"), s.sem("b_ready")
        ctx_loaded = s.sems("ctx_loaded")
        xn_ready = s.sem("xn_ready")
        proj, outp = s.sem("proj"), s.sem("outp")
        proj_read = s.sem("proj_read")
        prod_ready, prod_used = s.sem("prod_ready"), s.sem("prod_used")
        dots_out, dotsT = s.sem("dots_out"), s.sem("dotsT")
        shifted, exped, probs, dve_chain = s.sem("shifted"), s.sem("exped"), s.sem("probs"), s.sem("dve_chain")
        hi, mid, lo, rest, rest2 = s.sem("hi"), s.sem("mid"), s.sem("lo"), s.sem("rest"), s.sem("rest2")
        pT_ps, pT_read = s.sem("pT_ps"), s.sem("pT_read")
        spread_ready, pv_ready, added, acc_ready = s.sem("spread_ready"), s.sem("pv_ready"), s.sem("added"), s.sem("acc_ready")
        upd_ready, x_new, stats = s.sem("upd_ready"), s.sem("x_new"), s.sem("stats")
        NP = WINDOW // WS
        def tpb(n):
            flat = tps[:, :, :, :].rearrange("p a b c -> p (a b c)").bitcast(BF16)
            return flat[0:2 * PARTS * BH, (n % 2) * 1024:(n % 2) * 1024 + 1024].rearrange("p (w t) -> p w t", w=2)

        with nc.Block() as block:
            @block.sync
            def _(sp):
                sp.wait_ge(w_zero, 1)
                for n, w in enumerate((wqT, wkT, wvT, woT)):
                    for b in range(2):
                        sp.dma_start(w4[64 * b:64 * b + 64, n, 64 * b:64 * b + 64], w).then_inc(w_in, 16)
                for n, w in enumerate((bq, bk, bv, bo)):
                    for b in range(2):
                        sp.dma_start(bias4[64 * b:64 * b + 64, n:n + 1], w.rearrange("(n o) -> n o", o=1)).then_inc(w_in, 16)
                sp.dma_start(sumw[:, :, :], head_sums).then_inc(w_in, 16)
                sp.dma_start(expw_in[:, :, :], head_spread).then_inc(w_in, 16)
                rows = rows_of(ctx_in)
                for u in range(2):
                    sp.dma_start(cin[:, u, :], rows[:, u, :]).then_inc(ctx_loaded[u], 16)
                with sp.Fori(0, TURNS - 1) as j:
                    for u in range(2):
                        sp.wait_ge(proj, j * 6 + 3 * u + 3)
                        sp.dma_start(cin[:, u, :], rows[:, 2 * j + u + 2, :]).then_inc(ctx_loaded[u], 16)


            @block.gpsimd
            def _(pool):
                def add(p, n):
                    need(pool, pv_ready, 8 * p + n + 1)
                    if n == 1:
                        need(pool, acc_ready, p)
                        pool.tensor_tensor(acc[:, :, :], pv[:, 0, :, :], pv[:, 1, :, :], ALU.add).then_inc(added, 2)
                    else:
                        need(pool, added, 8 * p + n)
                        pool.tensor_tensor(acc[:, :, :], acc[:, :, :], pv[:, n, :, :], ALU.add).then_inc(added, 1)

                def step(v, par, has):
                    for n in range(1, 7):
                        if has(0):
                            add(v, n)
                        if n == 3 and has(-1):
                            need(pool, upd_ready, v)
                            pool.tensor_tensor(c.x[:, v - 1, :], c.x[:, v - 1, :], upd[:, :], ALU.add).then_inc(x_new, 1)
                    if has(1):
                        need(pool, hi, v + 2)
                        pool.tensor_tensor(pr[:, :, :, :], pr[:, :, :, :], parts[:, :, :, 0, :], ALU.subtract).then_inc(rest, 1)
                    if has(0):
                        add(v, 7)
                    if has(1):
                        need(pool, mid, v + 2)
                        pool.tensor_tensor(parts[:, :, :, 2, :], pr[:, :, :, :], parts[:, :, :, 1, :], ALU.subtract).then_inc(lo, 1)
                    if has(0):
                        need(pool, added, 8 * v + 8)
                        need(pool, outp, v)
                        pool.tensor_tensor(acc1[:, :], acc[:, 0, :], acc[:, 1, :], ALU.add).then_inc(acc_ready, 1)

                pipelined(pool, step, -1, 2)

            @block.scalar
            def _(act):
                act.wait_ge(b_ready, 3)
                act.wait_ge(w_zero, 3)

                def dots_half(p, h):
                    need(act, prod_used, NP * p + (h + 1) * NP // 2)
                    need(act, dotsT, p)
                    act.copy(dots[:, h, :], dps[:, :]).then_inc(dots_out, 1)

                def step(v, par, has):
                    if has(1):
                        dots_half(v + 1, 0)
                    if has(0):
                        for n in range(4):
                            need(act, pT_ps, v * 4 + n + 1)
                            if n == 0:
                                need(act, spread_ready, v * 8)
                            act.copy(pT[:, 2 * n:2 * n + 2, :], tpb(n)).then_inc(pT_read, 1)
                    if has(1):
                        dots_half(v + 1, 1)
                    if has(-1):
                        need(act, outp, v)
                        need(act, x_new, v - 1)
                        act.activation(upd[:, :], mm[:, :], ACT.Identity, bias=bias4[:, 3:4], scale=c.gate[:, 0:1]).then_inc(upd_ready, 1)
                    if has(1):
                        need(act, shifted, v + 2)
                        act.activation(e[:, :, :, :], e[:, :, :, :], ACT.Exp).then_inc(exped, 1)
                    if has(2):
                        p = v + 2
                        need(act, proj, p * 3 + 1)
                        need(act, prod_ready, (p - 1) * NP)
                        act.activation(q[:, par, :], mm[:, :], ACT.Identity, bias=bias4[:, 0:1], scale=HD0 ** -0.5).then_inc(proj_read, 1)
                        need(act, proj, p * 3 + 2)
                        act.activation(kp[:, par, PAD_L:PAD_L + D], mm[:, :], ACT.Identity, bias=bias4[:, 1:2]).then_inc(proj_read, 1)
                        need(act, proj, p * 3 + 3)
                        need(act, pv_ready, (p - 1) * 8)
                        act.activation(vp[:, par, PAD_L:PAD_L + D], mm[:, :], ACT.Identity, bias=bias4[:, 2:3]).then_inc(proj_read, 1)
                    if has(1):
                        need(act, probs, v + 2)
                        need(act, pT_ps, (v + 1) * 4)
                        act.copy(parts[:, :, :, 0, :], pr[:, :, :, :]).then_inc(hi, 1)
                        need(act, rest, v + 2)
                        act.copy(parts[:, :, :, 1, :], pr[:, :, :, :]).then_inc(mid, 1)

                pipelined(act, step, -1, 2)

            @block.tensor
            def _(pe):
                pe.wait_ge(w_in, 16 * 18)
                pe.wait_ge(b_ready, 1)

                def reduce(p, n):
                    need(pe, prod_ready, p * NP + n + 1)
                    need(pe, dots_out, 2 * p + n // 2)
                    for wl in range(WS):
                        w = n * WS + wl
                        g, par = w % 8 // 2, w % 2
                        ins = pe.matmul(dps[32 * g:32 * g + 32, :], sumw[:, par, :], prod[:, n % 2, wl, :],
                                        start=(par == 0), stop=(par == 1))
                    ins.then_inc(prod_used, 1)

                def spread_probs(p, n):
                    if n % 2 == 0:
                        need(pe, pT_read, p * 4 + n // 2 + 1)
                    need(pe, pv_ready, p * 8 + n - 1)
                    for par in range(2):
                        ins = pe.matmul(eps_[:, n % 2, par, :], expw[:, par, :], pT[:, n, :], start=True, stop=True)
                    ins.then_inc(spread_ready, 1)

                def step(v, par, has):
                    if has(1):
                        for n in range(3):
                            reduce(v + 1, n)
                    if has(0):
                        need(pe, lo, v + 1)
                        for n in range(4):
                            need(pe, pT_read, v * 4 + max(0, n - 1))
                            for wp in range(2):
                                for tb in range(TB):
                                    ins = pe.transpose(tpb(n)[:, wp, P * tb:P * tb + P],
                                                       parts[:, tb, 4 * n + 2 * wp:4 * n + 2 * wp + 2, :, :].rearrange("p a b c -> p (a b c)"),
                                                       c.identb[:, :])
                            ins.then_inc(pT_ps, 1)
                        spread_probs(v, 0)
                        spread_probs(v, 1)
                    if has(1):
                        reduce(v + 1, 3)
                    if has(0):
                        spread_probs(v, 2)
                        spread_probs(v, 3)
                    if has(-1):
                        need(pe, acc_ready, v)
                        need(pe, proj_read, min(3 * v + 6, 3 * PAIRS) if isinstance(v, int) else 3 * v + 6)
                        pe.matmul(mm[:, :], w4[:, 3, :], acc1[:, :], start=True, stop=True).then_inc(outp, 1)
                    if has(1):
                        need(pe, dots_out, 2 * v + 4)
                        need(pe, pT_read, 4 * v + 4)
                        for tb in range(TB):
                            for half in range(2):
                                ins = pe.transpose(tps[:, tb, 8 * half:8 * half + 8, :].rearrange("p a b -> p (a b)"),
                                                   dots[:, half, P * tb:P * tb + P], c.ident[:, :])
                        ins.then_inc(dotsT, 1)
                    if has(0):
                        for n in range(4, 8):
                            spread_probs(v, n)
                    if has(2):
                        p = v + 2
                        need(pe, xn_ready, p + 1)
                        need(pe, upd_ready, p - 2)
                        pe.matmul(mm[:, :], w4[:, 0, :], xn[:, par, :], start=True, stop=True).then_inc(proj, 1)
                        need(pe, ctx_loaded[par], 16 * (p // 2 + 1) if isinstance(p, int) else (p - par) * 8 + 16)
                        need(pe, proj_read, p * 3 + 1)
                        pe.matmul(mm[:, :], w4[:, 1, :], cin[:, par, :], start=True, stop=True).then_inc(proj, 1)
                        need(pe, proj_read, p * 3 + 2)
                        pe.matmul(mm[:, :], w4[:, 2, :], cin[:, par, :], start=True, stop=True).then_inc(proj, 1)

                pipelined(pe, step, -1, 2)

            @block.vector
            def _(dve):
                dve.memset(w4[:, :, :], 0.0).then_inc(w_zero, 1)
                dve.memset(kp[:, :, :], 0.0).then_inc(w_zero, 1)
                dve.memset(vp[:, :, :], 0.0).then_inc(w_zero, 1)
                dve.wait_ge(w_in, 16 * 18)
                dve.tensor_copy(expw[:, :, :], expw_in[:, :, :]).then_inc(b_ready, 1)
                dve.tensor_scalar(bias4[:, 0:1], bias4[:, 0:1], HD0 ** -0.5, None, ALU.mult).then_inc(b_ready, 1)
                dve.tensor_scalar(bias4[:, 3:4], bias4[:, 3:4], c.gate[:, 0:1], None, ALU.mult).then_inc(b_ready, 1)

                def weigh(p, par, n):
                    need(dve, spread_ready, p * 8 + n + 1)
                    need(dve, added, 8 * (p - 1) + max(2, n + 1))
                    dve.tensor_tensor(pv[:, n, :, :], eps_[:, n % 2, :, :], overlapped(vp[:, par, 2 * n:2 * n + D], 1, 2, D),
                                      ALU.mult).then_inc(pv_ready, 1)

                def step(v, par, has):
                    if has(1):
                        p, other = v + 1, 1 - par
                        need(dve, proj_read, p * 3 + 2)
                        for n in range(NP):
                            need(dve, prod_used, p * NP + n - 1)
                            dve.tensor_tensor(prod[:, n % 2, :, :],
                                              q[:, other:other + 1, :].to_broadcast([P, WS, D]),
                                              overlapped(kp[:, other, WS * n:WS * n + D], 1, WS, D), ALU.mult).then_inc(prod_ready, 1)
                    if has(0):
                        need(dve, proj_read, v * 3 + 3)
                        for n in range(4):
                            weigh(v, par, n)
                    if has(1):
                        need(dve, dotsT, p + 1)
                        ch = Chain(dve, dve_chain, p, 3)
                        ch.step(dve.tensor_reduce(mx[:, :, :], tps[:, :, :, :].rearrange("p a w b -> p a b w"), X, ALU.max))
                        dve.tensor_tensor(e[:, :, :, :], tps[:, :, :, :], mx[:, :, :].unsqueeze(2).to_broadcast([P, TB, WINDOW, BH]),
                                          ALU.subtract).then_inc(shifted, 1)
                    if has(0):
                        for n in range(4, 8):
                            weigh(v, par, n)
                    if has(2):
                        need(dve, proj, 3 * v + 1)
                        normalised(c, dve, xn[:, par, :], v + 2).then_inc(xn_ready, 1)
                    if has(1):
                        need(dve, exped, p + 1)
                        ch.step(dve.tensor_reduce(sm[:, :, :], e[:, :, :, :].rearrange("p a w b -> p a b w"), X, ALU.add))
                        ch.step(dve.reciprocal(sm[:, :, :], sm[:, :, :]))
                        need(dve, lo, p)
                        dve.tensor_tensor(pr[:, :, :, :], e[:, :, :, :], sm[:, :, :].unsqueeze(2).to_broadcast([P, TB, WINDOW, BH]),
                                          ALU.mult).then_inc(probs, 1)
                        ch.end()
                    if has(-1):
                        need(dve, x_new, v)
                        dve.bn_stats(c.stats[:, v - 1, :], c.x[:, v - 1, :]).then_inc(stats, 1)

                pipelined(dve, step, -1, 2)


EXPERTS, RANK0 = 8, 16
SCALING0 = 8.0 / RANK0
ER = EXPERTS * RANK0


def lora_mixture_stage(c, aT, bT, router_b):
    nc = c.nc
    with Stage(nc, "moe") as s:
        a_sb = s.sb("a", [P, KT, ER + EXPERTS])
        b_sb = s.sb("b", [P, D])
        rb = s.sb("rb", [P, EXPERTS])
        g = s.sb("g", [P, 1])
        iota = s.sb("iota", [P, EXPERTS])
        xn = s.sb("xn", [P, 2, D])
        xT = s.sb("xT", [P, 2, KT, P])
        lg = s.sb("lg", [P, EXPERTS])
        top = s.sb("top", [P, 8])
        at_top = s.sb("at_top", [P, 8], U32)
        at_topf = s.sb("at_topf", [P, 8])
        diff = s.sb("diff", [P, 2])
        ex = s.sb("ex", [P, 2])
        wt = s.sb("wt", [P, 2, EXPERTS])
        hw = s.sb("hw", [P, 2, ER])
        hT = s.sb("hT", [P, 2, P])
        xT_ps = s.ps("xT_ps", [P, 2, KT, P])
        h_ps = s.ps("h_ps", [P, 2, 512])
        hT_ps = s.ps("hT_ps", [P, 512])
        out_ps = s.ps("out_ps", [P, 2, D])
        w_in, iota_set, g_set = s.sem("w_in"), s.sem("iota"), s.sem("g_set")
        xn_ready, xT_made, xT_ready, h_ready = s.sem("xn"), s.sem("xT_made"), s.sem("xT_ready"), s.sem("h_ready")
        diffs, exps, hw_ready, hT_made, hT_ready = s.sem("diffs"), s.sem("exps"), s.sem("hw"), s.sem("hT_made"), s.sem("hT_ready")
        out_ready, x_new, chain, stats = s.sem("out_ready"), s.sem("x_new"), s.sem("chain"), s.sem("stats")
        with nc.Block() as block:
            @block.sync
            def _(sp):
                sp.dma_start(a_sb[:, :, :], aT.rearrange("(k p) n -> p k n", p=P)).then_inc(w_in, 16)
                sp.dma_start(b_sb[:, :], bT).then_inc(w_in, 16)
                sp.dma_start(rb[:, :], router_b.rearrange("(o n) -> o n", o=1).to_broadcast([P, EXPERTS])).then_inc(w_in, 16)

            @block.gpsimd
            def _(pool):
                pool.iota(iota[:, :], [[1, EXPERTS]], base=0, channel_multiplier=0, allow_small_or_imprecise_dtypes=True).then_inc(iota_set, 1)


            @block.tensor
            def _(pe):
                pe.wait_ge(w_in, 48)

                def step(v, par, has):
                    if has(2):
                        need(pe, xn_ready, v + 3)
                        need(pe, xT_ready, v + 1)
                        for k in range(KT):
                            ins = pe.transpose(xT_ps[:, par, k, :], xn[:, par, P * k:P * k + P], c.ident[:, :])
                        ins.then_inc(xT_made, 1)
                    if has(0):
                        need(pe, hT_ready, v + 1)
                        need(pe, x_new, v)
                        pe.matmul(out_ps[:, par, :], hT[:, par, :], b_sb[:, :], start=True, stop=True).then_inc(out_ready, 1)
                    if has(2):
                        need(pe, xT_ready, v + 3)
                        need(pe, hw_ready, v + 1)
                        for k in range(KT):
                            ins = pe.matmul(h_ps[:, par, 0:ER + EXPERTS], xT[:, par, k, :], a_sb[:, k, :], start=(k == 0), stop=(k == KT - 1))
                        ins.then_inc(h_ready, 1)
                    if has(1):
                        need(pe, hw_ready, v + 2)
                        need(pe, hT_ready, v + 1)
                        pe.transpose(hT_ps[:, 0:P], hw[:, 1 - par, :], c.ident[:, :]).then_inc(hT_made, 1)

                pipelined(pe, step, 0, 3)

            @block.scalar
            def _(act):
                def step(v, par, has):
                    if has(2):
                        need(act, xT_made, v + 3)
                        need(act, h_ready, v + 1)
                        act.copy(xT[:, par, :, :], xT_ps[:, par, :, :]).then_inc(xT_ready, 1)
                    if has(1):
                        need(act, diffs, v + 2)
                        act.activation(ex[:, :], diff[:, :], ACT.Exp).then_inc(exps, 1)
                        need(act, hT_made, v + 2)
                        need(act, out_ready, v)
                        act.copy(hT[:, 1 - par, :], hT_ps[:, 0:P]).then_inc(hT_ready, 1)

                pipelined(act, step, 0, 3)

            @block.vector
            def _(dve):
                dve.wait_ge(w_in, 48)
                dve.wait_ge(iota_set, 1)
                dve.tensor_scalar(g[:, :], c.gate[:, 4:5], SCALING0, None, ALU.mult).then_inc(g_set, 1)
                dve.wait_ge(g_set, 1)

                def step(v, par, has):
                    u = 1 - par
                    if has(1):
                        need(dve, h_ready, v + 2)
                        ch = Chain(dve, chain, v + 1, 8)
                        ch.step(dve.tensor_tensor(lg[:, :], h_ps[:, u, ER:ER + EXPERTS], rb[:, :], ALU.add))
                        dve.tensor_copy(diff[:, 0:1], lg[:, 0:1])
                        ch.step(dve.max(out=top[:, :], in_=lg[:, :]))
                        dve.tensor_tensor(diff[:, 0:1], top[:, 1:2], top[:, 0:1], ALU.subtract)
                        dve.tensor_tensor(diff[:, 1:2], top[:, 0:1], top[:, 1:2], ALU.subtract).then_inc(diffs, 1)
                        ch.step(dve.max_index(out=at_top[:, :], in_max=top[:, :], in_values=lg[:, :]))
                        ch.step(dve.tensor_copy(at_topf[:, :], at_top[:, :]))
                    if has(3):
                        need(dve, xT_made, v + 2)
                        normalised(c, dve, xn[:, u, :], v + 3).then_inc(xn_ready, 1)
                    if has(1):
                        need(dve, exps, v + 2)
                        ch.step(dve.tensor_scalar(ex[:, :], ex[:, :], 1.0, None, ALU.add))
                        ch.step(dve.reciprocal(ex[:, :], ex[:, :]))
                        dve.tensor_scalar(wt[:, 0, :], iota[:, :], at_topf[:, 0:1], ex[:, 0:1], ALU.is_equal, ALU.mult)
                        ch.step(dve.tensor_scalar(wt[:, 1, :], iota[:, :], at_topf[:, 1:2], ex[:, 1:2], ALU.is_equal, ALU.mult))
                        ch.step(dve.tensor_tensor(wt[:, 0, :], wt[:, 0, :], wt[:, 1, :], ALU.add))
                        need(dve, hT_made, v)
                        dve.tensor_tensor(hw[:, u, :].rearrange("p (e r) -> p e r", e=EXPERTS),
                                          h_ps[:, u, 0:ER].rearrange("p (e r) -> p e r", e=EXPERTS),
                                          spread(wt[:, 0, :], RANK0), ALU.mult).then_inc(hw_ready, 1)
                        ch.end()
                    if has(0):
                        need(dve, out_ready, v + 1)
                        dve.scalar_tensor_tensor(out=c.x[:, v, :], in0=out_ps[:, par, :], scalar=g[:, 0:1], in1=c.x[:, v, :],
                                                 op0=ALU.mult, op1=ALU.add).then_inc(x_new, 1)
                        need(dve, x_new, v + 1)
                        dve.bn_stats(c.stats[:, v, :], c.x[:, v, :]).then_inc(stats, 1)

                pipelined(dve, step, 0, 3)


KV, GROUP, HD1, MAX_POS, THETA = 8, 4, 128, 512, 10000.0
STEP = 4 * P
STEPS = B * S // STEP
KEEP, MASKED = 3.0e38, -1.0e9 * HD1 ** 0.5


XS = 256.0


def prepare_stage(c, pos, mask, tables, cosT, sinT, limit, ctxT, cT16, c_unit, xT16):
    nc = c.nc
    with Stage(nc, "rope") as s:
        pos_i = s.sb("pos_i", [P, PAIRS], I32)
        pos_f = s.sb("pos_f", [P, PAIRS])
        wrap = s.sb("wrap", [P, PAIRS])
        idx = s.sb("idx", [P, PAIRS], U32)
        rows = s.sb("rows", [P, PAIRS, 2 * HD1])
        m_i = s.sb("m_i", [P, PAIRS, S], I32)
        masked = s.sb("masked", [P, PAIRS, S])
        keep = s.sb("keep", [P, PAIRS, S])
        raw = s.sb("raw", [P, KT, B * S])
        mags = s.sb("mags", [P, KT + 2])
        c_scale = s.sb("c_scale", [P, 1])
        xn = s.sb("xn", [P, 2, D])
        xT_ps = s.ps("xT_ps", [P, 2, KT, P])
        xn_ready, xT_made, x_hi, x_lo = s.sem("xn"), s.sem("xT_made"), s.sem("x_hi"), s.sem("x_lo")
        t_ps = s.ps("t_ps", [P, 2, 4, P])
        p_in, m_in, chain, idx_ready = s.sem("p_in"), s.sem("m_in"), s.sem("chain"), s.sem("idx_ready")
        gathered, turned, out = s.sem("gathered"), s.sem("turned"), s.sem("out")
        c_in, maxed, reduced, scaled, c_hi, c_lo = s.sems("c_in", KT), s.sem("maxed"), s.sem("reduced"), s.sem("scaled"), s.sem("c_hi"), s.sem("c_lo")
        with nc.Block() as block:
            @block.sync
            def _(sp):
                with nc.allow_non_contiguous_dma(reason="2048 positions, once"):
                    sp.dma_start(pos_i[:, :], pos.rearrange("(i b) s -> (b s) i", b=2)).then_inc(p_in, 16)
                sp.dma_start(m_i[:, :, :], mask.rearrange("(i b) q k -> (b q) i k", b=2)).then_inc(m_in, 16)
                for k in range(KT):
                    sp.dma_start(raw[:, k, :], ctxT[P * k:P * k + P, :]).then_inc(c_in[k], 16)

            @block.vector
            def _(dve):
                dve.wait_ge(p_in, 16)
                ch = Chain(dve, chain)
                ch.step(dve.tensor_copy(pos_f[:, :], pos_i[:, :]))
                ch.step(dve.tensor_scalar(wrap[:, :], pos_f[:, :], 0.0, float(MAX_POS), ALU.is_lt, ALU.mult))
                ch.step(dve.tensor_tensor(pos_f[:, :], pos_f[:, :], wrap[:, :], ALU.add))
                ch.step(dve.tensor_scalar(pos_f[:, :], pos_f[:, :], 0.0, float(MAX_POS - 1), ALU.max, ALU.min))
                dve.tensor_copy(idx[:, :], pos_f[:, :]).then_inc(idx_ready, 1)

                def step(v, par, has):
                    if has(1):
                        need(dve, xT_made, v)
                        normalised(c, dve, xn[:, 1 - par, :], v + 1).then_inc(xn_ready, 1)
                    if has(0):
                        need(dve, x_hi, v + 1)
                        cols = bass.ds(v * P, P)
                        dve.scalar_tensor_tensor(out=xT16[:, 1, :, cols], in0=xT_ps[:, par, :, :], scalar=XS, in1=xT16[:, 0, :, cols],
                                                 op0=ALU.mult, op1=ALU.subtract).then_inc(x_lo, 1)

                pipelined(dve, step, 0, 1)
                dve.wait_ge(m_in, 16)
                ch.step(dve.tensor_scalar(masked[:, :, :], m_i[:, :, :], 0.0, MASKED, ALU.is_equal, ALU.mult))
                ch.step(dve.tensor_scalar(keep[:, :, :], m_i[:, :, :], 0.0, KEEP, ALU.not_equal, ALU.mult))
                ch.step(dve.tensor_tensor(limit[:, :, :], keep[:, :, :], masked[:, :, :], ALU.add))
                for k in range(KT):
                    dve.wait_ge(c_in[k], 16)
                    ins = dve.tensor_reduce(mags[:, k:k + 1], raw[:, k, :], X, ALU.max, apply_absolute_value=True)
                ch.step(ins)
                dve.tensor_reduce(mags[:, KT:KT + 1], mags[:, 0:KT], X, ALU.max).then_inc(maxed, 1)
                dve.wait_ge(reduced, 1)
                ch.step(dve.tensor_scalar(mags[:, KT + 1:KT + 2], mags[:, KT + 1:KT + 2], TINY, None, ALU.max))
                ch.step(dve.tensor_scalar(c_unit, mags[:, KT + 1:KT + 2], 1 / TOP16, None, ALU.mult))
                dve.reciprocal(c_scale[:, :], c_unit).then_inc(scaled, 1)
                dve.wait_ge(scaled, 1)
                for k in range(KT):
                    dve.wait_ge(c_hi, k + 1)
                    dve.scalar_tensor_tensor(out=cT16[:, 1, k, :], in0=raw[:, k, :], scalar=c_scale[:, :], in1=cT16[:, 0, k, :],
                                             op0=ALU.mult, op1=ALU.subtract).then_inc(c_lo, 1)

            @block.gpsimd
            def _(pool):
                pool.wait_ge(idx_ready, 1)
                for i in range(PAIRS):
                    pool.indirect_dma_start(out=rows[:, i, :], out_offset=None, in_=tables,
                                            in_offset=bass.IndirectOffsetOnAxis(ap=idx[:, i:i + 1], axis=0)).then_inc(gathered, 16)
                pool.wait_ge(maxed, 1)
                pool.partition_all_reduce(mags[:, KT + 1:KT + 2], mags[:, KT:KT + 1], P, RMAX).then_inc(reduced, 1)

            @block.tensor
            def _(pe):
                def step(v, par, has):
                    need(pe, xn_ready, v + 2)
                    need(pe, x_lo, v)
                    for k in range(KT):
                        ins = pe.transpose(xT_ps[:, 1 - par, k, :], xn[:, 1 - par, P * k:P * k + P], c.ident[:, :])
                    ins.then_inc(xT_made, 1)

                pipelined(pe, step, 1, 1)
                pe.wait_ge(gathered, 16 * PAIRS)
                for i in range(PAIRS):
                    if i >= 2:
                        pe.wait_ge(out, i - 1)
                    for n in range(2):
                        ins = pe.transpose(t_ps[:, i % 2, n, :], rows[:, i, HD1 * n:HD1 * n + HD1], c.ident[:, :])
                    ins.then_inc(turned, 1)

            @block.scalar
            def _(act):
                with act.Fori(0, TURNS) as j:
                    for u in range(2):
                        t = 2 * j + u
                        act.wait_ge(xT_made, t + 1)
                        act.activation(xT16[:, 0, :, bass.ds(t * P, P)], xT_ps[:, u, :, :], ACT.Copy, scale=XS).then_inc(x_hi, 1)
                act.wait_ge(scaled, 1)
                for k in range(KT):
                    act.activation(cT16[:, 0, k, :], raw[:, k, :], ACT.Copy, scale=c_scale[:, :]).then_inc(c_hi, 1)
                for i in range(PAIRS):
                    act.wait_ge(turned, i + 1)
                    act.copy(cosT[:, P * i:P * i + P], t_ps[:, i % 2, 0, :])
                    act.copy(sinT[:, P * i:P * i + P], t_ps[:, i % 2, 1, :]).then_inc(out, 1)


def rope_tables():
    inv = (1.0 / np.float32(THETA) ** (np.arange(0, HD1, 2, dtype=np.float32) / np.float32(HD1))).astype(np.float32)
    f = np.arange(MAX_POS, dtype=np.float32)[:, None] * inv[None]
    cos, sin = np.cos(f).astype(np.float32), np.sin(f).astype(np.float32)
    return np.concatenate([cos, cos, -sin, sin], axis=1)


def grouped_attention_stage(c, wq, wk, wv, wo, cosT, sinT, limit, xT16, cT16, c_unit):
    nc = c.nc
    with Stage(nc, "gqa") as s:
        W_K, W_Q, W_V, W_O = range(4)
        SIZES = (KT * HD1, KT * GROUP * HD1, KT * HD1, GROUP * D)
        OFFS = [sum(SIZES[:n]) for n in range(4)]
        w16 = s.sb("w16", [P, 2, 2, sum(SIZES)], F16)
        raw = s.sb("raw", [P, max(SIZES)])
        mag = s.sb("mag", [P, 3])
        unit = s.sb("unit", [P, 3])
        fac = s.sb("fac", [P, 2, 4])
        cg = s.sb("cg", [P, 1])
        qk = s.sb("qk", [P, 1 + GROUP, STEP])
        v = s.sb("v", [P, 2, 4, HD1])
        sw = s.sb("sw", [P, 2, STEP])
        e = s.sb("e", [P, 4 * GROUP, S])
        mx = s.sb("mx", [P, 4 * GROUP])
        sm = s.sb("sm", [P, 4 * GROUP])
        probs = s.sb("probs", [P, 4 * GROUP, P])
        pT = s.sb("pT", [P, 2, GROUP * P])
        oT16 = s.sb("oT16", [P, 2, 2, GROUP, P], F16)
        proj_ps = s.ps("proj", [P, 2, STEP])
        s_ps = s.ps("scores", [P, 4, GROUP, S])
        t_ps = s.ps("pT_ps", [P, GROUP, P])
        o_ps = s.ps("o_ps", [P, GROUP, P])
        y_ps = s.ps("y_ps", [P, 2, D])
        raw_in, w_maxed, w_reduced, w_scaled, w_hi, w_lo = (s.sem(n) for n in ("raw_in", "w_maxed", "w_reduced", "w_scaled", "w_hi", "w_lo"))
        first_in = s.sems("first_in", 3)
        probs_zero, gated, w_chain = s.sem("probs_zero"), s.sem("gated"), s.sem("w_chain")
        filled, swapped, cosed, sined, roped = s.sem("filled"), s.sem("swapped"), s.sem("cosed"), s.sem("sined"), s.sem("roped")
        scored, bounded, shifted, exped, normed = s.sem("scored"), s.sem("bounded"), s.sem("shifted"), s.sem("exped"), s.sem("normed")
        turned, turned_out, headed, o_hi, o_lo = s.sem("turned"), s.sem("turned_out"), s.sem("headed"), s.sem("o_hi"), s.sem("o_lo")
        summed, added, chain, stats, maxed = s.sem("summed"), s.sem("added"), s.sem("chain"), s.sem("stats"), s.sem("maxed")
        GT = KV // 2
        R = 2 * STEPS
        FILLS, ROPES = 6, 5
        V_SCALE = 2.0 ** 14 / (KT * P * TOP16 * TOP16)

        def weight(gb, part, n, k, cols):
            width = SIZES[n] // KT
            return w16[:, gb, part, OFFS[n] + width * k + cols.start:OFFS[n] + width * k + cols.stop]

        def raw_of(t, n):
            if isinstance(t, int) and t in (W_K, W_V):
                return qk[:, t // 2, :]
            return raw[:, 0:SIZES[n]]

        def turns(eng, body):
            with eng.Fori(0, GT - 1) as j:
                for r in range(R):
                    body(R * j + r, r, 2, True)
            for r in range(R):
                body(R * (GT - 1) + r, r, R - 1 - r, r < STEPS)

        with nc.Block() as block:
            @block.sync
            def _(sp):
                def load(t, r, head):
                    n = r % 4
                    need(sp, w_lo, t)
                    if n == W_O:
                        src = wo.rearrange("(g h p) n -> p g h n", h=GROUP, p=P)[:, head, :, :]
                    else:
                        w = (wk, wq, wv)[n]
                        src = w.rearrange("(k p) n -> p k n", p=P)[:, :, bass.ts(head, SIZES[n] // KT)]
                    sp.dma_start(raw_of(t, n).rearrange("p (k n) -> p k n", k=KT), src).then_inc(raw_in, 16)

                for n in range(3):
                    source = (wk, wq, wv)[n].rearrange("(k p) n -> p k n", p=P)[:, :, 0:SIZES[n] // KT]
                    sp.dma_start(raw_of(n, n).rearrange("p (k n) -> p k n", k=KT), source).then_inc(first_in[n], 16)
                load(3, 3, 0)
                with sp.Fori(0, GT - 1) as j:
                    for r in range(R):
                        load(R * j + r + 4, r, 2 * j + (r // 4 + 1))
                for r in range(4):
                    load(R * (GT - 1) + r + 4, r, KV - 1)

            @block.tensor
            def _(pe):
                pe.wait_ge(probs_zero, 1)

                def project(t, r, n):
                    gb, step = r // STEPS, r % STEPS
                    if step == 0 and n in (0, 1, 5):
                        need(pe, w_lo, t + (1 if n == 0 else 2 if n == 1 else 3))
                    need(pe, swapped, FILLS * t + n - 1)
                    need(pe, cosed, ROPES * t + max(0, n - 1))
                    last = (KT - 1, SPLIT[-1])
                    for i in range(4 if n == 5 else 1):
                        for k in range(KT):
                            for pw, px in SPLIT:
                                flags = dict(start=(k, (pw, px)) == (0, SPLIT[0]), stop=(k, (pw, px)) == last)
                                cols = slice(STEP * step, STEP * step + STEP)
                                if n == 0:
                                    ins = pe.matmul(proj_ps[:, 0, :], weight(gb, pw, W_K, k, slice(0, HD1)), cT16[:, px, k, cols], **flags)
                                elif n < 5:
                                    ins = pe.matmul(proj_ps[:, n % 2, :], weight(gb, pw, W_Q, k, slice(HD1 * (n - 1), HD1 * n)), xT16[:, px, k, cols], **flags)
                                else:
                                    rows = slice(STEP * step + P * i, STEP * step + P * i + P)
                                    ins = pe.matmul(proj_ps[:, 1, HD1 * i:HD1 * i + HD1], cT16[:, pw, k, rows], weight(gb, px, W_V, k, slice(0, HD1)), **flags)
                    ins.then_inc(filled, 1)

                def scores(t):
                    need(pe, roped, ROPES * (t + 1))
                    need(pe, bounded, t)
                    for i in range(4):
                        for h in range(GROUP):
                            for b in range(2):
                                rows = slice(P * i + S * b, P * i + S * b + S)
                                ins = pe.matmul(s_ps[S * b:S * b + S, i, h, :], qk[:, 1 + h, rows], qk[:, 0, rows], start=True, stop=True)
                    ins.then_inc(scored, 1)

                def turn(t, i):
                    if i == 0:
                        need(pe, normed, 2 * t + 2)
                    need(pe, turned_out, 4 * t + i)
                    for h in range(GROUP):
                        ins = pe.transpose(t_ps[:, h, :], probs[:, GROUP * i + h, :], c.ident[:, :])
                    ins.then_inc(turned, 1)

                def attend(t, r, i):
                    if i == 0:
                        need(pe, swapped, FILLS * (t + 1))
                    need(pe, turned_out, 4 * t + i + 1)
                    need(pe, o_lo, 4 * t + i)
                    pe.matmul(o_ps[:, :, :], v[:, r % 2, i, :], pT[:, i % 2, :], start=True, stop=True).then_inc(headed, 1)

                def project_out(t, r, i):
                    if i == 0 and r % STEPS == 0:
                        need(pe, w_lo, t + 4)
                    need(pe, o_lo, 4 * t + i + 1)
                    need(pe, added, 4 * t + max(0, i - 1))
                    for h in range(GROUP):
                        for po, pw in SPLIT:
                            ins = pe.matmul(y_ps[:, i % 2, :], oT16[:, i % 2, po, h, :], weight(r // STEPS, pw, W_O, h, slice(0, D)),
                                            start=(h == 0 and (po, pw) == SPLIT[0]), stop=(h == GROUP - 1 and (po, pw) == SPLIT[-1]))
                    ins.then_inc(summed, 1)

                def body(t, r, more, prep):
                    def fill(ahead, n):
                        if more >= ahead:
                            project(t + ahead, (r + ahead) % R, n)

                    turn(t, 0)
                    fill(1, 3)
                    attend(t, r, 0)
                    turn(t, 1)
                    fill(1, 4)
                    attend(t, r, 1)
                    turn(t, 2)
                    project_out(t, r, 0)
                    attend(t, r, 2)
                    turn(t, 3)
                    project_out(t, r, 1)
                    if more:
                        scores(t + 1)
                    attend(t, r, 3)
                    project_out(t, r, 2)
                    fill(1, 5)
                    project_out(t, r, 3)
                    for n in range(3):
                        fill(2, n)

                for n in range(FILLS):
                    project(0, 0, n)
                scores(0)
                for n in range(3):
                    project(1, 1, n)
                turns(pe, body)

            @block.scalar
            def _(act):
                def split(t, r, gb):
                    n = r % 4
                    need(act, w_scaled, t + 1)
                    act.activation(w16[:, gb, 0, OFFS[n]:OFFS[n] + SIZES[n]], raw_of(t, n), ACT.Copy, scale=unit[:, 1:2]).then_inc(w_hi, 1)

                def read(t, r, n):
                    need(act, filled, FILLS * t + n + 1)
                    gb = r // STEPS
                    if n < ROPES:
                        par = (r + n) % 2
                        f = slice(W_K, W_K + 1) if n == 0 else slice(W_Q, W_Q + 1)
                        need(act, roped, ROPES * t + n - 1)
                        act.activation(sw[0:64, par, :], proj_ps[64:128, n % 2, :], ACT.Copy, scale=fac[64:128, gb, f])
                        act.activation(sw[64:128, par, :], proj_ps[0:64, n % 2, :], ACT.Copy, scale=fac[0:64, gb, f]).then_inc(swapped, 1)
                    else:
                        need(act, headed, 4 * (t - 1))
                        act.activation(v[:, r % 2, :, :], proj_ps[:, 1, :].rearrange("p (i d) -> p i d", i=4), ACT.Copy, scale=V_SCALE).then_inc(swapped, 1)

                def exps(t):
                    need(act, shifted, t + 1)
                    act.activation(e[:, :, :], e[:, :, :], ACT.Exp, scale=HD1 ** -0.5).then_inc(exped, 1)

                def body(t, r, more, prep):
                    def fill(ahead, n):
                        if more >= ahead:
                            read(t + ahead, (r + ahead) % R, n)

                    def turned_copy(i):
                        need(act, turned, 4 * t + i + 1)
                        need(act, headed, 4 * t + max(0, i - 1))
                        act.copy(pT[:, i % 2, :], t_ps[:, :, :].rearrange("p h q -> p (h q)")).then_inc(turned_out, 1)

                    def head(i):
                        need(act, headed, 4 * t + i + 1)
                        need(act, summed, 4 * t + max(0, i - 1))
                        act.copy(oT16[:, i % 2, 0, :, :], o_ps[:, :, :]).then_inc(o_hi, 1)

                    turned_copy(0)
                    fill(1, 3)
                    head(0)
                    turned_copy(1)
                    fill(1, 4)
                    head(1)
                    turned_copy(2)
                    head(2)
                    turned_copy(3)
                    head(3)
                    if more:
                        exps(t + 1)
                    if prep:
                        split(t + 4, r, 1 - r // STEPS)
                    fill(1, 5)
                    for n in range(3):
                        fill(2, n)

                for r in range(3):
                    split(r, r, 0)
                for n in range(FILLS):
                    read(0, 0, n)
                    if n == 3:
                        split(3, 3, 0)
                exps(0)
                for n in range(3):
                    read(1, 1, n)
                turns(act, body)

            @block.gpsimd
            def _(pool):
                def reduce(t):
                    need(pool, w_maxed, t + 1)
                    pool.tensor_tensor(mag[:, 2:3], mag[:, 0:1], mag[:, 0:1], ALU.add)
                    pool.partition_all_reduce(mag[:, 1:2], mag[:, 0:1], P, RMAX).then_inc(w_reduced, 1)

                def sin(t, r, n):
                    need(pool, swapped, FILLS * t + n + 1)
                    par = (r + n) % 2
                    pool.tensor_tensor(sw[:, par, :], sw[:, par, :], sinT[:, STEP * (r % STEPS):STEP * (r % STEPS) + STEP], ALU.mult).then_inc(sined, 1)

                def body(t, r, more, prep):
                    if more:
                        sin(t + 1, (r + 1) % R, 3)
                        sin(t + 1, (r + 1) % R, 4)
                    if prep:
                        reduce(t + 4)
                    for n in range(3):
                        if more > 1:
                            sin(t + 2, (r + 2) % R, n)

                for r in range(3):
                    reduce(r)
                for n in range(ROPES):
                    sin(0, 0, n)
                    if n == 1:
                        reduce(3)
                for n in range(3):
                    sin(1, 1, n)
                turns(pool, body)

            @block.vector
            def _(dve):
                dve.memset(probs[:, :, :], 0.0).then_inc(probs_zero, 1)
                dve.tensor_tensor(cg[:, :], c_unit, c.gate[:, 1:2], ALU.mult).then_inc(gated, 1)
                dve.wait_ge(gated, 1)

                WCH = 3

                def magnitude(t, r):
                    n = r % 4
                    if isinstance(t, int) and t < 3:
                        dve.wait_ge(first_in[t], 16)
                    else:
                        need(dve, raw_in, 16 * (t - 2))
                    dve.tensor_reduce(mag[:, 0:1], raw_of(t, n), X, ALU.max, apply_absolute_value=True).then_inc(w_maxed, 1)

                def scale(t, r, gb):
                    n = r % 4
                    need(dve, w_reduced, t + 1)
                    ch = Chain(dve, w_chain, t, WCH)
                    ch.step(dve.tensor_scalar(unit[:, 0:1], mag[:, 1:2], TINY, 1 / TOP16, ALU.max, ALU.mult))
                    f = fac[:, gb, n:n + 1]
                    if n == W_Q:
                        ins = dve.tensor_scalar(f, unit[:, 0:1], 1 / XS, None, ALU.mult)
                    elif n == W_K:
                        ins = dve.tensor_tensor(f, unit[:, 0:1], c_unit, ALU.mult)
                    elif n == W_V:
                        ins = dve.tensor_tensor(f, unit[:, 0:1], cg[:, :], ALU.mult)
                    else:
                        ins = dve.scalar_tensor_tensor(out=f, in0=unit[:, 0:1], scalar=1 / V_SCALE, in1=fac[:, gb, W_V:W_V + 1], op0=ALU.mult, op1=ALU.mult)
                    ch.step(ins)
                    ch.step(dve.reciprocal(unit[:, 1:2], unit[:, 0:1]))
                    ch.end()
                    dve.sem_inc(w_scaled, 1)

                def split(t, r, gb):
                    n = r % 4
                    cols = slice(OFFS[n], OFFS[n] + SIZES[n])
                    need(dve, w_hi, t + 1)
                    dve.scalar_tensor_tensor(out=w16[:, gb, 1, cols], in0=raw_of(t, n), scalar=unit[:, 1:2], in1=w16[:, gb, 0, cols],
                                             op0=ALU.mult, op1=ALU.subtract).then_inc(w_lo, 1)

                def rope(t, r, n):
                    cols = slice(STEP * (r % STEPS), STEP * (r % STEPS) + STEP)
                    need(dve, swapped, FILLS * t + n + 1)
                    if n == 0:
                        need(dve, scored, t)
                    f = W_K if n == 0 else W_Q
                    dve.scalar_tensor_tensor(out=qk[:, n, :], in0=proj_ps[:, n % 2, :], scalar=fac[:, r // STEPS, f:f + 1], in1=cosT[:, cols],
                                             op0=ALU.mult, op1=ALU.mult).then_inc(cosed, 1)
                    need(dve, sined, ROPES * t + n + 1)
                    need(dve, cosed, ROPES * t + n + 1)
                    dve.tensor_tensor(qk[:, n, :], qk[:, n, :], sw[:, (r + n) % 2, :], ALU.add).then_inc(roped, 1)

                def shift(t, r):
                    need(dve, scored, t + 1)
                    lim = limit[:, 4 * (r % STEPS):4 * (r % STEPS) + 4, :].unsqueeze(2).to_broadcast([P, 4, GROUP, S])
                    dve.tensor_tensor(e[:, :, :].rearrange("p (i h) k -> p i h k", h=GROUP), s_ps[:, :, :, :], lim, ALU.min).then_inc(bounded, 1)
                    need(dve, bounded, t + 1)
                    dve.tensor_reduce(mx[:, :], e[:, :, :], X, ALU.max).then_inc(maxed, 1)
                    need(dve, maxed, t + 1)
                    dve.tensor_tensor(e[:, :, :], e[:, :, :], spread(mx[:, :], S), ALU.subtract).then_inc(shifted, 1)

                def norm(t):
                    need(dve, exped, t + 1)
                    ch = Chain(dve, chain, t, 2)
                    ch.step(dve.tensor_reduce(sm[:, :], e[:, :, :], X, ALU.add))
                    ch.step(dve.reciprocal(sm[:, :], sm[:, :]))
                    ch.end()
                    need(dve, turned, 4 * t)
                    for b in range(2):
                        rows = slice(S * b, S * b + S)
                        dve.tensor_tensor(probs[rows, :, rows], e[rows, :, :], spread(sm[rows, :], S), ALU.mult).then_inc(normed, 1)

                def body(t, r, more, prep):
                    def fill(ahead, n):
                        if more >= ahead:
                            rope(t + ahead, (r + ahead) % R, n)

                    def low(i):
                        need(dve, o_hi, 4 * t + i + 1)
                        dve.tensor_tensor(oT16[:, i % 2, 1, :, :], o_ps[:, :, :], oT16[:, i % 2, 0, :, :], ALU.subtract).then_inc(o_lo, 1)

                    def add(i):
                        row = 4 * (r % STEPS) + i
                        need(dve, summed, 4 * t + i + 1)
                        dve.scalar_tensor_tensor(out=c.x[:, row, :], in0=y_ps[:, i % 2, :], scalar=fac[:, r // STEPS, W_O:W_O + 1], in1=c.x[:, row, :],
                                                 op0=ALU.mult, op1=ALU.add).then_inc(added, 1)
                        if isinstance(t, int) and r >= STEPS:
                            dve.wait_ge(added, 4 * t + i + 1)
                            dve.bn_stats(c.stats[:, row, :], c.x[:, row, :]).then_inc(stats, 1)

                    fill(1, 3)
                    low(0)
                    fill(1, 4)
                    low(1)
                    if prep:
                        magnitude(t + 4, r)
                    add(0)
                    low(2)
                    add(1)
                    if more:
                        shift(t + 1, (r + 1) % R)
                    if prep:
                        scale(t + 4, r, 1 - r // STEPS)
                    low(3)
                    add(2)
                    if more:
                        norm(t + 1)
                    if prep:
                        split(t + 4, r, 1 - r // STEPS)
                    add(3)
                    for n in range(3):
                        fill(2, n)

                for r in range(3):
                    magnitude(r, r)
                    scale(r, r, 0)
                    split(r, r, 0)
                for n in range(ROPES):
                    rope(0, 0, n)
                    if n == 1:
                        magnitude(3, 3)
                    if n == 2:
                        scale(3, 3, 0)
                split(3, 3, 0)
                shift(0, 0)
                rope(1, 1, 0)
                norm(0)
                rope(1, 1, 1)
                rope(1, 1, 2)
                turns(dve, body)


LORAS, RANK1, GROUPS1 = 16, 32, 8
NR = LORAS * RANK1
ROWS1 = B * S // GROUPS1
LR = 2 * RANK1


def lora_linear_stage(c, kernel, bias, gateT, pick, a_all, b_allT, a_sharedT, b_sharedT):
    nc = c.nc
    with Stage(nc, "lora") as s:
        NT, G = NR // P, GROUPS1
        w = s.sb("w", [P, KT, D])
        a_n = s.sb("a_n", [P, NT, D])
        b_n = s.sb("b_n", [P, NT, D])
        gate = s.sb("gate", [P, NT, G])
        eye = s.sb("eye", [P, RANK1])
        mix = s.sb("mix", [P, NT, G, RANK1])
        a_all_g = s.sb("a_all_g", [P, KT, G * RANK1])
        a_s = s.sb("a_s", [P, KT, RANK1])
        a_g = s.sb("a_g", [P, 2, KT, LR])
        b_g = s.sb("b_g", [LR + 1, G, D])
        xn = s.sb("xn", [P, 2, D])
        xT = s.sb("xT", [P, 2, KT, ROWS1])
        ax = s.sb("ax", [LR + 1, 2, ROWS1])
        mix_ps = s.ps("mix_ps", [P, 2, 512])
        xT_ps = s.ps("xT_ps", [P, 2, KT, P])
        ax_ps = s.ps("ax_ps", [P, 512])
        y_ps = s.ps("y_ps", [P, 2, D])
        gate_in, ab_in, shared_in, w_in = s.sem("gate_in"), s.sem("ab_in"), s.sem("shared_in"), s.sem("w_in")
        mixed, ones, shared_set = s.sem("mixed"), s.sem("ones"), s.sem("shared_set")
        a_made, a_out, b_made, b_out = s.sem("a_made"), s.sem("a_out"), s.sem("b_made"), s.sem("b_out")
        xn_ready, xT_made, xT_out = s.sem("xn"), s.sem("xT_made"), s.sem("xT_out")
        picked, ax_made, ax_out = s.sem("picked"), s.sem("ax_made"), s.sem("ax_out")
        summed, x_new, stats = s.sem("summed"), s.sem("x_new"), s.sem("stats")
        with nc.Block() as block:
            @block.sync
            def _(sp):
                sp.dma_start(gate[:, :, :], gateT).then_inc(gate_in, 16)
                sp.dma_start(eye[:, :], pick).then_inc(gate_in, 16)
                sp.dma_start(a_n[:, :, :], a_all.rearrange("(k p) n -> p k n", p=P)).then_inc(ab_in, 16)
                sp.dma_start(b_n[:, :, :], b_allT.rearrange("(k p) n -> p k n", p=P)).then_inc(ab_in, 16)
                sp.dma_start(a_s[:, :, :], a_sharedT.rearrange("(k p) n -> p k n", p=P)).then_inc(shared_in, 16)
                sp.dma_start(b_g[RANK1:LR, :, :], b_sharedT.unsqueeze(1).to_broadcast([RANK1, G, D])).then_inc(shared_in, 16)
                sp.dma_start(b_g[LR:LR + 1, :, :], bias.rearrange("(o g n) -> o g n", o=1, g=1).to_broadcast([1, G, D])).then_inc(shared_in, 16)
                sp.dma_start(w[:, :, :], kernel.rearrange("(k p) n -> p k n", p=P)).then_inc(w_in, 16)


            @block.tensor
            def _(pe):
                pe.wait_ge(ab_in, 32)
                pe.wait_ge(mixed, 1)
                for k in range(KT):
                    for n in range(NT):
                        ins = pe.matmul(mix_ps[:, k // 2, G * RANK1 * (k % 2):G * RANK1 * (k % 2 + 1)], a_n[:, n, P * k:P * k + P],
                                        mix[:, n, :, :].rearrange("p g r -> p (g r)"), start=(n == 0), stop=(n == NT - 1))
                    ins.then_inc(a_made, 1)
                for half in range(2):
                    pe.wait_ge(a_out, half + 1)
                    for n in range(NT):
                        ins = pe.matmul(mix_ps[:, half, :], mix[:, n, 4 * half:4 * half + 4, :].rearrange("p g r -> p (g r)"), b_n[:, n, :],
                                        start=(n == 0), stop=(n == NT - 1))
                    ins.then_inc(b_made, 1)
                pe.wait_ge(w_in, 16)
                pe.wait_ge(shared_in, 48)
                pe.wait_ge(ones, 1)
                pe.wait_ge(b_out, G)

                def turn(g, u, i):
                    need(pe, xn_ready, 2 * g + i + 1)
                    need(pe, xT_out, 2 * g + i - 1)
                    for k in range(KT):
                        ins = pe.transpose(xT_ps[:, i, k, :], xn[:, i, P * k:P * k + P], c.ident[:, :])
                    ins.then_inc(xT_made, 1)

                def step(v, par, has):
                    if has(0):
                        need(pe, xT_out, 2 * v + 2)
                        need(pe, picked, v + 1)
                        need(pe, ax_out, v)
                        for k in range(KT):
                            ins = pe.matmul(ax_ps[0:LR, 0:ROWS1], a_g[:, par, k, :], xT[:, par, k, :], start=(k == 0), stop=(k == KT - 1))
                        ins.then_inc(ax_made, 1)
                    for i in range(2):
                        if has(1):
                            turn(v + 1, 1 - par, i)
                        if has(0):
                            need(pe, x_new, 2 * v + max(0, i - 1))
                            for k in range(KT):
                                pe.matmul(y_ps[:, i, :], xT[:, par, k, P * i:P * i + P], w[:, k, :], start=(k == 0), stop=False)
                            if i == 0:
                                need(pe, ax_out, v + 1)
                            pe.matmul(y_ps[:, i, :], ax[:, par, P * i:P * i + P], b_g[:, v, :], start=False, stop=True).then_inc(summed, 1)

                pipelined(pe, step, 0, 2, G)

            @block.gpsimd
            def _(pool):
                pool.wait_ge(shared_set, 2)
                pool.wait_ge(a_out, 2)

                def step(v, par, has):
                    if has(1):
                        need(pool, ax_made, v)
                        pool.tensor_copy(a_g[:, 1 - par, :, 0:RANK1], a_all_g[:, :, bass.ds((v + 1) * RANK1, RANK1)]).then_inc(picked, 1)

                pipelined(pool, step, 0, 2, G)

            @block.scalar
            def _(act):
                act.wait_ge(a_made, 2)
                act.copy(a_all_g[:, 0:2, :], mix_ps[:, 0, :].rearrange("p (k n) -> p k n", k=2)).then_inc(a_out, 1)
                act.wait_ge(a_made, 4)
                act.copy(a_all_g[:, 2:4, :], mix_ps[:, 1, :].rearrange("p (k n) -> p k n", k=2)).then_inc(a_out, 1)
                act.wait_ge(shared_in, 48)
                for u in range(2):
                    act.copy(a_g[:, u, :, RANK1:LR], a_s[:, :, :]).then_inc(shared_set, 1)
                for g in range(G):
                    act.wait_ge(b_made, g // 4 + 1)
                    act.copy(b_g[0:RANK1, g, :], mix_ps[RANK1 * (g % 4):RANK1 * (g % 4 + 1), g // 4, :]).then_inc(b_out, 1)

                def step(v, par, has):
                    if has(0):
                        need(act, ax_made, v + 1)
                        need(act, summed, 2 * v)
                        act.copy(ax[0:LR, par, :], ax_ps[0:LR, 0:ROWS1]).then_inc(ax_out, 1)
                    if has(1):
                        for i in range(2):
                            need(act, xT_made, 2 * (v + 1) + i + 1)
                            need(act, summed, 2 * v)
                            act.copy(xT[:, 1 - par, :, P * i:P * i + P], xT_ps[:, i, :, :]).then_inc(xT_out, 1)

                pipelined(act, step, 0, 2, G)

            @block.vector
            def _(dve):
                dve.memset(ax[LR:LR + 1, :, :], 1.0).then_inc(ones, 1)
                dve.wait_ge(gate_in, 32)
                dve.tensor_tensor(mix[:, :, :, :].rearrange("p n g r -> p (n g) r"), spread(gate[:, :, :].rearrange("p n g -> p (n g)"), RANK1),
                                  eye[:, :].unsqueeze(1).to_broadcast([P, NT * G, RANK1]), ALU.mult).then_inc(mixed, 1)

                def step(v, par, has):
                    for i in range(2):
                        if has(2):
                            need(dve, xT_made, 2 * (v + 1) + i + 1)
                            normalised(c, dve, xn[:, i, :], 2 * (v + 2) + i).then_inc(xn_ready, 1)
                        if has(0):
                            t = 2 * v + i
                            need(dve, summed, t + 1)
                            dve.scalar_tensor_tensor(out=c.x[:, t, :], in0=y_ps[:, i, :], scalar=c.gate[:, 5:6], in1=c.x[:, t, :],
                                                     op0=ALU.mult, op1=ALU.add).then_inc(x_new, 1)
                            need(dve, x_new, t + 1)
                            dve.bn_stats(c.stats[:, t, :], c.x[:, t, :]).then_inc(stats, 1)

                pipelined(dve, step, 0, 2, G)


TOP = 8
LOW = -3.0e38


def dft(n, rows):
    j, h = np.arange(rows)[:, None], n // 2
    return np.concatenate([np.cos(2 * np.pi * j * np.arange(h + 1) / n), -np.sin(2 * np.pi * j * np.arange(1, h) / n)], axis=1)


def swap_parts(m, n):
    h, out = n // 2, np.zeros_like(m)
    out[:, 1:h] = m[:, h + 1:]
    out[:, h + 1:] = m[:, 1:h]
    return out


def inverse_parts(n, cols):
    h = n // 2
    t, f = np.arange(cols)[None, :], np.arange(1, h)[:, None]
    cos, sin = 2 * np.cos(2 * np.pi * f * t / n), 2 * np.sin(2 * np.pi * f * t / n)
    one, alt = np.ones((1, cols)), np.cos(np.pi * np.arange(cols))[None]
    a = np.concatenate([one, cos, alt, cos]) / n
    b = np.concatenate([0 * one, -sin, 0 * alt, sin]) / n
    return a, b


def correlation_tables():
    two = lambda m: np.kron(np.eye(2), m)
    q = dft(S, S)
    ia, ib = inverse_parts(S, S)
    w = dft(2 * S, S)
    ends = dft(2 * S, 2 * S)
    v = np.concatenate([ends[:S - 1], ends[S - 1:].sum(0, keepdims=True)])
    va, vb = inverse_parts(2 * S, S)
    both = lambda m: np.concatenate([m, m])
    t = {"dft_q": two(q), "dft_qs": two(swap_parts(q, S)), "inv_a": two(ia), "inv_b": two(ib),
         "dft_w": both(w), "dft_v": both(v), "dft_vs": both(swap_parts(v, 2 * S)),
         "inv_v": np.concatenate([va, vb], axis=1)}
    return np.concatenate([t[k] for k in ("dft_q", "dft_qs", "inv_a", "inv_b", "dft_w", "dft_v", "dft_vs", "inv_v")], axis=1).astype(np.float32)


def correlation_stage(c, ctx_in, tables):
    nc = c.nc
    with Stage(nc, "corr") as s:
        m = s.sb("m", [P, 8, P])
        cin = s.sb("cin", [P, 2, 2, D])
        xn = s.sb("xn", [P, 2, D])
        kf = s.sb("kf", [P, D])
        pa = s.sb("pa", [P, 2, 2, D])
        top = s.sb("top", [P, 8, TOP])
        z = s.sb("z", [P, 8, S])
        cor = s.sb("cor", [P, 8, S])
        e = s.sb("e", [P, 8, S])
        te = s.sb("te", [P, 8, TOP])
        sm = s.sb("sm", [P, 8])
        wT = s.sb("wT", [P, D])
        wf = s.sb("wf", [P, 2, D])
        pv = s.sb("pv", [P, 2, 2, D])
        qf_ps = s.ps("qf", [P, 2, D])
        kf_ps = s.ps("kf_ps", [P, D])
        cor_ps = s.ps("cor_ps", [P, 8, S])
        wT_ps = s.ps("wT_ps", [P, D])
        vf_ps = s.ps("vf_ps", [P, 2, D])
        y_ps = s.ps("y_ps", [P, D])
        m_in, k_in, v_in, xn_ready = s.sem("m_in"), s.sems("k_in"), s.sems("v_in"), s.sem("xn")
        kf_made, kf_out, qf_made, qf_used = s.sem("kf_made"), s.sem("kf_out"), s.sem("qf_made"), s.sem("qf_used")
        cor_made, cor_out, chain, shifted, exped = s.sem("cor_made"), s.sem("cor_out"), s.sem("chain"), s.sem("shifted"), s.sem("exped")
        w_ready, wT_made, wT_out = s.sem("w_ready"), s.sem("wT_made"), s.sem("wT_out")
        wf_made, wf_out, vf_made, vf_used, summed, x_new, stats = (s.sem(n) for n in ("wf_made", "wf_out", "vf_made", "vf_used", "summed", "x_new", "stats"))
        with nc.Block() as block:
            @block.sync
            def _(sp):
                sp.dma_start(m[:, :, :], tables.rearrange("p (n f) -> p n f", n=8)).then_inc(m_in, 16)
                rows = rows_of(ctx_in)
                for u in range(2):
                    sp.dma_start(cin[:, 0, u, :], rows[:, u, :]).then_inc(k_in[u], 16)
                for u in range(2):
                    sp.dma_start(cin[:, 1, u, :], rows[:, u, :]).then_inc(v_in[u], 16)
                with sp.Fori(0, TURNS - 1) as j:
                    for u in range(2):
                        sp.wait_ge(kf_made, j * 2 + (u + 1))
                        sp.dma_start(cin[:, 0, u, :], rows[:, 2 * j + u + 2, :]).then_inc(k_in[u], 16)
                        sp.wait_ge(vf_made, j * 4 + (2 * u + 2))
                        sp.dma_start(cin[:, 1, u, :], rows[:, 2 * j + u + 2, :]).then_inc(v_in[u], 16)


            @block.tensor
            def _(pe):
                pe.wait_ge(m_in, 16)

                def values(p, par, b):
                    half = slice(S * b, S * b + S)
                    need(pe, v_in[par], (p - par) * 8 + 16)
                    need(pe, vf_used, p * 2 + b)
                    for n in range(2):
                        ins = pe.matmul(vf_ps[:, n, :], m[half, 5 + n, :], cin[half, 1, par, :], start=True, stop=True)
                    ins.then_inc(vf_made, 1)

                def weights(p, b, keys):
                    half = slice(S * b, S * b + S)
                    need(pe, wT_out, p + 1)
                    need(pe, kf_out, keys)
                    need(pe, wf_out, p * 2 + b)
                    pe.matmul(kf_ps[:, :], m[half, 4, :], wT[half, :], start=True, stop=True).then_inc(wf_made, 1)

                def step(i, par, has):
                    if has(0):
                        need(pe, w_ready, i + 1)
                        need(pe, wT_out, i)
                        for k in range(KT):
                            ins = pe.transpose(wT_ps[:, P * k:P * k + P], e[:, 2 * k:2 * k + 2, :].rearrange("p a b -> p (a b)"), c.ident[:, :])
                        ins.then_inc(wT_made, 1)
                    if has(1):
                        need(pe, qf_used, i * 2 + 4)
                        need(pe, cor_out, i + 1)
                        for k in range(KT):
                            for n in range(2):
                                ins = pe.matmul(cor_ps[:, 2 * k:2 * k + 2, :].rearrange("p a b -> p (a b)"), pa[:, 1 - par, n, P * k:P * k + P], m[:, 2 + n, :],
                                                start=(n == 0), stop=(n == 1))
                        ins.then_inc(cor_made, 1)
                    if has(0):
                        weights(i, 0, i + 2 if not isinstance(i, int) else min(i + 2, PAIRS))
                        values(i, par, 0)
                    if has(2):
                        p = i + 2
                        need(pe, k_in[par], (p - par) * 8 + 16)
                        need(pe, kf_out, p)
                        need(pe, wf_out, 2 * i + 1)
                        pe.matmul(kf_ps[:, :], m[:, 0, :], cin[:, 0, par, :], start=True, stop=True).then_inc(kf_made, 1)
                        need(pe, xn_ready, p + 1)
                        need(pe, qf_used, p * 2)
                        for n in range(2):
                            ins = pe.matmul(qf_ps[:, n, :], m[:, n, :], xn[:, par, :], start=True, stop=True)
                        ins.then_inc(qf_made, 1)
                    if has(0):
                        weights(i, 1, i + 3 if not isinstance(i, int) else min(i + 3, PAIRS))
                        values(i, par, 1)
                        for b in range(2):
                            need(pe, vf_used, i * 2 + b + 1)
                            need(pe, x_new, i)
                            for n in range(2):
                                ins = pe.matmul(y_ps[S * b:S * b + S, :], m[:, 7, S * n:S * n + S], pv[:, b, n, :], start=(n == 0), stop=(n == 1))
                        ins.then_inc(summed, 1)

                pipelined(pe, step, 0, 2)

            @block.scalar
            def _(act):
                def weights(p, b):
                    need(act, wf_made, p * 2 + b + 1)
                    need(act, vf_used, p * 2)
                    act.copy(wf[:, b, :], kf_ps[:, :]).then_inc(wf_out, 1)

                def step(i, par, has):
                    if has(0):
                        need(act, wT_made, i + 1)
                        need(act, wf_made, i * 2)
                        act.copy(wT[:, :], wT_ps[:, :]).then_inc(wT_out, 1)
                    if has(1):
                        need(act, cor_made, i + 2)
                        need(act, w_ready, i + 1)
                        act.copy(cor[:, :, :], cor_ps[:, :, :]).then_inc(cor_out, 1)
                    if has(0):
                        weights(i, 0)
                    if has(2):
                        need(act, kf_made, i + 3)
                        need(act, qf_used, i * 2 + 4)
                        act.copy(kf[:, :], kf_ps[:, :]).then_inc(kf_out, 1)
                    if has(1):
                        need(act, shifted, i + 2)
                        act.activation(te[:, :, :], te[:, :, :], ACT.Exp).then_inc(exped, 1)
                        act.activation(e[:, :, :], e[:, :, :], ACT.Exp).then_inc(exped, 1)
                    if has(0):
                        weights(i, 1)

                pipelined(act, step, 0, 2)

            @block.vector
            def _(dve):
                def values(p, b):
                    need(dve, vf_made, p * 2 + b + 1)
                    need(dve, wf_out, p * 2 + b + 1)
                    need(dve, summed, p)
                    dve.tensor_tensor(pv[:, b, :, :], vf_ps[:, :, :], wf[:, b:b + 1, :].to_broadcast([P, 2, D]), ALU.mult).then_inc(vf_used, 1)

                def step(i, par, has):
                    if has(2):
                        need(dve, qf_made, i + 1)
                        normalised(c, dve, xn[:, par, :], i + 2).then_inc(xn_ready, 1)
                    if has(1):
                        ch = Chain(dve, chain, i + 1, 6)
                        need(dve, cor_out, i + 2)
                        need(dve, wT_made, i + 1)
                        dve.tensor_copy(sm[:, 0:1], cor[:, 0, 0:1])
                        for g in range(8):
                            ins = dve.max(out=top[:, g, :], in_=cor[:, g, :])
                        ch.step(ins)
                        dve.tensor_tensor(te[:, :, :], top[:, :, :], spread(top[:, :, 0], TOP), ALU.subtract)
                        dve.tensor_tensor(e[:, :, :], cor[:, :, :], spread(top[:, :, 0], S), ALU.subtract).then_inc(shifted, 1)
                        for g in range(8):
                            ins = dve.match_replace(out=z[:, g, :], in_to_replace=top[:, g, :], in_values=cor[:, g, :], imm_value=LOW)
                        ch.step(ins)
                        ch.step(dve.tensor_tensor(z[:, :, :], cor[:, :, :], z[:, :, :], ALU.not_equal))
                    if has(0):
                        values(i, 0)
                    if has(2):
                        need(dve, qf_made, i + 3)
                        need(dve, kf_out, i + 3)
                        need(dve, cor_made, i + 1)
                        for n in range(2):
                            dve.tensor_tensor(pa[:, par, n, :], qf_ps[:, n, :], kf[:, :], ALU.mult).then_inc(qf_used, 1)
                    if has(1):
                        need(dve, exped, i * 2 + 4)
                        ch.step(dve.tensor_reduce(sm[:, :], te[:, :, :], X, ALU.add))
                        ch.step(dve.reciprocal(sm[:, :], sm[:, :]))
                        ch.step(dve.tensor_tensor(e[:, :, :], e[:, :, :], z[:, :, :], ALU.mult))
                        dve.tensor_tensor(e[:, :, :], e[:, :, :], spread(sm[:, :], S), ALU.mult).then_inc(w_ready, 1)
                        ch.end()
                    if has(0):
                        values(i, 1)
                        need(dve, summed, i + 1)
                        dve.scalar_tensor_tensor(out=c.x[:, i, :], in0=y_ps[:, :], scalar=c.gate[:, 2:3], in1=c.x[:, i, :],
                                                 op0=ALU.mult, op1=ALU.add).then_inc(x_new, 1)
                        need(dve, x_new, i + 1)
                        dve.bn_stats(c.stats[:, i, :], c.x[:, i, :]).then_inc(stats, 1)

                pipelined(dve, step, 0, 2)


FP8_MAX = 448.0
EXP_BITS = 0x7F800000


def fp8_linear_stage(c, w8T, w_scale, bias16):
    nc = c.nc
    with Stage(nc, "fp8") as s:
        xn = s.sb("xn", [P, PAIRS, D])
        mags = s.sb("mags", [P, PAIRS])
        amax, amax_all, sc = s.sb("amax", [P, 1]), s.sb("amax_all", [P, 1]), s.sb("sc", [P, 4])
        w_raw = s.sb("w_raw", [P, KT, D], U8)
        w_int = s.sb("w_int", [P, KT, D], I32)
        w_t = s.sb("w_t", [P, KT, D], I32)
        w_a = s.sb("w_a", [P, KT, D])
        w = s.sb("w", [P, KT, D], BF16)
        bias = s.sb("bias", [P, D], BF16)
        ws = s.sb("ws", [P, 1])
        y = s.sb("y", [P, 2, D])
        unit = s.sb("unit", [P, 2, D])
        q = s.sb("q", [P, 2, D], BF16)
        xT = s.sb("xT", [P, 2, KT, P], BF16)
        o16 = s.sb("o16", [P, 2, D], BF16)
        xT_ps = s.ps("xT_ps", [P, 2, 2 * KT, P], BF16)
        y_ps = s.ps("y_ps", [P, 2, D])
        w_in, b_in, chain, maxed, scaled = s.sem("w_in"), s.sem("b_in"), s.sem("chain"), s.sem("maxed"), s.sem("scaled")
        xn_made, w_made, reduced = s.sem("xn_made"), s.sem("w_made"), s.sem("reduced")
        x_scaled, stats = s.sem("x_scaled"), s.sem("stats")
        bounded, united, q_ready, lchain = s.sem("bounded"), s.sem("united"), s.sem("q_ready"), s.sem("lchain")
        xT_made, xT_out, summed, out_ready, x_new = (s.sem(n) for n in ("xT_made", "xT_out", "summed", "out_ready", "x_new"))
        with nc.Block() as block:
            @block.sync
            def _(sp):
                sp.dma_start(w_raw[:, :, :], w8T.rearrange("(k p) n -> p k n", p=P)).then_inc(w_in, 16)
                sp.dma_start(bias[:, :], bias16.rearrange("(o n) -> o n", o=1).to_broadcast([P, D])).then_inc(b_in, 16)
                sp.dma_start(ws[:, :], w_scale.rearrange("(o n) -> o n", o=1).to_broadcast([P, 1])).then_inc(b_in, 16)

            @block.gpsimd
            def _(pool):
                pool.wait_ge(maxed, 1)
                pool.partition_all_reduce(amax_all[:, :], amax[:, :], P, RMAX).then_inc(reduced, 1)
                pool.wait_ge(scaled, 1)

                def step(v, par, has):
                    if has(0):
                        need(pool, out_ready, v + 1)
                        pool.tensor_tensor(o16[:, par, :], o16[:, par, :], bias[:, :], ALU.add).then_inc(bounded, 1)

                pipelined(pool, step, 0, 2)

            @block.vector
            def _(dve):
                for t in range(PAIRS):
                    dve.wait_ge(xn_made, t + 1)
                    ins = dve.tensor_reduce(mags[:, t:t + 1], xn[:, t, :], X, ALU.max, apply_absolute_value=True)
                ch = Chain(dve, chain)
                ch.step(ins)
                dve.tensor_reduce(amax[:, :], mags[:, :], X, ALU.max).then_inc(maxed, 1)
                dve.wait_ge(w_in, 16)
                ch.step(dve.tensor_copy(w_int[:, :, :], w_raw[:, :, :]))
                ch.step(dve.tensor_scalar(w_t[:, :, :], w_int[:, :, :], 0x7F, 20, ALU.bitwise_and, ALU.logical_shift_left))
                ch.step(dve.tensor_scalar(w_t[:, :, :], w_t[:, :, :], 0x40000000, None, ALU.bitwise_or))
                ch.step(dve.tensor_scalar(w_a[:, :, :], w_t[:, :, :].bitcast(F32), 2.0 ** -7, -2.0 ** -6, ALU.mult, ALU.add))
                ch.step(dve.scalar_tensor_tensor(out=w_a[:, :, :], in0=w_t[:, :, :].bitcast(F32), scalar=2.0 ** -8, in1=w_a[:, :, :],
                                                 op0=ALU.mult, op1=ALU.min))
                ch.step(dve.tensor_scalar(w_int[:, :, :], w_int[:, :, :], 0x80, 24, ALU.bitwise_and, ALU.logical_shift_left))
                ch.step(dve.tensor_tensor(w_int[:, :, :], w_int[:, :, :], w_a[:, :, :].bitcast(I32), ALU.bitwise_or))
                ch.step(dve.tensor_copy(w[:, :, :], w_int[:, :, :].bitcast(F32)))
                dve.sem_inc(w_made, 1)
                dve.wait_ge(reduced, 1)
                dve.wait_ge(b_in, 32)
                ch.step(dve.tensor_scalar(sc[:, 0:1], amax_all[:, :], 1.0 / FP8_MAX, 1e-12, ALU.mult, ALU.max))
                ch.step(dve.reciprocal(sc[:, 1:2], sc[:, 0:1]))
                dve.tensor_tensor(sc[:, 2:3], sc[:, 0:1], ws[:, :], ALU.mult).then_inc(scaled, 1)
                dve.wait_ge(scaled, 1)

                def step(v, par, has):
                    if has(1):
                        u = 1 - par
                        need(dve, x_scaled, v + 2)
                        lc = Chain(dve, lchain, v + 1, 3)
                        lc.step(dve.tensor_scalar(y[:, u, :], y[:, u, :], FP8_MAX, -FP8_MAX, ALU.min, ALU.max))
                        lc.step(dve.tensor_scalar(unit[:, u, :].bitcast(I32), y[:, u, :].bitcast(I32), EXP_BITS, None, ALU.bitwise_and))
                        lc.step(dve.tensor_scalar(unit[:, u, :], unit[:, u, :], 2.0 ** -6, 1.5 * 2.0 ** 20, ALU.max, ALU.mult))
                        dve.tensor_tensor(y[:, u, :], y[:, u, :], unit[:, u, :], ALU.add).then_inc(united, 1)
                        need(dve, united, v + 2)
                        need(dve, xT_made, v)
                        dve.tensor_tensor(q[:, u, :], y[:, u, :], unit[:, u, :], ALU.subtract).then_inc(q_ready, 1)
                        lc.end()
                    if has(0):
                        need(dve, bounded, v + 1)
                        dve.scalar_tensor_tensor(out=c.x[:, v, :], in0=o16[:, par, :], scalar=c.gate[:, 6:7], in1=c.x[:, v, :],
                                                 op0=ALU.mult, op1=ALU.add).then_inc(x_new, 1)
                        need(dve, x_new, v + 1)
                        dve.bn_stats(c.stats[:, v, :], c.x[:, v, :]).then_inc(stats, 1)

                pipelined(dve, step, 0, 2)

            @block.tensor
            def _(pe):
                pe.wait_ge(w_made, 1)

                def step(v, par, has):
                    if has(1):
                        u = 1 - par
                        need(pe, q_ready, v + 2)
                        need(pe, xT_out, v)
                        for k in range(KT):
                            ins = pe.transpose(xT_ps[:, u, k, :], q[:, u, P * k:P * k + P], c.identb[:, :])
                        ins.then_inc(xT_made, 1)
                        need(pe, xT_out, v + 2)
                        need(pe, out_ready, v)
                        for k in range(KT):
                            ins = pe.matmul(y_ps[:, u, :], xT[:, u, k, :], w[:, k, :], start=(k == 0), stop=(k == KT - 1))
                        ins.then_inc(summed, 1)

                pipelined(pe, step, 0, 2)

            @block.scalar
            def _(act):
                for t in range(PAIRS):
                    act.activation(xn[:, t, :], c.x[:, t, :], ACT.Identity, bias=c.shift[:, t:t + 1], scale=c.rstd[:, t:t + 1]).then_inc(xn_made, 1)
                act.wait_ge(scaled, 1)

                def step(v, par, has):
                    if has(2):
                        need(act, q_ready, v + 1)
                        act.activation(y[:, par, :], xn[:, v + 2, :], ACT.Copy, scale=sc[:, 1:2]).then_inc(x_scaled, 1)
                    if has(1):
                        u = 1 - par
                        need(act, xT_made, v + 2)
                        need(act, summed, v)
                        act.copy(xT[:, u, :, :], xT_ps[:, u, 0:KT, :]).then_inc(xT_out, 1)
                        need(act, summed, v + 2)
                        need(act, x_new, v)
                        act.activation(o16[:, u, :], y_ps[:, u, :], ACT.Copy, scale=sc[:, 2:3]).then_inc(out_ready, 1)

                pipelined(act, step, 0, 2)


HEADS3, HD3, LQ, LKV = 16, 32, 64, 32


def latent_attention_stage(c, ctxT, wq_dT, w_qk, wkv_d4, wv_u):
    nc = c.nc
    with Stage(nc, "mla") as s:
        HT = HEADS3 * LKV // P
        wq = s.sb("wq", [P, KT, LQ])
        wqk = s.sb("wqk", [LQ, HEADS3 * LKV])
        wkv = s.sb("wkv", [P, KT, P])
        wv = s.sb("wv", [LKV, D])
        xn = s.sb("xn", [P, 2, D])
        xT = s.sb("xT", [P, 2, KT, P])
        cT = s.sb("cT", [P, 2, KT, P])
        cq = s.sb("cq", [LQ, 2, P])
        ql = s.sb("ql", [P, 2, HT, P])
        kl = s.sb("kl", [LKV, 2, P])
        kbd = s.sb("kbd", [P, 2, 2, 4, S])
        v = s.sb("v", [P, 2, D])
        d = s.sb("d", [P, HEADS3, S])
        mx = s.sb("mx", [P, HEADS3])
        e = s.sb("e", [P, 2, HEADS3, P])
        sm = s.sb("sm", [P, 2, HEADS3])
        eT = s.sb("eT", [P, 2, 4, P])
        o = s.sb("o", [P, D])
        a_ps = s.ps("a_ps", [P, KT, P])
        b_ps = s.ps("b_ps", [P, 4, P])
        v_ps = s.ps("v_ps", [P, D])
        s_ps = s.ps("s_ps", [P, HEADS3, S])
        t_ps = s.ps("t_ps", [P, 2, 4, P])
        o_ps = s.ps("o_ps", [P, D])
        w_in, c_in, zeros = s.sem("w_in"), s.sems("c_in"), s.sem("zeros")
        xn_ready, xT_made, xT_out, lat_made, lat_out = (s.sem(n) for n in ("xn", "xT_made", "xT_out", "lat_made", "lat_out"))
        ql_made, ql_out, v_made, v_out = (s.sem(n) for n in ("ql_made", "ql_out", "v_made", "v_out"))
        scored, maxed, shifted, exped, sums, chain = (s.sem(n) for n in ("scored", "maxed", "shifted", "exped", "sums", "chain"))
        turned, turned_out, summed, divided, x_new = (s.sem(n) for n in ("turned", "turned_out", "summed", "divided", "x_new"))
        with nc.Block() as block:
            @block.sync
            def _(sp):
                sp.dma_start(wq[:, :, :], wq_dT.rearrange("(k p) n -> p k n", p=P)).then_inc(w_in, 16)
                sp.dma_start(wqk[:, :], w_qk).then_inc(w_in, 16)
                sp.dma_start(wkv[:, :, :], wkv_d4.rearrange("(k p) n -> p k n", p=P)).then_inc(w_in, 16)
                sp.dma_start(wv[:, :], wv_u).then_inc(w_in, 16)
                cols = ctxT.rearrange("(k p) n -> p k n", p=P)
                for u in range(2):
                    sp.dma_start(cT[:, u, :, :], cols[:, :, P * u:P * u + P]).then_inc(c_in[u], 16)
                with sp.Fori(0, TURNS - 1) as j:
                    for u in range(2):
                        sp.wait_ge(lat_made, j * 2 + (u + 1))
                        sp.dma_start(cT[:, u, :, :], cols[:, :, bass.ds((2 * j + u + 2) * P, P)]).then_inc(c_in[u], 16)


            @block.tensor
            def _(pe):
                pe.wait_ge(w_in, 64)
                pe.wait_ge(zeros, 2)

                def turn(p, par, n):
                    if n == 0:
                        need(pe, exped, p + 1)
                    need(pe, turned_out, p * 4 + max(0, n - 1))
                    for h in range(4):
                        ins = pe.transpose(t_ps[:, n % 2, h, :], e[:, par, 4 * n + h, :], c.ident[:, :])
                    ins.then_inc(turned, 1)

                def weigh(p, par, n):
                    need(pe, turned_out, p * 4 + n + 1)
                    if n == 0:
                        need(pe, divided, p)
                        need(pe, v_out, p + 1)
                    for h in range(4):
                        cols = slice(HD3 * (4 * n + h), HD3 * (4 * n + h) + HD3)
                        ins = pe.matmul(o_ps[:, cols], eT[:, n % 2, h, :], v[:, par, cols], start=True, stop=True)
                    ins.then_inc(summed, 1)

                def step(i, par, has):
                    p = i + 2
                    if has(1):
                        u = 1 - par
                        need(pe, ql_out, i + 2)
                        need(pe, shifted, i + 1)
                        for b in range(2):
                            for n in range(HT):
                                ins = pe.matmul(s_ps[S * b:S * b + S, 4 * n:4 * n + 4, :].rearrange("p h k -> p (h k)"), ql[:, u, n, S * b:S * b + S],
                                                kbd[:, u, b, :, :].rearrange("p h k -> p (h k)"), start=True, stop=True)
                        ins.then_inc(scored, 1)
                    if has(0):
                        turn(i, par, 0)
                    if has(2):
                        need(pe, xn_ready, p + 1)
                        need(pe, ql_out, p)
                        for k in range(KT):
                            ins = pe.transpose(a_ps[:, k, :], xn[:, par, P * k:P * k + P], c.ident[:, :])
                        ins.then_inc(xT_made, 1)
                    if has(0):
                        turn(i, par, 1)
                        weigh(i, par, 0)
                    if has(2):
                        need(pe, xT_out, p + 1)
                        need(pe, c_in[par], (p - par) * 8 + 16)
                        need(pe, lat_out, p)
                        for k in range(KT):
                            pe.matmul(b_ps[0:LQ, 0, :], wq[:, k, :], xT[:, par, k, :], start=(k == 0), stop=(k == KT - 1))
                        for k in range(KT):
                            ins = pe.matmul(b_ps[:, 1, :], wkv[:, k, :], cT[:, par, k, :], start=(k == 0), stop=(k == KT - 1))
                        ins.then_inc(lat_made, 1)
                    if has(0):
                        turn(i, par, 2)
                        weigh(i, par, 1)
                    if has(2):
                        need(pe, lat_out, p + 1)
                        for n in range(HT):
                            ins = pe.matmul(a_ps[:, n, :], wqk[:, P * n:P * n + P], cq[:, par, :], start=True, stop=True)
                        ins.then_inc(ql_made, 1)
                        need(pe, v_out, p)
                        pe.matmul(v_ps[:, :], kl[:, par, :], wv[:, :], start=True, stop=True).then_inc(v_made, 1)
                    if has(0):
                        turn(i, par, 3)
                        weigh(i, par, 2)
                        weigh(i, par, 3)

                pipelined(pe, step, 0, 2)

            @block.scalar
            def _(act):
                act.wait_ge(zeros, 2)

                def turned_copy(p, n):
                    need(act, turned, p * 4 + n + 1)
                    need(act, summed, p * 4 + max(0, n - 1))
                    act.copy(eT[:, n % 2, :, :], t_ps[:, n % 2, :, :]).then_inc(turned_out, 1)

                def step(i, par, has):
                    p = i + 2
                    if has(0):
                        turned_copy(i, 0)
                    if has(2):
                        need(act, xT_made, p + 1)
                        act.copy(xT[:, par, :, :], a_ps[:, :, :]).then_inc(xT_out, 1)
                    if has(0):
                        turned_copy(i, 1)
                    if has(1):
                        u = 1 - par
                        need(act, shifted, i + 2)
                        need(act, sums, i)
                        need(act, turned, 4 * i)
                        for b in range(2):
                            half = slice(S * b, S * b + S)
                            ins = act.activation(e[half, u, :, half], d[half, :, :], ACT.Exp, scale=LKV ** -0.5)
                        ins.then_inc(exped, 1)
                    if has(2):
                        need(act, lat_made, p + 1)
                        need(act, v_made, p - 1)
                        need(act, scored, p - 1)
                        act.copy(cq[:, par, :], b_ps[0:LQ, 0, :])
                        act.copy(kl[:, par, :], b_ps[0:LKV, 1, :])
                        for h in range(4):
                            part = slice(LKV * h, LKV * h + LKV)
                            ins = act.copy(kbd[part, par, :, h, :], b_ps[part, 1, :].rearrange("p (b k) -> p b k", b=2))
                        ins.then_inc(lat_out, 1)
                    if has(0):
                        turned_copy(i, 2)
                    if has(2):
                        need(act, ql_made, p + 1)
                        act.copy(ql[:, par, :, :], a_ps[:, :, :]).then_inc(ql_out, 1)
                    if has(0):
                        turned_copy(i, 3)
                    if has(2):
                        need(act, v_made, p + 1)
                        need(act, summed, 4 * (p - 1))
                        act.copy(v[:, par, :], v_ps[:, :]).then_inc(v_out, 1)

                pipelined(act, step, 0, 2)

            @block.vector
            def _(dve):
                dve.memset(kbd[:, :, :, :, :], 0.0).then_inc(zeros, 1)
                dve.memset(e[:, :, :, :], 0.0).then_inc(zeros, 1)

                def step(i, par, has):
                    if has(2):
                        need(dve, xT_made, i + 1)
                        normalised(c, dve, xn[:, par, :], i + 2).then_inc(xn_ready, 1)
                    if has(1):
                        need(dve, scored, i + 2)
                        dve.tensor_reduce(mx[:, :], s_ps[:, :, :], X, ALU.max).then_inc(maxed, 1)
                        need(dve, maxed, i + 2)
                        need(dve, exped, i + 1)
                        dve.tensor_tensor(d[:, :, :], s_ps[:, :, :], spread(mx[:, :], S), ALU.subtract).then_inc(shifted, 1)
                    if has(0):
                        ch = Chain(dve, chain, i, 2)
                        need(dve, exped, i + 1)
                        for b in range(2):
                            half = slice(S * b, S * b + S)
                            ins = dve.tensor_reduce(sm[half, 0, :], e[half, par, :, half], X, ALU.add)
                        ins.then_inc(sums, 1)
                        need(dve, sums, i + 1)
                        ch.step(dve.reciprocal(sm[:, 1, :], sm[:, 0, :]))
                        need(dve, summed, i * 4 + 4)
                        dve.tensor_tensor(o[:, :].rearrange("p (h d) -> p h d", h=HEADS3), o_ps[:, :].rearrange("p (h d) -> p h d", h=HEADS3),
                                          spread(sm[:, 1, :], HD3), ALU.mult).then_inc(divided, 1)
                        need(dve, divided, i + 1)
                        dve.scalar_tensor_tensor(out=c.x[:, i, :], in0=o[:, :], scalar=c.gate[:, 3:4], in1=c.x[:, i, :],
                                                 op0=ALU.mult, op1=ALU.add).then_inc(x_new, 1)
                        need(dve, x_new, i + 1)
                        ch.step(dve.bn_stats(c.stats[:, i, :], c.x[:, i, :]))
                        ch.end()

                pipelined(dve, step, 0, 2)


HIDDEN, RANK3 = 1376, 16
H_TILES = [(P * n, min(P, HIDDEN - P * n)) for n in range(-(-HIDDEN // P))]


def swiglu_stage(c, gate_wT, up_wT, down_wT, gate_a, gate_bT, up_a, up_bT, down_a, down_bT, out):
    nc = c.nc
    with Stage(nc, "glu") as s:
        NH = len(H_TILES)
        w = s.sb("w", [P, 2, KT, HIDDEN])
        wd = s.sb("wd", [P, NH, D])
        a = s.sb("a", [RANK3, 2, D])
        b = s.sb("b", [RANK3, 2, HIDDEN])
        da = s.sb("da", [RANK3, HIDDEN])
        db = s.sb("db", [RANK3, D])
        xn = s.sb("xn", [P, 2, D])
        xT = s.sb("xT", [P, 2, KT, STEP])
        g = s.sb("g", [P, 2, STEP])
        h = s.sb("h", [P, 2, STEP])
        p_ps = s.ps("p_ps", [P, 4, STEP])
        y_ps = s.ps("y_ps", [P, 4, D])
        w_in, lora_in = s.sems("w_in", 3), s.sem("lora_in")
        fold_made, folded = s.sem("fold_made"), s.sem("folded")
        xn_ready, xT_made, xT_out = (s.sem(n) for n in ("xn", "xT_made", "xT_out"))
        projected, silued, h_ready, downed, x_new, stored = (s.sem(n) for n in ("projected", "silued", "h_ready", "downed", "x_new", "stored"))
        used = s.sem("used")
        pieces = [(n, k, c0, min(512, HIDDEN - c0)) for n in range(2) for k in range(KT) for c0 in range(0, HIDDEN, 512)]
        FOLDS = len(pieces) + NH
        with nc.Block() as block:
            @block.sync
            def _(sp):
                for n, (x_a, x_b) in enumerate(((gate_a, gate_bT), (up_a, up_bT))):
                    sp.dma_start(a[:, n, :], x_a).then_inc(lora_in, 16)
                    sp.dma_start(b[:, n, :], x_b).then_inc(lora_in, 16)
                sp.dma_start(da[:, :], down_a).then_inc(lora_in, 16)
                sp.dma_start(db[:, :], down_bT).then_inc(lora_in, 16)
                for n, m in enumerate((gate_wT, up_wT)):
                    sp.dma_start(w[:, n, :, :], m.rearrange("(k p) n -> p k n", p=P)).then_inc(w_in[n], 16)
                full = (NH - 1) * P
                sp.dma_start(wd[:, 0:NH - 1, :], down_wT[0:full, :].rearrange("(n p) d -> p n d", p=P)).then_inc(w_in[2], 16)
                sp.dma_start(wd[0:HIDDEN - full, NH - 1, :], down_wT[full:HIDDEN, :]).then_inc(w_in[2], 16)
                rows = rows_of(out)
                with sp.Fori(0, STEPS) as j:
                    for i in range(4):
                        sp.wait_ge(x_new, j * 4 + i + 1)
                        sp.dma_start(rows[:, 4 * j + i, :], c.x[:, 4 * j + i, :]).then_inc(stored, 16)
                sp.wait_ge(stored, 16 * PAIRS)

            @block.vector
            def _(dve):
                for f in range(FOLDS):
                    dve.wait_ge(fold_made, f + 1)
                    if f < len(pieces):
                        n, k, c0, wid = pieces[f]
                        dve.wait_ge(w_in[n], 16)
                        dst, rows = w[:, n, k, c0:c0 + wid], P
                    else:
                        t = f - len(pieces)
                        dve.wait_ge(w_in[2], 32)
                        rows, wid = H_TILES[t][1], D
                        dst = wd[0:rows, t, :]
                    dve.tensor_tensor(dst, dst, p_ps[0:rows, f % 2, 0:wid], ALU.add).then_inc(folded, 1)
                with dve.Fori(0, STEPS) as j:
                    for i in range(4):
                        t = 4 * j + i
                        dve.wait_ge(xT_made, t)
                        normalised(c, dve, xn[:, i % 2, :], t).then_inc(xn_ready, 1)
                    for n in range(NH):
                        rows = H_TILES[n][1]
                        dve.wait_ge(silued, j * NH + n + 1)
                        dve.wait_ge(downed, j * NH + max(0, n - 1))
                        dve.tensor_tensor(h[0:rows, n % 2, :], g[0:rows, n % 2, :], p_ps[0:rows, 2 * (n % 2) + 1, :], ALU.mult).then_inc(h_ready, 1)
                    for i in range(4):
                        t = 4 * j + i
                        dve.wait_ge(downed, j * NH + NH)
                        dve.scalar_tensor_tensor(out=c.x[:, t, :], in0=y_ps[:, i, :], scalar=c.gate[:, 7:8], in1=c.x[:, t, :],
                                                 op0=ALU.mult, op1=ALU.add).then_inc(x_new, 1)

            @block.scalar
            def _(act):
                with act.Fori(0, STEPS) as j:
                    for i in range(4):
                        act.wait_ge(xT_made, j * 4 + i + 1)
                        act.copy(xT[:, 0, :, P * i:P * i + P], p_ps[:, i % 2, :].rearrange("p (k r) -> p k r", k=KT)).then_inc(xT_out, 1)
                    for n in range(NH):
                        rows = H_TILES[n][1]
                        act.wait_ge(projected, j * NH + n + 1)
                        act.wait_ge(h_ready, j * NH + max(0, n - 1))
                        act.activation(g[0:rows, n % 2, :], p_ps[0:rows, 2 * (n % 2), :], ACT.Silu).then_inc(silued, 1)

            @block.tensor
            def _(pe):
                pe.wait_ge(lora_in, 96)
                for f in range(FOLDS):
                    pe.wait_ge(folded, f - 1) if f >= 2 else None
                    if f < len(pieces):
                        n, k, c0, wid = pieces[f]
                        ins = pe.matmul(p_ps[:, f % 2, 0:wid], a[:, n, P * k:P * k + P], b[:, n, c0:c0 + wid], start=True, stop=True)
                    else:
                        c0, rows = H_TILES[f - len(pieces)]
                        ins = pe.matmul(p_ps[0:rows, f % 2, :], da[:, c0:c0 + rows], db[:, :], start=True, stop=True)
                    ins.then_inc(fold_made, 1)
                pe.wait_ge(folded, FOLDS)
                with pe.Fori(0, STEPS) as j:
                    for i in range(4):
                        pe.wait_ge(xn_ready, j * 4 + i + 1)
                        pe.wait_ge(xT_out, j * 4 + max(0, i - 1))
                        if i == 0:
                            pe.wait_ge(h_ready, j * NH)
                        for k in range(KT):
                            ins = pe.transpose(p_ps[:, i % 2, P * k:P * k + P], xn[:, i % 2, P * k:P * k + P], c.ident[:, :])
                        ins.then_inc(xT_made, 1)
                    pe.wait_ge(xT_out, j * 4 + 4)
                    for n in range(NH + 1):
                        if n < NH:
                            c0, rows = H_TILES[n]
                            pe.wait_ge(h_ready, j * NH + max(0, n - 1))
                            for m in range(2):
                                for k in range(KT):
                                    ins = pe.matmul(p_ps[0:rows, 2 * (n % 2) + m, :], w[:, m, k, c0:c0 + rows], xT[:, 0, k, :], start=(k == 0), stop=(k == KT - 1))
                            ins.then_inc(projected, 1)
                        if n > 0:
                            q, rows = n - 1, H_TILES[n - 1][1]
                            pe.wait_ge(h_ready, j * NH + q + 1)
                            if q == 0:
                                pe.wait_ge(x_new, j * 4)
                            for i in range(4):
                                ins = pe.matmul(y_ps[:, i, :], h[0:rows, q % 2, P * i:P * i + P], wd[0:rows, q, :], start=(q == 0), stop=(q == NH - 1))
                            ins.then_inc(downed, 1)


def store_stage(c, out):
    nc = c.nc
    with Stage(nc, "store") as s:
        stored = s.sem("stored")
        with nc.Block() as block:
            @block.sync
            def _(sp):
                for q in range(4):
                    sp.dma_start(rows_of(out)[:, 4 * q:4 * q + 4, :], c.x[:, 4 * q:4 * q + 4, :]).then_inc(stored, 16)
                sp.wait_ge(stored, 64)


def program(nc, a, out, first=0, last=7):
    with ExitStack() as ctx:
        c = Core(nc, ctx)
        load_stage(c, a["x"], a["g_xattn"], a["g_ffn"])
        for n in range(first, last + 1):
            norm_stage(c, f"norm{n}")
            STAGES[n](c, {**a, "out": out})
        if last < 7:
            store_stage(c, out)


def _window(c, a):
    window_attention_stage(c, a["ctx"], *[a[f"w0{k}T"] for k in "qkvo"], *[a[f"b0{k}"] for k in "qkvo"], a["sum_heads"], a["expand_heads"])


def _moe(c, a):
    lora_mixture_stage(c, a["a0T"], a["b0T"], a["router_b"])


def _gqa(c, a):
    with Stage(c.nc, "gqa_in") as s:
        cosT, sinT = s.sb("cosT", [P, B * S]), s.sb("sinT", [P, B * S])
        limit = s.sb("limit", [P, PAIRS, S])
        xT16, cT16 = s.sb("xT16", [P, 2, KT, B * S], F16), s.sb("cT16", [P, 2, KT, B * S], F16)
        unit = s.sb("c_unit", [P, 1])
        prepare_stage(c, a["pos"], a["mask"], a["rope"], cosT, sinT, limit, a["ctxT"], cT16, unit[:, :], xT16)
        grouped_attention_stage(c, a["w1q"], a["w1k"], a["w1v"], a["w1o"], cosT, sinT, limit, xT16, cT16, unit[:, :])


def _lora(c, a):
    lora_linear_stage(c, a["w1"], a["b1"], a["gate1"], a["eye32"], a["a1"], a["b1T"], a["a1sT"], a["b1sT"])


def _corr(c, a):
    correlation_stage(c, a["ctx"], a["dfts"])


def _fp8(c, a):
    fp8_linear_stage(c, a["w8T"], a["w8_scale"], a["b8"])


def _mla(c, a):
    latent_attention_stage(c, a["ctxT"], a["wq_d"], a["w_qk"], a["wkv_d4"], a["wv_u"])


def _glu(c, a):
    swiglu_stage(c, *[a[k] for k in ("gate_wT", "up_wT", "down_wT", "gate_a", "gate_bT", "up_a", "up_bT", "down_a", "down_bT")], a["out"])


STAGES = (_window, _moe, _gqa, _lora, _corr, _fp8, _mla, _glu)


def layouts(i):
    t = lambda w: np.ascontiguousarray(np.asarray(w).T)
    m = {"x": np.asarray(i["x"]), "ctx": np.asarray(i["ctx_4096"]), "g_xattn": np.asarray(i["g_xattn"]), "g_ffn": np.asarray(i["g_ffn"])}
    for k in "qkvo":
        m[f"w0{k}T"] = t(i[f"L0_xattn_W{k}"])
        m[f"b0{k}"] = np.asarray(i[f"L0_xattn_b{k}"])
    m["a0T"] = t(np.concatenate([np.asarray(i["L0_ffn_A"]).reshape(ER, D), np.asarray(i["L0_ffn_router_w"])]))
    m["b0T"] = np.ascontiguousarray(np.asarray(i["L0_ffn_Bm"]).transpose(0, 2, 1).reshape(ER, D))
    m["pos"], m["mask"] = np.asarray(i["pos_BxS2"]), np.asarray(i["mask_BxSxS2_ik0"])
    m["rope"] = rope_tables()
    m["ctxT"] = t(np.asarray(i["ctx_4096"]).reshape(B * S, D))
    for k in "qkvo":
        m[f"w1{k}"] = np.asarray(i[f"L1_xattn_W{k}"])
    m["w1"], m["b1"] = np.asarray(i["L1_ffn_kernel"]), np.asarray(i["L1_ffn_bias"])
    m["gate1"] = np.ascontiguousarray(np.repeat(np.asarray(i["L1_ffn_gate"]).T, RANK1, axis=0).reshape(4, P, GROUPS1).transpose(1, 0, 2))
    m["eye32"] = np.tile(np.eye(RANK1, dtype=np.float32), (4, 1))
    m["a1"] = np.asarray(i["L1_ffn_lora_A"]).reshape(NR, D)
    m["b1T"] = np.ascontiguousarray(np.asarray(i["L1_ffn_lora_B"]).transpose(0, 2, 1).reshape(NR, D))
    m["a1sT"], m["b1sT"] = t(i["L1_ffn_lora_A_shared"]), t(i["L1_ffn_lora_B_shared"])
    m["dfts"] = correlation_tables()
    m["w8T"] = t(np.asarray(i["L2_ffn_weight_fp8"]).view(np.uint8))
    m["w8_scale"] = np.asarray(i["L2_ffn_weight_scale"]).reshape(1)
    m["b8"] = np.asarray(i["L2_ffn_bias"])
    m["wq_d"], m["w_qk"], m["wv_u"] = (np.asarray(i[f"L3_xattn_{k}"]) for k in ("Wq_d", "W_qk", "Wv_u"))
    m["wkv_d4"] = np.tile(np.asarray(i["L3_xattn_Wkv_d"]), (1, 4))
    for k in ("gate_w", "up_w", "down_w", "gate_b", "up_b", "down_b"):
        m[f"{k}T"] = t(i[f"L3_ffn_{k}"])
    for k in ("gate_a", "up_a", "down_a"):
        m[k] = np.asarray(i[f"L3_ffn_{k}"])
    m["router_b"] = np.asarray(i["L0_ffn_router_b"])
    m.update(window_tables())
    return m


def window_tables():
    p = np.arange(P)
    head = p // HD0
    sums = np.zeros((P, 2, 32), np.float32)
    expand = np.zeros((2, PARTS, BH, 2, P), np.float32)
    for par in range(2):
        sums[p, par, BH * par + head] = 1
        for part in range(PARTS):
            expand[par, part, head, par, p] = 1
    return {"sum_heads": sums, "expand_heads": expand.reshape(2 * PARTS * BH, 2, P)}


def kernel(**inputs):
    import concourse.bacc as bacc
    from concourse.bass_utils import run_bass_kernel_spmd

    nc = bacc.Bacc("TRN2", target_bir_lowering=False, num_devices=1)
    arrays = layouts(inputs)
    aps = {name: nc.dram_tensor(name, v.shape, mybir.dt.from_np(v.dtype), kind="ExternalInput").ap() for name, v in arrays.items()}
    out = nc.dram_tensor("y", (B, S, D), F32, kind="ExternalOutput").ap()
    program(nc, aps, out)
    return run_bass_kernel_spmd(nc, [arrays], core_ids=[0]).results[0]["y"]
```

```python
from contextlib import ExitStack

import concourse.bass as bass
import numpy as np
from concourse import mybir

F32 = mybir.dt.float32
BF16 = mybir.dt.bfloat16
I32 = mybir.dt.int32
U32 = mybir.dt.uint32
U8 = mybir.dt.uint8
F16 = mybir.dt.float16
ALU = mybir.AluOpType
ACT = mybir.ActivationFunctionType
X = mybir.AxisListType.X
RMAX = bass.bass_isa.ReduceOp.max

B, S, D = 32, 64, 512
P = 128
PAIRS = B * S // P
KT = D // P
EPS = 1e-5
TURNS = PAIRS // 2


def overlapped(ap, step, count, width):
    part = ap.ap[0]
    return bass.AP(tensor=ap.tensor, offset=ap.offset, ap=[list(part), [step, count], [1, width]])


def spread(ap, count):
    return ap.unsqueeze(len(ap.shape)).to_broadcast([*ap.shape, count])


class Stage:

    def __init__(self, nc, name):
        self.nc, self.name, self.ctx, self.used = nc, name, ExitStack(), []

    def __enter__(self):
        self.ctx.__enter__()
        return self

    def __exit__(self, *e):
        self.nc.clear_and_free_semaphores(self.used)
        self.nc.all_engine_barrier()
        return self.ctx.__exit__(*e)

    def sb(self, name, shape, dt=F32):
        return self.ctx.enter_context(self.nc.sbuf_tensor(f"{self.name}_{name}", shape, dt))

    def ps(self, name, shape, dt=F32):
        return self.ctx.enter_context(self.nc.psum_tensor(f"{self.name}_{name}", shape, dt))

    def sem(self, name):
        self.used.append(self.nc.alloc_semaphore(f"{self.name}_{name}"))
        return self.used[-1]

    def sems(self, name, n=2):
        return [self.sem(f"{name}{u}") for u in range(n)]


class Chain:

    def __init__(self, eng, sem, turn=0, per=0):
        self.eng, self.sem, self.base, self.per, self.n = eng, sem, turn * per, per, 0

    def step(self, ins):
        self.n += 1
        ins.then_inc(self.sem, 1)
        self.eng.wait_ge(self.sem, self.base + self.n)

    def end(self):
        assert self.n == self.per, (self.n, self.per)


class Core:

    def __init__(self, nc, ctx):
        def sb(name, shape, dt=F32):
            return ctx.enter_context(nc.sbuf_tensor(name, shape, dt))

        self.nc = nc
        self.x = sb("x_sb", [P, PAIRS, D])
        self.stats = sb("ln_stats", [P, PAIRS, 6])
        self.mv = sb("ln_mean_var", [P, PAIRS, 2])
        self.rstd = sb("ln_rstd", [P, PAIRS])
        self.shift = sb("ln_shift", [P, PAIRS])
        self.t1 = sb("ln_t1", [P, PAIRS])
        self.gate = sb("tanh_gates", [P, 8])
        self.ident = sb("ident", [P, P])
        self.identb = sb("ident_bf", [P, P], BF16)


def rows_of(ap):
    return ap.rearrange("(i b) s d -> (b s) i d", b=2)


def load_stage(c, x, g_xattn, g_ffn):
    nc = c.nc
    with Stage(nc, "load") as s:
        x_in, g_in, id_set, ids, stats = s.sems("x_in", 8), s.sem("g_in"), s.sem("id_set"), s.sem("ids"), s.sem("stats")
        g_raw = s.sb("g_raw", [P, 8])
        tanh_done = s.sem("tanh")
        with nc.Block() as block:
            @block.sync
            def _(sp):
                for q in range(8):
                    sp.dma_start(c.x[:, 2 * q:2 * q + 2, :], rows_of(x)[:, 2 * q:2 * q + 2, :]).then_inc(x_in[q], 16)
                sp.dma_start(g_raw[:, 0:4], g_xattn.rearrange("(o n) -> o n", o=1).to_broadcast([P, 4])).then_inc(g_in, 16)
                sp.dma_start(g_raw[:, 4:8], g_ffn.rearrange("(o n) -> o n", o=1).to_broadcast([P, 4])).then_inc(g_in, 16)

            @block.gpsimd
            def _(pool):
                pool.memset(c.ident[:, :], 0.0).then_inc(id_set, 1)
                pool.memset(c.identb[:, :], 0.0).then_inc(id_set, 1)
                pool.wait_ge(id_set, 2)
                for m in (c.ident, c.identb):
                    pool.affine_select(out=m[:, :], in_=m[:, :], compare_op=ALU.not_equal, fill=1.0,
                                       base=0, pattern=[[-1, P]], channel_multiplier=1).then_inc(ids, 1)

            @block.scalar
            def _(act):
                act.wait_ge(g_in, 32)
                act.activation(c.gate[:, :], g_raw[:, :], ACT.Tanh).then_inc(tanh_done, 1)

            @block.vector
            def _(dve):
                for i in range(PAIRS):
                    if i % 2 == 0:
                        dve.wait_ge(x_in[i // 2], 16)
                    dve.bn_stats(c.stats[:, i, :], c.x[:, i, :]).then_inc(stats, 1)


class Norm:

    STEPS = 6

    def __init__(self, c, s):
        self.c = c
        self.aggr, self.var_ready, self.root_ready, self.chain = s.sem("ln_aggr"), s.sem("ln_var"), s.sem("ln_root"), s.sem("ln_chain")
        self.var, self.root, self.t = s.sb("ln_var", [P, PAIRS]), s.sb("ln_root", [P, PAIRS]), s.sb("ln_t", [P, PAIRS])

    def act(self, act):
        act.wait_ge(self.var_ready, 1)
        act.activation(self.root[:, :], self.var[:, :], ACT.Sqrt).then_inc(self.root_ready, 1)

    def dve(self, dve):
        c, var, t = self.c, self.var, self.t
        for i in range(PAIRS):
            dve.bn_aggr(c.mv[:, i, :], c.stats[:, i, :]).then_inc(self.aggr, 1)
        dve.wait_ge(self.aggr, PAIRS)
        dve.tensor_scalar(var[:, :], c.mv[:, :, 1], EPS, None, ALU.add).then_inc(self.var_ready, 1)
        dve.wait_ge(self.root_ready, 1)
        dve.wait_ge(self.var_ready, 1)
        ch = Chain(dve, self.chain)
        ch.step(dve.reciprocal(c.rstd[:, :], self.root[:, :]))
        ch.step(dve.tensor_tensor(t[:, :], c.rstd[:, :], c.rstd[:, :], ALU.mult))
        ch.step(dve.tensor_tensor(t[:, :], t[:, :], var[:, :], ALU.mult))
        ch.step(dve.tensor_scalar(t[:, :], t[:, :], -0.5, 1.5, ALU.mult, ALU.add))
        ch.step(dve.tensor_tensor(c.rstd[:, :], c.rstd[:, :], t[:, :], ALU.mult))
        ch.step(dve.scalar_tensor_tensor(out=c.shift[:, :], in0=c.mv[:, :, 0], scalar=-1.0,
                                         in1=c.rstd[:, :], op0=ALU.mult, op1=ALU.mult))


def normalised(c, dve, out, t):
    t = bass.ds(t, 1)
    return dve.tensor_scalar(out, c.x[:, t, :].rearrange("p o d -> p (o d)"), c.rstd[:, t], c.shift[:, t], ALU.mult, ALU.add)


SPLIT = ((0, 0), (0, 1), (1, 0))
TOP16 = 2.0 ** 12
TINY = 1e-30


def need(eng, sem, value):
    if not isinstance(value, int) or value > 0:
        eng.wait_ge(sem, value)


def pipelined(eng, step, first, last, count=PAIRS):
    lo = -first + (-first) % 2
    hi = count - last
    hi -= (hi - lo) % 2

    def alone(v):
        step(v, v % 2, lambda off: 0 <= v + off < count)

    for v in range(-last, lo):
        alone(v)
    with eng.Fori(0, (hi - lo) // 2) as j:
        for par in range(2):
            step(2 * j + (lo + par), par, lambda off: True)
    for v in range(hi, count - first):
        alone(v)


WINDOW, HEADS0, HD0 = 16, 8, 8
PAD_L, PAD_R = WINDOW // 2, WINDOW - WINDOW // 2 - 1
BH = 2 * HEADS0
PARTS = 2
PROB_SCALE = 1024.0
BLOCK = P // (PARTS * BH)


def window_attention_stage(c, ctx_in, weightsT, biases, head_sums, head_spread):
    nc = c.nc
    with Stage(nc, "win") as s:
        TB = D // P
        w4 = s.sb("w4", [P, 4, P])
        bias4 = s.sb("bias4", [P, 4])
        sumw = s.sb("sumw", [P, 2, 32])
        expw = s.sb("expw", [P, BLOCK, P], F16)
        expw_in = s.sb("expw_in", [P, BLOCK, P])
        ident16 = s.sb("ident16", [P, P], F16)
        cin = s.sb("cin", [P, 2, D])
        xn = s.sb("xn", [P, 2, D])
        q = s.sb("q", [P, 2, D])
        kp = s.sb("kp", [P, 2, D + WINDOW])
        vp = s.sb("vp", [P, 2, D + WINDOW])
        WS = 4
        prod = s.sb("prod", [P, WINDOW // WS, WS, D])
        dots = s.sb("dots", [P, 2, D])
        e = s.sb("e", [P, TB, WINDOW, BH])
        pr = s.sb("pr", [P, TB, WINDOW, BH])
        mx = s.sb("mx", [P, TB, BH])
        sm = s.sb("sm", [P, TB, BH])
        parts = s.sb("parts", [P, TB, WINDOW, PARTS, BH], F16)
        pT = s.sb("pT", [P, WINDOW // BLOCK, D], F16)
        pv = s.sb("pv", [P, WINDOW // 2, 2, D])
        acc = s.sb("acc", [P, 2, D])
        acc1 = s.sb("acc1", [P, D])
        upd = s.sb("upd", [P, D])
        mm = s.ps("mm", [P, D])
        dps = s.ps("dps", [P, D])
        tps = s.ps("tps", [P, TB, WINDOW, BH])
        eps_ = s.ps("eps", [P, 2, 2, D])

        w_in, w_zero, b_ready = s.sem("w_in"), s.sem("w_zero"), s.sem("b_ready")
        ctx_loaded = s.sems("ctx_loaded")
        xn_ready = s.sem("xn_ready")
        proj, outp = s.sem("proj"), s.sem("outp")
        proj_read = s.sem("proj_read")
        prod_ready, prod_used = s.sem("prod_ready"), s.sem("prod_used")
        dots_out, dotsT = s.sem("dots_out"), s.sem("dotsT")
        shifted, exped, probs, dve_chain = s.sem("shifted"), s.sem("exped"), s.sem("probs"), s.sem("dve_chain")
        hi, lo = s.sem("hi"), s.sem("lo")
        pT_ps, pT_read = s.sem("pT_ps"), s.sem("pT_read")
        spread_ready, pv_ready, added, acc_ready = s.sem("spread_ready"), s.sem("pv_ready"), s.sem("added"), s.sem("acc_ready")
        upd_ready, x_new, stats = s.sem("upd_ready"), s.sem("x_new"), s.sem("stats")
        NP = WINDOW // WS
        def tph(n):
            flat = tps[:, :, :, :].rearrange("p a b c -> p (a b c)").bitcast(F16)
            return flat[:, 1024 * n:1024 * n + 1024].rearrange("p (w t) -> p w t", w=2)

        norm = Norm(c, s)
        with nc.Block() as block:
            @block.sync
            def _(sp):
                rows = rows_of(ctx_in)
                for u in range(2):
                    sp.dma_start(cin[:, u, :], rows[:, u, :]).then_inc(ctx_loaded[u], 16)
                sp.wait_ge(w_zero, 1)
                for b in range(2):
                    sp.dma_start(w4[64 * b:64 * b + 64, :, 64 * b:64 * b + 64], weightsT).then_inc(w_in, 16)
                sp.dma_start(bias4[:, :], biases).then_inc(w_in, 16)
                sp.dma_start(sumw[:, :, :], head_sums).then_inc(w_in, 16)
                sp.dma_start(expw_in[:, :, :], head_spread).then_inc(w_in, 16)
                with sp.Fori(0, TURNS - 1) as j:
                    for u in range(2):
                        sp.wait_ge(proj, j * 6 + 3 * u + 2)
                        sp.dma_start(cin[:, u, :], rows[:, 2 * j + u + 2, :]).then_inc(ctx_loaded[u], 16)


            @block.gpsimd
            def _(pool):
                def add(p, n):
                    need(pool, pv_ready, 8 * p + n + 1)
                    if n == 1:
                        need(pool, acc_ready, p)
                        pool.tensor_tensor(acc[:, :, :], pv[:, 0, :, :], pv[:, 1, :, :], ALU.add).then_inc(added, 2)
                    else:
                        need(pool, added, 8 * p + n)
                        pool.tensor_tensor(acc[:, :, :], acc[:, :, :], pv[:, n, :, :], ALU.add).then_inc(added, 1)

                def step(v, par, has):
                    for n in range(1, 6):
                        if has(0):
                            add(v, n)
                        if n == 3 and has(-1):
                            need(pool, upd_ready, v)
                            pool.tensor_tensor(c.x[:, v - 1, :], c.x[:, v - 1, :], upd[:, :], ALU.add).then_inc(x_new, 1)
                    if has(1):
                        need(pool, hi, v + 2)
                        pool.tensor_tensor(parts[:, :, :, 1, :], pr[:, :, :, :], parts[:, :, :, 0, :], ALU.subtract).then_inc(lo, 1)
                    if has(0):
                        add(v, 6)
                        add(v, 7)
                    if has(0):
                        need(pool, added, 8 * v + 8)
                        need(pool, outp, v)
                        pool.tensor_tensor(acc1[:, :], acc[:, 0, :], acc[:, 1, :], ALU.add).then_inc(acc_ready, 1)

                pipelined(pool, step, -1, 2)

            @block.scalar
            def _(act):
                norm.act(act)
                act.wait_ge(norm.chain, Norm.STEPS)
                act.wait_ge(b_ready, 3)
                act.wait_ge(w_zero, 3)

                def dots_half(p, h):
                    need(act, prod_used, NP * p + (h + 1) * NP // 2)
                    need(act, dotsT, p)
                    act.copy(dots[:, h, :], dps[:, :]).then_inc(dots_out, 1)

                def pT_copy(v, n):
                    need(act, pT_ps, v * 2 + n + 1)
                    if n == 0:
                        need(act, spread_ready, v * 8)
                    act.copy(pT[:, 2 * n:2 * n + 2, :], tph(n)).then_inc(pT_read, 1)

                def step(v, par, has):
                    p = v + 2
                    if has(0):
                        pT_copy(v, 0)
                        pT_copy(v, 1)
                    if has(1):
                        dots_half(v + 1, 0)
                        dots_half(v + 1, 1)
                    if has(-1):
                        need(act, outp, v)
                        need(act, x_new, v - 1)
                        act.activation(upd[:, :], mm[:, :], ACT.Identity, bias=bias4[:, 3:4], scale=c.gate[:, 0:1]).then_inc(upd_ready, 1)
                    if has(2):
                        need(act, proj, 3 * v + 3)
                        t = bass.ds(p, 1)
                        act.activation(xn[:, par, :], c.x[:, t, :].rearrange("p o d -> p (o d)"), ACT.Identity,
                                       bias=c.shift[:, t], scale=c.rstd[:, t]).then_inc(xn_ready, 1)
                        need(act, proj, p * 3 + 1)
                        need(act, prod_ready, (p - 1) * NP)
                        act.activation(kp[:, par, PAD_L:PAD_L + D], mm[:, :], ACT.Identity, bias=bias4[:, 1:2]).then_inc(proj_read, 1)
                    if has(1):
                        need(act, shifted, v + 2)
                        act.activation(e[:, :, :, :], e[:, :, :, :], ACT.Exp).then_inc(exped, 1)
                    if has(2):
                        need(act, proj, p * 3 + 2)
                        need(act, pv_ready, (p - 1) * 8)
                        act.activation(vp[:, par, PAD_L:PAD_L + D], mm[:, :], ACT.Identity, bias=bias4[:, 2:3]).then_inc(proj_read, 1)
                        need(act, proj, p * 3 + 3)
                        act.activation(q[:, par, :], mm[:, :], ACT.Identity, bias=bias4[:, 0:1], scale=HD0 ** -0.5).then_inc(proj_read, 1)
                    if has(1):
                        need(act, probs, v + 2)
                        need(act, pT_ps, (v + 1) * 2)
                        act.copy(parts[:, :, :, 0, :], pr[:, :, :, :]).then_inc(hi, 1)

                pipelined(act, step, -1, 2)

            @block.tensor
            def _(pe):
                pe.wait_ge(w_in, 16 * 5)
                pe.wait_ge(b_ready, 1)

                def reduce(p, n):
                    need(pe, prod_ready, p * NP + n + 1)
                    need(pe, dots_out, 2 * p + n // 2)
                    par = n % 2
                    for g in range(WS):
                        ins = pe.matmul(dps[32 * g:32 * g + 32, :], sumw[:, par, :], prod[:, n, g, :], start=(par == 0), stop=(par == 1))
                    ins.then_inc(prod_used, 1)

                def spread_probs(p, n):
                    if n % 4 == 0:
                        need(pe, pT_read, p * 2 + n // 4 + 1)
                    need(pe, pv_ready, p * 8 + n - 1)
                    for b in range(2):
                        ins = pe.matmul(eps_[:, n % 2, b, :], expw[:, 2 * (n % 2) + b, :], pT[:, n // 2, :], start=True, stop=True)
                    ins.then_inc(spread_ready, 1)

                def turn(v, n):
                    if n == 0:
                        need(pe, lo, v + 1)
                    need(pe, pT_read, v * 2)
                    for wp in range(2):
                        first = BLOCK * (2 * n + wp)
                        for tb in range(TB):
                            ins = pe.transpose(tph(n)[:, wp, P * tb:P * tb + P],
                                               parts[:, tb, first:first + BLOCK, :, :].rearrange("p a b c -> p (a b c)"), ident16[:, :])
                    ins.then_inc(pT_ps, 1)

                def project(p, par, m, src):
                    need(pe, proj_read, p * 3 + m)
                    pe.matmul(mm[:, :], w4[:, (1, 2, 0)[m], :], src[:, par, :], start=True, stop=True).then_inc(proj, 1)

                def step(v, par, has):
                    p = v + 2
                    if has(1):
                        reduce(v + 1, 0)
                    if has(0):
                        turn(v, 0)
                        turn(v, 1)
                        spread_probs(v, 0)
                        spread_probs(v, 1)
                    for n in range(1, NP):
                        if has(1):
                            reduce(v + 1, n)
                        if has(0):
                            spread_probs(v, n + 1)
                    if has(0):
                        spread_probs(v, NP + 1)
                    if has(-1):
                        need(pe, acc_ready, v)
                        need(pe, proj_read, min(3 * v + 6, 3 * PAIRS) if isinstance(v, int) else 3 * v + 6)
                        pe.matmul(mm[:, :], w4[:, 3, :], acc1[:, :], start=True, stop=True).then_inc(outp, 1)
                    if has(1):
                        need(pe, dots_out, 2 * v + 4)
                        need(pe, pT_read, 2 * v + 2)
                        for tb in range(TB):
                            for half in range(2):
                                ins = pe.transpose(tps[:, tb, 8 * half:8 * half + 8, :].rearrange("p a b -> p (a b)"),
                                                   dots[:, half, P * tb:P * tb + P], c.ident[:, :])
                        ins.then_inc(dotsT, 1)
                    if has(2):
                        need(pe, upd_ready, p - 2)
                        need(pe, ctx_loaded[par], 16 * (p // 2 + 1) if isinstance(p, int) else (p - par) * 8 + 16)
                        project(p, par, 0, cin)
                    if has(0):
                        spread_probs(v, 6)
                    if has(2):
                        project(p, par, 1, cin)
                    if has(0):
                        spread_probs(v, 7)
                    if has(2):
                        need(pe, xn_ready, p + 1)
                        project(p, par, 2, xn)

                pipelined(pe, step, -1, 2)

            @block.vector
            def _(dve):
                dve.memset(w4[:, :, :], 0.0).then_inc(w_zero, 1)
                norm.dve(dve)
                dve.memset(kp[:, :, :], 0.0).then_inc(w_zero, 1)
                dve.memset(vp[:, :, :], 0.0).then_inc(w_zero, 1)
                dve.wait_ge(w_in, 16 * 5)
                dve.tensor_copy(ident16[:, :], c.ident[:, :])
                dve.tensor_copy(expw[:, :, :], expw_in[:, :, :]).then_inc(b_ready, 1)
                dve.tensor_scalar(bias4[:, 0:1], bias4[:, 0:1], HD0 ** -0.5, None, ALU.mult).then_inc(b_ready, 1)
                dve.tensor_scalar(bias4[:, 3:4], bias4[:, 3:4], c.gate[:, 0:1], None, ALU.mult).then_inc(b_ready, 1)

                def weigh(p, par, n):
                    first = 8 * (n // 4) + n % 4
                    need(dve, spread_ready, p * 8 + n + 1)
                    need(dve, added, 8 * (p - 1) + max(2, n + 1))
                    dve.tensor_tensor(pv[:, n, :, :], eps_[:, n % 2, :, :], overlapped(vp[:, par, first:first + D], WS, 2, D),
                                      ALU.mult).then_inc(pv_ready, 1)

                def step(v, par, has):
                    if has(1):
                        p, other = v + 1, 1 - par
                        need(dve, proj_read, p * 3 + 3)
                        for n in range(NP):
                            need(dve, prod_used, (p - 1) * NP + n + 1)
                            dve.tensor_tensor(prod[:, n, :, :],
                                              q[:, other:other + 1, :].to_broadcast([P, WS, D]),
                                              overlapped(kp[:, other, WS * n:WS * n + D], 1, WS, D), ALU.mult).then_inc(prod_ready, 1)
                    if has(0):
                        need(dve, proj_read, v * 3 + 3)
                        for n in range(6):
                            weigh(v, par, n)
                    if has(1):
                        need(dve, dotsT, p + 1)
                        ch = Chain(dve, dve_chain, p, 4)
                        ch.step(dve.tensor_reduce(mx[:, :, :], tps[:, :, :, :].rearrange("p a w b -> p a b w"), X, ALU.max))
                        dve.tensor_tensor(e[:, :, :, :], tps[:, :, :, :], mx[:, :, :].unsqueeze(2).to_broadcast([P, TB, WINDOW, BH]),
                                          ALU.subtract).then_inc(shifted, 1)
                    if has(0):
                        for n in range(6, 8):
                            weigh(v, par, n)
                    if has(1):
                        need(dve, exped, p + 1)
                        ch.step(dve.tensor_reduce(sm[:, :, :], e[:, :, :, :].rearrange("p a w b -> p a b w"), X, ALU.add))
                        ch.step(dve.tensor_scalar(sm[:, :, :], sm[:, :, :], 1 / PROB_SCALE, None, ALU.mult))
                        ch.step(dve.reciprocal(sm[:, :, :], sm[:, :, :]))
                        need(dve, lo, p)
                        dve.tensor_tensor(pr[:, :, :, :], e[:, :, :, :], sm[:, :, :].unsqueeze(2).to_broadcast([P, TB, WINDOW, BH]),
                                          ALU.mult).then_inc(probs, 1)
                        ch.end()
                    if has(-1):
                        need(dve, x_new, v)
                        dve.bn_stats(c.stats[:, v - 1, :], c.x[:, v - 1, :]).then_inc(stats, 1)

                pipelined(dve, step, -1, 2)


EXPERTS, RANK0 = 8, 16
SCALING0 = 8.0 / RANK0
ER = EXPERTS * RANK0


def lora_mixture_stage(c, aT, bT, router_b):
    nc = c.nc
    with Stage(nc, "moe") as s:
        a_sb = s.sb("a", [P, KT, ER + EXPERTS])
        b_sb = s.sb("b", [P, D])
        rb = s.sb("rb", [P, EXPERTS])
        g = s.sb("g", [P, 1])
        iota = s.sb("iota", [P, EXPERTS])
        xn = s.sb("xn", [P, 2, D])
        xT = s.sb("xT", [P, 2, KT, P])
        lg = s.sb("lg", [P, EXPERTS])
        top = s.sb("top", [P, 8])
        at_top = s.sb("at_top", [P, 8], U32)
        at_topf = s.sb("at_topf", [P, 8])
        diff = s.sb("diff", [P, 2])
        ex = s.sb("ex", [P, 2])
        wt = s.sb("wt", [P, 2, EXPERTS])
        hw = s.sb("hw", [P, 2, ER])
        hT = s.sb("hT", [P, 2, P])
        xT_ps = s.ps("xT_ps", [P, 2, KT, P])
        h_ps = s.ps("h_ps", [P, 2, 512])
        hT_ps = s.ps("hT_ps", [P, 512])
        out_ps = s.ps("out_ps", [P, 2, D])
        w_in, iota_set, g_set = s.sem("w_in"), s.sem("iota"), s.sem("g_set")
        xn_ready, xT_made, xT_ready, h_ready = s.sem("xn"), s.sem("xT_made"), s.sem("xT_ready"), s.sem("h_ready")
        diffs, exps, hw_ready, hT_made, hT_ready = s.sem("diffs"), s.sem("exps"), s.sem("hw"), s.sem("hT_made"), s.sem("hT_ready")
        out_ready, x_new, chain, stats = s.sem("out_ready"), s.sem("x_new"), s.sem("chain"), s.sem("stats")
        norm = Norm(c, s)
        with nc.Block() as block:
            @block.sync
            def _(sp):
                sp.dma_start(a_sb[:, :, :], aT.rearrange("(k p) n -> p k n", p=P)).then_inc(w_in, 16)
                sp.dma_start(b_sb[:, :], bT).then_inc(w_in, 16)
                sp.dma_start(rb[:, :], router_b.rearrange("(o n) -> o n", o=1).to_broadcast([P, EXPERTS])).then_inc(w_in, 16)

            @block.gpsimd
            def _(pool):
                pool.iota(iota[:, :], [[1, EXPERTS]], base=0, channel_multiplier=0, allow_small_or_imprecise_dtypes=True).then_inc(iota_set, 1)


            @block.tensor
            def _(pe):
                pe.wait_ge(w_in, 48)

                def step(v, par, has):
                    if has(2):
                        need(pe, xn_ready, v + 3)
                        need(pe, xT_ready, v + 1)
                        for k in range(KT):
                            ins = pe.transpose(xT_ps[:, par, k, :], xn[:, par, P * k:P * k + P], c.ident[:, :])
                        ins.then_inc(xT_made, 1)
                    if has(0):
                        need(pe, hT_ready, v + 1)
                        need(pe, x_new, v)
                        pe.matmul(out_ps[:, par, :], hT[:, par, :], b_sb[:, :], start=True, stop=True).then_inc(out_ready, 1)
                    if has(2):
                        need(pe, xT_ready, v + 3)
                        need(pe, hw_ready, v + 1)
                        for k in range(KT):
                            ins = pe.matmul(h_ps[:, par, 0:ER + EXPERTS], xT[:, par, k, :], a_sb[:, k, :], start=(k == 0), stop=(k == KT - 1))
                        ins.then_inc(h_ready, 1)
                    if has(1):
                        need(pe, hw_ready, v + 2)
                        need(pe, hT_ready, v + 1)
                        pe.transpose(hT_ps[:, 0:P], hw[:, 1 - par, :], c.ident[:, :]).then_inc(hT_made, 1)

                pipelined(pe, step, 0, 3)

            @block.scalar
            def _(act):
                norm.act(act)
                act.wait_ge(norm.chain, Norm.STEPS)
                def step(v, par, has):
                    if has(2):
                        need(act, xT_made, v + 3)
                        need(act, h_ready, v + 1)
                        act.copy(xT[:, par, :, :], xT_ps[:, par, :, :]).then_inc(xT_ready, 1)
                    if has(3):
                        need(act, xT_made, v + 2)
                        t = bass.ds(v + 3, 1)
                        act.activation(xn[:, 1 - par, :], c.x[:, t, :].rearrange("p o d -> p (o d)"), ACT.Identity,
                                       bias=c.shift[:, t], scale=c.rstd[:, t]).then_inc(xn_ready, 1)
                    if has(1):
                        need(act, diffs, v + 2)
                        act.activation(ex[:, :], diff[:, :], ACT.Exp).then_inc(exps, 1)
                        need(act, hT_made, v + 2)
                        need(act, out_ready, v)
                        act.copy(hT[:, 1 - par, :], hT_ps[:, 0:P]).then_inc(hT_ready, 1)

                pipelined(act, step, 0, 3)

            @block.vector
            def _(dve):
                norm.dve(dve)
                dve.wait_ge(w_in, 48)
                dve.wait_ge(iota_set, 1)
                dve.tensor_scalar(g[:, :], c.gate[:, 4:5], SCALING0, None, ALU.mult).then_inc(g_set, 1)
                dve.wait_ge(g_set, 1)

                def step(v, par, has):
                    u = 1 - par
                    if has(1):
                        need(dve, h_ready, v + 2)
                        ch = Chain(dve, chain, v + 1, 8)
                        ch.step(dve.tensor_tensor(lg[:, :], h_ps[:, u, ER:ER + EXPERTS], rb[:, :], ALU.add))
                        dve.tensor_copy(diff[:, 0:1], lg[:, 0:1])
                        ch.step(dve.max(out=top[:, :], in_=lg[:, :]))
                        dve.tensor_tensor(diff[:, 0:1], top[:, 1:2], top[:, 0:1], ALU.subtract)
                        dve.tensor_tensor(diff[:, 1:2], top[:, 0:1], top[:, 1:2], ALU.subtract).then_inc(diffs, 1)
                        ch.step(dve.max_index(out=at_top[:, :], in_max=top[:, :], in_values=lg[:, :]))
                        ch.step(dve.tensor_copy(at_topf[:, :], at_top[:, :]))
                    if has(1):
                        need(dve, exps, v + 2)
                        ch.step(dve.tensor_scalar(ex[:, :], ex[:, :], 1.0, None, ALU.add))
                        ch.step(dve.reciprocal(ex[:, :], ex[:, :]))
                        dve.tensor_scalar(wt[:, 0, :], iota[:, :], at_topf[:, 0:1], ex[:, 0:1], ALU.is_equal, ALU.mult)
                        ch.step(dve.tensor_scalar(wt[:, 1, :], iota[:, :], at_topf[:, 1:2], ex[:, 1:2], ALU.is_equal, ALU.mult))
                        ch.step(dve.tensor_tensor(wt[:, 0, :], wt[:, 0, :], wt[:, 1, :], ALU.add))
                        need(dve, hT_made, v)
                        dve.tensor_tensor(hw[:, u, :].rearrange("p (e r) -> p e r", e=EXPERTS),
                                          h_ps[:, u, 0:ER].rearrange("p (e r) -> p e r", e=EXPERTS),
                                          spread(wt[:, 0, :], RANK0), ALU.mult).then_inc(hw_ready, 1)
                        ch.end()
                    if has(0):
                        need(dve, out_ready, v + 1)
                        dve.scalar_tensor_tensor(out=c.x[:, v, :], in0=out_ps[:, par, :], scalar=g[:, 0:1], in1=c.x[:, v, :],
                                                 op0=ALU.mult, op1=ALU.add).then_inc(x_new, 1)
                        need(dve, x_new, v + 1)
                        dve.bn_stats(c.stats[:, v, :], c.x[:, v, :]).then_inc(stats, 1)

                pipelined(dve, step, 0, 3)


KV, GROUP, HD1, MAX_POS, THETA = 8, 4, 128, 512, 10000.0
STEP = 4 * P
STEPS = B * S // STEP
KEEP, MASKED = 3.0e38, -1.0e9 * HD1 ** 0.5


XS = 256.0


def prepare_stage(c, pos, mask, tables, cosT, sinT, limit, ctxT, cT16, c_unit, xT16):
    nc = c.nc
    with Stage(nc, "rope") as s:
        pos_i = s.sb("pos_i", [P, PAIRS], I32)
        pos_f = s.sb("pos_f", [P, PAIRS])
        wrap = s.sb("wrap", [P, PAIRS])
        idx = s.sb("idx", [P, PAIRS], U32)
        rows = s.sb("rows", [P, PAIRS, 2 * HD1])
        m_i = s.sb("m_i", [P, PAIRS, S], I32)
        masked = s.sb("masked", [P, PAIRS, S])
        keep = s.sb("keep", [P, PAIRS, S])
        raw = s.sb("raw", [P, KT, B * S])
        mags = s.sb("mags", [P, KT + 2])
        c_scale = s.sb("c_scale", [P, 1])
        xn = s.sb("xn", [P, 2, D])
        xT_ps = s.ps("xT_ps", [P, 2, KT, P])
        xn_ready, xT_made, x_hi, x_lo = s.sem("xn"), s.sem("xT_made"), s.sem("x_hi"), s.sem("x_lo")
        t_ps = s.ps("t_ps", [P, 2, 4, P])
        p_in, m_in, chain, idx_ready = s.sem("p_in"), s.sem("m_in"), s.sem("chain"), s.sem("idx_ready")
        gathered, turned, out = s.sem("gathered"), s.sem("turned"), s.sem("out")
        c_in, maxed, reduced, scaled, c_hi, c_lo = s.sems("c_in", KT), s.sem("maxed"), s.sem("reduced"), s.sem("scaled"), s.sem("c_hi"), s.sem("c_lo")
        norm = Norm(c, s)
        with nc.Block() as block:
            @block.sync
            def _(sp):
                with nc.allow_non_contiguous_dma(reason="2048 positions, once"):
                    sp.dma_start(pos_i[:, :], pos.rearrange("(i b) s -> (b s) i", b=2)).then_inc(p_in, 16)
                sp.dma_start(m_i[:, :, :], mask.rearrange("(i b) q k -> (b q) i k", b=2)).then_inc(m_in, 16)
                for k in range(KT):
                    sp.dma_start(raw[:, k, :], ctxT[P * k:P * k + P, :]).then_inc(c_in[k], 16)

            @block.vector
            def _(dve):
                norm.dve(dve)
                dve.wait_ge(p_in, 16)
                ch = Chain(dve, chain)
                ch.step(dve.tensor_copy(pos_f[:, :], pos_i[:, :]))
                ch.step(dve.tensor_scalar(wrap[:, :], pos_f[:, :], 0.0, float(MAX_POS), ALU.is_lt, ALU.mult))
                ch.step(dve.tensor_tensor(pos_f[:, :], pos_f[:, :], wrap[:, :], ALU.add))
                ch.step(dve.tensor_scalar(pos_f[:, :], pos_f[:, :], 0.0, float(MAX_POS - 1), ALU.max, ALU.min))
                dve.tensor_copy(idx[:, :], pos_f[:, :]).then_inc(idx_ready, 1)

                with dve.Fori(0, TURNS) as j:
                    for u in range(2):
                        dve.wait_ge(x_hi, 2 * j + (u + 1))
                        cols = bass.ds((2 * j + u) * P, P)
                        dve.scalar_tensor_tensor(out=xT16[:, 1, :, cols], in0=xT_ps[:, u, :, :], scalar=XS, in1=xT16[:, 0, :, cols],
                                                 op0=ALU.mult, op1=ALU.subtract).then_inc(x_lo, 1)
                dve.wait_ge(m_in, 16)
                ch.step(dve.tensor_scalar(masked[:, :, :], m_i[:, :, :], 0.0, MASKED, ALU.is_equal, ALU.mult))
                ch.step(dve.tensor_scalar(keep[:, :, :], m_i[:, :, :], 0.0, KEEP, ALU.not_equal, ALU.mult))
                ch.step(dve.tensor_tensor(limit[:, :, :], keep[:, :, :], masked[:, :, :], ALU.add))
                for k in range(KT):
                    dve.wait_ge(c_in[k], 16)
                    ins = dve.tensor_reduce(mags[:, k:k + 1], raw[:, k, :], X, ALU.max, apply_absolute_value=True)
                ch.step(ins)
                dve.tensor_reduce(mags[:, KT:KT + 1], mags[:, 0:KT], X, ALU.max).then_inc(maxed, 1)
                dve.wait_ge(reduced, 1)
                ch.step(dve.tensor_scalar(mags[:, KT + 1:KT + 2], mags[:, KT + 1:KT + 2], TINY, None, ALU.max))
                ch.step(dve.tensor_scalar(c_unit, mags[:, KT + 1:KT + 2], 1 / TOP16, None, ALU.mult))
                dve.reciprocal(c_scale[:, :], c_unit).then_inc(scaled, 1)
                dve.wait_ge(scaled, 1)
                for k in range(KT):
                    dve.wait_ge(c_hi, k + 1)
                    dve.scalar_tensor_tensor(out=cT16[:, 1, k, :], in0=raw[:, k, :], scalar=c_scale[:, :], in1=cT16[:, 0, k, :],
                                             op0=ALU.mult, op1=ALU.subtract).then_inc(c_lo, 1)

            @block.gpsimd
            def _(pool):
                pool.wait_ge(idx_ready, 1)
                for i in range(PAIRS):
                    pool.indirect_dma_start(out=rows[:, i, :], out_offset=None, in_=tables,
                                            in_offset=bass.IndirectOffsetOnAxis(ap=idx[:, i:i + 1], axis=0)).then_inc(gathered, 16)
                pool.wait_ge(maxed, 1)
                pool.partition_all_reduce(mags[:, KT + 1:KT + 2], mags[:, KT:KT + 1], P, RMAX).then_inc(reduced, 1)

            @block.tensor
            def _(pe):
                def step(v, par, has):
                    need(pe, xn_ready, v + 2)
                    need(pe, x_lo, v)
                    for k in range(KT):
                        ins = pe.transpose(xT_ps[:, 1 - par, k, :], xn[:, 1 - par, P * k:P * k + P], c.ident[:, :])
                    ins.then_inc(xT_made, 1)

                pipelined(pe, step, 1, 1)
                pe.wait_ge(gathered, 16 * PAIRS)
                for i in range(PAIRS):
                    if i >= 2:
                        pe.wait_ge(out, i - 1)
                    for n in range(2):
                        ins = pe.transpose(t_ps[:, i % 2, n, :], rows[:, i, HD1 * n:HD1 * n + HD1], c.ident[:, :])
                    ins.then_inc(turned, 1)

            @block.scalar
            def _(act):
                norm.act(act)
                act.wait_ge(norm.chain, Norm.STEPS)

                def step(v, par, has):
                    if has(1):
                        need(act, xT_made, v)
                        t = bass.ds(v + 1, 1)
                        act.activation(xn[:, 1 - par, :], c.x[:, t, :].rearrange("p o d -> p (o d)"), ACT.Identity,
                                       bias=c.shift[:, t], scale=c.rstd[:, t]).then_inc(xn_ready, 1)
                    if has(0):
                        need(act, xT_made, v + 1)
                        act.activation(xT16[:, 0, :, bass.ds(v * P, P)], xT_ps[:, par, :, :], ACT.Copy, scale=XS).then_inc(x_hi, 1)

                pipelined(act, step, 0, 1)
                for i in range(PAIRS):
                    act.wait_ge(turned, i + 1)
                    act.copy(cosT[:, P * i:P * i + P], t_ps[:, i % 2, 0, :])
                    act.copy(sinT[:, P * i:P * i + P], t_ps[:, i % 2, 1, :]).then_inc(out, 1)
                act.wait_ge(scaled, 1)
                for k in range(KT):
                    act.activation(cT16[:, 0, k, :], raw[:, k, :], ACT.Copy, scale=c_scale[:, :]).then_inc(c_hi, 1)


def rope_tables():
    inv = (1.0 / np.float32(THETA) ** (np.arange(0, HD1, 2, dtype=np.float32) / np.float32(HD1))).astype(np.float32)
    f = np.arange(MAX_POS, dtype=np.float32)[:, None] * inv[None]
    cos, sin = np.cos(f).astype(np.float32), np.sin(f).astype(np.float32)
    return np.concatenate([cos, cos, -sin, sin], axis=1)


def grouped_attention_stage(c, wq, wk, wv, wo, cosT, sinT, limit, xT16, cT16, c_unit):
    nc = c.nc
    with Stage(nc, "gqa") as s:
        W_K, W_Q, W_V, W_O = range(4)
        SIZES = (KT * HD1, KT * GROUP * HD1, KT * HD1, GROUP * D)
        OFFS = [sum(SIZES[:n]) for n in range(4)]
        w16 = s.sb("w16", [P, 2, 2, sum(SIZES)], F16)
        raw = s.sb("raw", [P, max(SIZES)])
        mag = s.sb("mag", [P, 3])
        unit = s.sb("unit", [P, 3])
        fac = s.sb("fac", [P, 2, 4])
        cg = s.sb("cg", [P, 1])
        qk = s.sb("qk", [P, 1 + GROUP, STEP])
        v = s.sb("v", [P, 2, 4, HD1])
        sw = s.sb("sw", [P, 2, STEP])
        e = s.sb("e", [P, 4 * GROUP, S])
        mx = s.sb("mx", [P, 4 * GROUP])
        sm = s.sb("sm", [P, 4 * GROUP])
        probs = s.sb("probs", [P, 4 * GROUP, P])
        pT = s.sb("pT", [P, 2, GROUP * P])
        oT16 = s.sb("oT16", [P, 2, 2, GROUP, P], F16)
        proj_ps = s.ps("proj", [P, 2, STEP])
        s_ps = s.ps("scores", [P, 4, GROUP, S])
        t_ps = s.ps("pT_ps", [P, GROUP, P])
        o_ps = s.ps("o_ps", [P, GROUP, P])
        y_ps = s.ps("y_ps", [P, 2, D])
        raw_in, w_maxed, w_reduced, w_scaled, w_hi, w_lo = (s.sem(n) for n in ("raw_in", "w_maxed", "w_reduced", "w_scaled", "w_hi", "w_lo"))
        first_in = s.sems("first_in", 3)
        probs_zero, gated, w_chain = s.sem("probs_zero"), s.sem("gated"), s.sem("w_chain")
        filled, swapped, cosed, sined, roped = s.sem("filled"), s.sem("swapped"), s.sem("cosed"), s.sem("sined"), s.sem("roped")
        scored, bounded, shifted, exped, normed = s.sem("scored"), s.sem("bounded"), s.sem("shifted"), s.sem("exped"), s.sem("normed")
        turned, turned_out, headed, o_hi, o_lo = s.sem("turned"), s.sem("turned_out"), s.sem("headed"), s.sem("o_hi"), s.sem("o_lo")
        summed, added, chain, stats, maxed = s.sem("summed"), s.sem("added"), s.sem("chain"), s.sem("stats"), s.sem("maxed")
        GT = KV // 2
        R = 2 * STEPS
        FILLS, ROPES = 6, 5
        V_SCALE = 2.0 ** 14 / (KT * P * TOP16 * TOP16)

        def weight(gb, part, n, k, cols):
            width = SIZES[n] // KT
            return w16[:, gb, part, OFFS[n] + width * k + cols.start:OFFS[n] + width * k + cols.stop]

        def raw_of(t, n):
            if isinstance(t, int) and t in (W_K, W_V):
                return qk[:, t // 2, :]
            return raw[:, 0:SIZES[n]]

        def turns(eng, body):
            with eng.Fori(0, GT - 1) as j:
                for r in range(R):
                    body(R * j + r, r, 2, True)
            for r in range(R):
                body(R * (GT - 1) + r, r, R - 1 - r, r < STEPS)

        with nc.Block() as block:
            @block.sync
            def _(sp):
                def load(t, r, head):
                    n = r % 4
                    need(sp, w_lo, t)
                    if n == W_O:
                        src = wo.rearrange("(g h p) n -> p g h n", h=GROUP, p=P)[:, head, :, :]
                    else:
                        w = (wk, wq, wv)[n]
                        src = w.rearrange("(k p) n -> p k n", p=P)[:, :, bass.ts(head, SIZES[n] // KT)]
                    sp.dma_start(raw_of(t, n).rearrange("p (k n) -> p k n", k=KT), src).then_inc(raw_in, 16)

                for n in range(3):
                    source = (wk, wq, wv)[n].rearrange("(k p) n -> p k n", p=P)[:, :, 0:SIZES[n] // KT]
                    sp.dma_start(raw_of(n, n).rearrange("p (k n) -> p k n", k=KT), source).then_inc(first_in[n], 16)
                load(3, 3, 0)
                with sp.Fori(0, GT - 1) as j:
                    for r in range(R):
                        load(R * j + r + 4, r, 2 * j + (r // 4 + 1))
                for r in range(4):
                    load(R * (GT - 1) + r + 4, r, KV - 1)

            @block.tensor
            def _(pe):
                pe.wait_ge(probs_zero, 1)

                def project(t, r, n):
                    gb, step = r // STEPS, r % STEPS
                    if step == 0 and n in (0, 1, 5):
                        need(pe, w_lo, t + (1 if n == 0 else 2 if n == 1 else 3))
                    need(pe, swapped, FILLS * t + n - 1)
                    need(pe, cosed, ROPES * t + max(0, n - 1))
                    last = (KT - 1, SPLIT[-1])
                    for i in range(4 if n == 5 else 1):
                        for k in range(KT):
                            for pw, px in SPLIT:
                                flags = dict(start=(k, (pw, px)) == (0, SPLIT[0]), stop=(k, (pw, px)) == last)
                                cols = slice(STEP * step, STEP * step + STEP)
                                if n == 0:
                                    ins = pe.matmul(proj_ps[:, 0, :], weight(gb, pw, W_K, k, slice(0, HD1)), cT16[:, px, k, cols], **flags)
                                elif n < 5:
                                    ins = pe.matmul(proj_ps[:, n % 2, :], weight(gb, pw, W_Q, k, slice(HD1 * (n - 1), HD1 * n)), xT16[:, px, k, cols], **flags)
                                else:
                                    rows = slice(STEP * step + P * i, STEP * step + P * i + P)
                                    ins = pe.matmul(proj_ps[:, 1, HD1 * i:HD1 * i + HD1], cT16[:, pw, k, rows], weight(gb, px, W_V, k, slice(0, HD1)), **flags)
                    ins.then_inc(filled, 1)

                def scores(t):
                    need(pe, roped, ROPES * (t + 1))
                    need(pe, bounded, t)
                    for i in range(4):
                        for h in range(GROUP):
                            for b in range(2):
                                rows = slice(P * i + S * b, P * i + S * b + S)
                                ins = pe.matmul(s_ps[S * b:S * b + S, i, h, :], qk[:, 1 + h, rows], qk[:, 0, rows], start=True, stop=True)
                    ins.then_inc(scored, 1)

                def turn(t, i):
                    if i == 0:
                        need(pe, normed, 2 * t + 2)
                    need(pe, turned_out, 4 * t + i)
                    for h in range(GROUP):
                        ins = pe.transpose(t_ps[:, h, :], probs[:, GROUP * i + h, :], c.ident[:, :])
                    ins.then_inc(turned, 1)

                def attend(t, r, i):
                    if i == 0:
                        need(pe, swapped, FILLS * (t + 1))
                    need(pe, turned_out, 4 * t + i + 1)
                    need(pe, o_lo, 4 * t + i)
                    pe.matmul(o_ps[:, :, :], v[:, r % 2, i, :], pT[:, i % 2, :], start=True, stop=True).then_inc(headed, 1)

                def project_out(t, r, i):
                    if i == 0 and r % STEPS == 0:
                        need(pe, w_lo, t + 4)
                    need(pe, o_lo, 4 * t + i + 1)
                    need(pe, added, 4 * t + max(0, i - 1))
                    for h in range(GROUP):
                        for po, pw in SPLIT:
                            ins = pe.matmul(y_ps[:, i % 2, :], oT16[:, i % 2, po, h, :], weight(r // STEPS, pw, W_O, h, slice(0, D)),
                                            start=(h == 0 and (po, pw) == SPLIT[0]), stop=(h == GROUP - 1 and (po, pw) == SPLIT[-1]))
                    ins.then_inc(summed, 1)

                def body(t, r, more, prep):
                    def fill(ahead, n):
                        if more >= ahead:
                            project(t + ahead, (r + ahead) % R, n)

                    turn(t, 0)
                    fill(1, 3)
                    attend(t, r, 0)
                    turn(t, 1)
                    fill(1, 4)
                    attend(t, r, 1)
                    turn(t, 2)
                    project_out(t, r, 0)
                    attend(t, r, 2)
                    turn(t, 3)
                    project_out(t, r, 1)
                    if more:
                        scores(t + 1)
                    attend(t, r, 3)
                    project_out(t, r, 2)
                    fill(1, 5)
                    project_out(t, r, 3)
                    for n in range(3):
                        fill(2, n)

                for n in range(FILLS):
                    project(0, 0, n)
                scores(0)
                for n in range(3):
                    project(1, 1, n)
                turns(pe, body)

            @block.scalar
            def _(act):
                def split(t, r, gb):
                    n = r % 4
                    need(act, w_scaled, t + 1)
                    act.activation(w16[:, gb, 0, OFFS[n]:OFFS[n] + SIZES[n]], raw_of(t, n), ACT.Copy, scale=unit[:, 1:2]).then_inc(w_hi, 1)

                def read(t, r, n):
                    need(act, filled, FILLS * t + n + 1)
                    gb = r // STEPS
                    if n < ROPES:
                        par = (r + n) % 2
                        f = slice(W_K, W_K + 1) if n == 0 else slice(W_Q, W_Q + 1)
                        need(act, roped, ROPES * t + n - 1)
                        act.activation(sw[0:64, par, :], proj_ps[64:128, n % 2, :], ACT.Copy, scale=fac[64:128, gb, f])
                        act.activation(sw[64:128, par, :], proj_ps[0:64, n % 2, :], ACT.Copy, scale=fac[0:64, gb, f]).then_inc(swapped, 1)
                    else:
                        need(act, headed, 4 * (t - 1))
                        act.activation(v[:, r % 2, :, :], proj_ps[:, 1, :].rearrange("p (i d) -> p i d", i=4), ACT.Copy, scale=V_SCALE).then_inc(swapped, 1)

                def exps(t):
                    need(act, shifted, t + 1)
                    act.activation(e[:, :, :], e[:, :, :], ACT.Exp, scale=HD1 ** -0.5).then_inc(exped, 1)

                def body(t, r, more, prep):
                    def fill(ahead, n):
                        if more >= ahead:
                            read(t + ahead, (r + ahead) % R, n)

                    def turned_copy(i):
                        need(act, turned, 4 * t + i + 1)
                        need(act, headed, 4 * t + max(0, i - 1))
                        act.copy(pT[:, i % 2, :], t_ps[:, :, :].rearrange("p h q -> p (h q)")).then_inc(turned_out, 1)

                    def head(i):
                        need(act, headed, 4 * t + i + 1)
                        need(act, summed, 4 * t + max(0, i - 1))
                        act.copy(oT16[:, i % 2, 0, :, :], o_ps[:, :, :]).then_inc(o_hi, 1)

                    turned_copy(0)
                    fill(1, 3)
                    head(0)
                    turned_copy(1)
                    fill(1, 4)
                    head(1)
                    turned_copy(2)
                    head(2)
                    turned_copy(3)
                    head(3)
                    if more:
                        exps(t + 1)
                    if prep:
                        split(t + 4, r, 1 - r // STEPS)
                    fill(1, 5)
                    for n in range(3):
                        fill(2, n)

                for r in range(3):
                    split(r, r, 0)
                for n in range(FILLS):
                    read(0, 0, n)
                    if n == 3:
                        split(3, 3, 0)
                exps(0)
                for n in range(3):
                    read(1, 1, n)
                turns(act, body)

            @block.gpsimd
            def _(pool):
                pool.memset(probs[:, :, :], 0.0).then_inc(probs_zero, 1)

                def reduce(t):
                    need(pool, w_maxed, t + 1)
                    pool.tensor_tensor(mag[:, 2:3], mag[:, 0:1], mag[:, 0:1], ALU.add)
                    pool.partition_all_reduce(mag[:, 1:2], mag[:, 0:1], P, RMAX).then_inc(w_reduced, 1)

                def sin(t, r, n):
                    need(pool, swapped, FILLS * t + n + 1)
                    par = (r + n) % 2
                    pool.tensor_tensor(sw[:, par, :], sw[:, par, :], sinT[:, STEP * (r % STEPS):STEP * (r % STEPS) + STEP], ALU.mult).then_inc(sined, 1)

                def body(t, r, more, prep):
                    if more:
                        sin(t + 1, (r + 1) % R, 3)
                        sin(t + 1, (r + 1) % R, 4)
                    if prep:
                        reduce(t + 4)
                    for n in range(3):
                        if more > 1:
                            sin(t + 2, (r + 2) % R, n)

                for r in range(3):
                    reduce(r)
                for n in range(ROPES):
                    sin(0, 0, n)
                    if n == 1:
                        reduce(3)
                for n in range(3):
                    sin(1, 1, n)
                turns(pool, body)

            @block.vector
            def _(dve):
                dve.tensor_tensor(cg[:, :], c_unit, c.gate[:, 1:2], ALU.mult).then_inc(gated, 1)
                dve.wait_ge(gated, 1)

                WCH = 3

                def magnitude(t, r):
                    n = r % 4
                    if isinstance(t, int) and t < 3:
                        dve.wait_ge(first_in[t], 16)
                    else:
                        need(dve, raw_in, 16 * (t - 2))
                    dve.tensor_reduce(mag[:, 0:1], raw_of(t, n), X, ALU.max, apply_absolute_value=True).then_inc(w_maxed, 1)

                def scale(t, r, gb):
                    n = r % 4
                    need(dve, w_reduced, t + 1)
                    ch = Chain(dve, w_chain, t, WCH)
                    ch.step(dve.tensor_scalar(unit[:, 0:1], mag[:, 1:2], TINY, 1 / TOP16, ALU.max, ALU.mult))
                    f = fac[:, gb, n:n + 1]
                    if n == W_Q:
                        ins = dve.tensor_scalar(f, unit[:, 0:1], 1 / XS, None, ALU.mult)
                    elif n == W_K:
                        ins = dve.tensor_tensor(f, unit[:, 0:1], c_unit, ALU.mult)
                    elif n == W_V:
                        ins = dve.tensor_tensor(f, unit[:, 0:1], cg[:, :], ALU.mult)
                    else:
                        ins = dve.scalar_tensor_tensor(out=f, in0=unit[:, 0:1], scalar=1 / V_SCALE, in1=fac[:, gb, W_V:W_V + 1], op0=ALU.mult, op1=ALU.mult)
                    ch.step(ins)
                    ch.step(dve.reciprocal(unit[:, 1:2], unit[:, 0:1]))
                    ch.end()
                    dve.sem_inc(w_scaled, 1)

                def split(t, r, gb):
                    n = r % 4
                    cols = slice(OFFS[n], OFFS[n] + SIZES[n])
                    need(dve, w_hi, t + 1)
                    dve.scalar_tensor_tensor(out=w16[:, gb, 1, cols], in0=raw_of(t, n), scalar=unit[:, 1:2], in1=w16[:, gb, 0, cols],
                                             op0=ALU.mult, op1=ALU.subtract).then_inc(w_lo, 1)

                def rope(t, r, n):
                    cols = slice(STEP * (r % STEPS), STEP * (r % STEPS) + STEP)
                    need(dve, swapped, FILLS * t + n + 1)
                    if n == 0:
                        need(dve, scored, t)
                    f = W_K if n == 0 else W_Q
                    dve.scalar_tensor_tensor(out=qk[:, n, :], in0=proj_ps[:, n % 2, :], scalar=fac[:, r // STEPS, f:f + 1], in1=cosT[:, cols],
                                             op0=ALU.mult, op1=ALU.mult).then_inc(cosed, 1)
                    need(dve, sined, ROPES * t + n + 1)
                    need(dve, cosed, ROPES * t + n + 1)
                    dve.tensor_tensor(qk[:, n, :], qk[:, n, :], sw[:, (r + n) % 2, :], ALU.add).then_inc(roped, 1)

                def shift(t, r):
                    need(dve, scored, t + 1)
                    lim = limit[:, 4 * (r % STEPS):4 * (r % STEPS) + 4, :].unsqueeze(2).to_broadcast([P, 4, GROUP, S])
                    dve.tensor_tensor(e[:, :, :].rearrange("p (i h) k -> p i h k", h=GROUP), s_ps[:, :, :, :], lim, ALU.min).then_inc(bounded, 1)
                    need(dve, bounded, t + 1)
                    dve.tensor_reduce(mx[:, :], e[:, :, :], X, ALU.max).then_inc(maxed, 1)
                    need(dve, maxed, t + 1)
                    dve.tensor_tensor(e[:, :, :], e[:, :, :], spread(mx[:, :], S), ALU.subtract).then_inc(shifted, 1)

                def norm(t):
                    need(dve, exped, t + 1)
                    ch = Chain(dve, chain, t, 2)
                    ch.step(dve.tensor_reduce(sm[:, :], e[:, :, :], X, ALU.add))
                    ch.step(dve.reciprocal(sm[:, :], sm[:, :]))
                    ch.end()
                    need(dve, turned, 4 * t)
                    for b in range(2):
                        rows = slice(S * b, S * b + S)
                        dve.tensor_tensor(probs[rows, :, rows], e[rows, :, :], spread(sm[rows, :], S), ALU.mult).then_inc(normed, 1)

                def body(t, r, more, prep):
                    def fill(ahead, n):
                        if more >= ahead:
                            rope(t + ahead, (r + ahead) % R, n)

                    def low(i):
                        need(dve, o_hi, 4 * t + i + 1)
                        dve.tensor_tensor(oT16[:, i % 2, 1, :, :], o_ps[:, :, :], oT16[:, i % 2, 0, :, :], ALU.subtract).then_inc(o_lo, 1)

                    def add(i):
                        row = 4 * (r % STEPS) + i
                        need(dve, summed, 4 * t + i + 1)
                        dve.scalar_tensor_tensor(out=c.x[:, row, :], in0=y_ps[:, i % 2, :], scalar=fac[:, r // STEPS, W_O:W_O + 1], in1=c.x[:, row, :],
                                                 op0=ALU.mult, op1=ALU.add).then_inc(added, 1)
                        if isinstance(t, int) and r >= STEPS:
                            dve.wait_ge(added, 4 * t + i + 1)
                            dve.bn_stats(c.stats[:, row, :], c.x[:, row, :]).then_inc(stats, 1)

                    fill(1, 3)
                    low(0)
                    fill(1, 4)
                    low(1)
                    if prep:
                        magnitude(t + 4, r)
                    add(0)
                    low(2)
                    add(1)
                    if more:
                        shift(t + 1, (r + 1) % R)
                    if prep:
                        scale(t + 4, r, 1 - r // STEPS)
                    low(3)
                    add(2)
                    if more:
                        norm(t + 1)
                    if prep:
                        split(t + 4, r, 1 - r // STEPS)
                    add(3)
                    for n in range(3):
                        fill(2, n)

                for r in range(3):
                    magnitude(r, r)
                    scale(r, r, 0)
                    split(r, r, 0)
                for n in range(ROPES):
                    rope(0, 0, n)
                    if n == 1:
                        magnitude(3, 3)
                    if n == 2:
                        scale(3, 3, 0)
                split(3, 3, 0)
                shift(0, 0)
                rope(1, 1, 0)
                norm(0)
                rope(1, 1, 1)
                rope(1, 1, 2)
                turns(dve, body)


LORAS, RANK1, GROUPS1 = 16, 32, 8
NR = LORAS * RANK1
ROWS1 = B * S // GROUPS1
LR = 2 * RANK1


def lora_linear_stage(c, kernel, bias, gateT, pick, a_all, b_allT, a_sharedT, b_sharedT):
    nc = c.nc
    with Stage(nc, "lora") as s:
        NT, G = NR // P, GROUPS1
        w = s.sb("w", [P, KT, D])
        a_n = s.sb("a_n", [P, NT, D])
        b_n = s.sb("b_n", [P, NT, D])
        gate = s.sb("gate", [P, NT, G])
        eye = s.sb("eye", [P, RANK1])
        mix = s.sb("mix", [P, NT, G, RANK1])
        a_all_g = s.sb("a_all_g", [P, KT, G * RANK1])
        a_s = s.sb("a_s", [P, KT, RANK1])
        a_g = s.sb("a_g", [P, 2, KT, LR])
        b_g = s.sb("b_g", [LR + 1, G, D])
        xn = s.sb("xn", [P, 2, D])
        xT = s.sb("xT", [P, 2, KT, ROWS1])
        ax = s.sb("ax", [LR + 1, 2, ROWS1])
        mix_ps = s.ps("mix_ps", [P, 2, 512])
        xT_ps = s.ps("xT_ps", [P, 2, KT, P])
        ax_ps = s.ps("ax_ps", [P, 512])
        y_ps = s.ps("y_ps", [P, 2, D])
        gate_in, ab_in, shared_in, w_in = s.sem("gate_in"), s.sem("ab_in"), s.sem("shared_in"), s.sem("w_in")
        mixed, ones, shared_set = s.sem("mixed"), s.sem("ones"), s.sem("shared_set")
        a_made, a_out, b_made, b_out = s.sem("a_made"), s.sem("a_out"), s.sem("b_made"), s.sem("b_out")
        xn_ready, xT_made, xT_out = s.sem("xn"), s.sem("xT_made"), s.sem("xT_out")
        picked, ax_made, ax_out = s.sem("picked"), s.sem("ax_made"), s.sem("ax_out")
        summed, x_new, stats = s.sem("summed"), s.sem("x_new"), s.sem("stats")
        norm = Norm(c, s)
        with nc.Block() as block:
            @block.sync
            def _(sp):
                sp.dma_start(gate[:, :, :], gateT).then_inc(gate_in, 16)
                sp.dma_start(eye[:, :], pick).then_inc(gate_in, 16)
                sp.dma_start(a_n[:, :, :], a_all.rearrange("(k p) n -> p k n", p=P)).then_inc(ab_in, 16)
                sp.dma_start(b_n[:, :, :], b_allT.rearrange("(k p) n -> p k n", p=P)).then_inc(ab_in, 16)
                sp.dma_start(a_s[:, :, :], a_sharedT.rearrange("(k p) n -> p k n", p=P)).then_inc(shared_in, 16)
                sp.dma_start(b_g[RANK1:LR, :, :], b_sharedT.unsqueeze(1).to_broadcast([RANK1, G, D])).then_inc(shared_in, 16)
                sp.dma_start(b_g[LR:LR + 1, :, :], bias.rearrange("(o g n) -> o g n", o=1, g=1).to_broadcast([1, G, D])).then_inc(shared_in, 16)
                sp.dma_start(w[:, :, :], kernel.rearrange("(k p) n -> p k n", p=P)).then_inc(w_in, 16)


            @block.tensor
            def _(pe):
                pe.wait_ge(ab_in, 32)
                pe.wait_ge(mixed, 1)
                for k in range(KT):
                    for n in range(NT):
                        ins = pe.matmul(mix_ps[:, k // 2, G * RANK1 * (k % 2):G * RANK1 * (k % 2 + 1)], a_n[:, n, P * k:P * k + P],
                                        mix[:, n, :, :].rearrange("p g r -> p (g r)"), start=(n == 0), stop=(n == NT - 1))
                    ins.then_inc(a_made, 1)
                for half in range(2):
                    pe.wait_ge(a_out, half + 1)
                    for n in range(NT):
                        ins = pe.matmul(mix_ps[:, half, :], mix[:, n, 4 * half:4 * half + 4, :].rearrange("p g r -> p (g r)"), b_n[:, n, :],
                                        start=(n == 0), stop=(n == NT - 1))
                    ins.then_inc(b_made, 1)
                pe.wait_ge(w_in, 16)
                pe.wait_ge(shared_in, 48)
                pe.wait_ge(ones, 1)
                pe.wait_ge(b_out, G)

                def turn(g, u, i):
                    need(pe, xn_ready, 2 * g + i + 1)
                    need(pe, xT_out, 2 * g + i - 1)
                    for k in range(KT):
                        ins = pe.transpose(xT_ps[:, i, k, :], xn[:, i, P * k:P * k + P], c.ident[:, :])
                    ins.then_inc(xT_made, 1)

                def step(v, par, has):
                    if has(0):
                        need(pe, xT_out, 2 * v + 2)
                        need(pe, picked, v + 1)
                        need(pe, ax_out, v)
                        for k in range(KT):
                            ins = pe.matmul(ax_ps[0:LR, 0:ROWS1], a_g[:, par, k, :], xT[:, par, k, :], start=(k == 0), stop=(k == KT - 1))
                        ins.then_inc(ax_made, 1)
                    for i in range(2):
                        if has(1):
                            turn(v + 1, 1 - par, i)
                        if has(0):
                            need(pe, x_new, 2 * v + max(0, i - 1))
                            for k in range(KT):
                                pe.matmul(y_ps[:, i, :], xT[:, par, k, P * i:P * i + P], w[:, k, :], start=(k == 0), stop=False)
                            if i == 0:
                                need(pe, ax_out, v + 1)
                            pe.matmul(y_ps[:, i, :], ax[:, par, P * i:P * i + P], b_g[:, v, :], start=False, stop=True).then_inc(summed, 1)

                pipelined(pe, step, 0, 2, G)

            @block.gpsimd
            def _(pool):
                pool.wait_ge(shared_set, 2)
                pool.wait_ge(a_out, 2)

                def step(v, par, has):
                    if has(1):
                        need(pool, ax_made, v)
                        pool.tensor_copy(a_g[:, 1 - par, :, 0:RANK1], a_all_g[:, :, bass.ds((v + 1) * RANK1, RANK1)]).then_inc(picked, 1)

                pipelined(pool, step, 0, 2, G)

            @block.scalar
            def _(act):
                norm.act(act)
                act.wait_ge(a_made, 2)
                act.copy(a_all_g[:, 0:2, :], mix_ps[:, 0, :].rearrange("p (k n) -> p k n", k=2)).then_inc(a_out, 1)
                act.wait_ge(a_made, 4)
                act.copy(a_all_g[:, 2:4, :], mix_ps[:, 1, :].rearrange("p (k n) -> p k n", k=2)).then_inc(a_out, 1)
                act.wait_ge(shared_in, 48)
                for u in range(2):
                    act.copy(a_g[:, u, :, RANK1:LR], a_s[:, :, :]).then_inc(shared_set, 1)
                for g in range(G):
                    act.wait_ge(b_made, g // 4 + 1)
                    act.copy(b_g[0:RANK1, g, :], mix_ps[RANK1 * (g % 4):RANK1 * (g % 4 + 1), g // 4, :]).then_inc(b_out, 1)

                def step(v, par, has):
                    if has(0):
                        need(act, ax_made, v + 1)
                        need(act, summed, 2 * v)
                        act.copy(ax[0:LR, par, :], ax_ps[0:LR, 0:ROWS1]).then_inc(ax_out, 1)
                    if has(1):
                        for i in range(2):
                            need(act, xT_made, 2 * (v + 1) + i + 1)
                            need(act, summed, 2 * v)
                            act.copy(xT[:, 1 - par, :, P * i:P * i + P], xT_ps[:, i, :, :]).then_inc(xT_out, 1)

                pipelined(act, step, 0, 2, G)

            @block.vector
            def _(dve):
                norm.dve(dve)
                dve.memset(ax[LR:LR + 1, :, :], 1.0).then_inc(ones, 1)
                dve.wait_ge(gate_in, 32)
                dve.tensor_tensor(mix[:, :, :, :].rearrange("p n g r -> p (n g) r"), spread(gate[:, :, :].rearrange("p n g -> p (n g)"), RANK1),
                                  eye[:, :].unsqueeze(1).to_broadcast([P, NT * G, RANK1]), ALU.mult).then_inc(mixed, 1)

                def step(v, par, has):
                    for i in range(2):
                        if has(2):
                            need(dve, xT_made, 2 * (v + 1) + i + 1)
                            normalised(c, dve, xn[:, i, :], 2 * (v + 2) + i).then_inc(xn_ready, 1)
                        if has(0):
                            t = 2 * v + i
                            need(dve, summed, t + 1)
                            dve.scalar_tensor_tensor(out=c.x[:, t, :], in0=y_ps[:, i, :], scalar=c.gate[:, 5:6], in1=c.x[:, t, :],
                                                     op0=ALU.mult, op1=ALU.add).then_inc(x_new, 1)
                            need(dve, x_new, t + 1)
                            dve.bn_stats(c.stats[:, t, :], c.x[:, t, :]).then_inc(stats, 1)

                pipelined(dve, step, 0, 2, G)


TOP = 8
LOW = -3.0e38


def dft(n, rows):
    j, h = np.arange(rows)[:, None], n // 2
    return np.concatenate([np.cos(2 * np.pi * j * np.arange(h + 1) / n), -np.sin(2 * np.pi * j * np.arange(1, h) / n)], axis=1)


def swap_parts(m, n):
    h, out = n // 2, np.zeros_like(m)
    out[:, 1:h] = m[:, h + 1:]
    out[:, h + 1:] = m[:, 1:h]
    return out


def inverse_parts(n, cols):
    h = n // 2
    t, f = np.arange(cols)[None, :], np.arange(1, h)[:, None]
    cos, sin = 2 * np.cos(2 * np.pi * f * t / n), 2 * np.sin(2 * np.pi * f * t / n)
    one, alt = np.ones((1, cols)), np.cos(np.pi * np.arange(cols))[None]
    a = np.concatenate([one, cos, alt, cos]) / n
    b = np.concatenate([0 * one, -sin, 0 * alt, sin]) / n
    return a, b


def correlation_tables():
    two = lambda m: np.kron(np.eye(2), m)
    q = dft(S, S)
    ia, ib = inverse_parts(S, S)
    w = dft(2 * S, S)
    ends = dft(2 * S, 2 * S)
    v = np.concatenate([ends[:S - 1], ends[S - 1:].sum(0, keepdims=True)])
    va, vb = inverse_parts(2 * S, S)
    both = lambda m: np.concatenate([m, m])
    t = {"dft_q": two(q), "dft_qs": two(swap_parts(q, S)), "inv_a": two(ia), "inv_b": two(ib),
         "dft_w": both(w), "dft_v": both(v), "dft_vs": both(swap_parts(v, 2 * S)),
         "inv_v": np.concatenate([va, vb], axis=1)}
    return np.concatenate([t[k] for k in ("dft_q", "dft_qs", "inv_a", "inv_b", "dft_w", "dft_v", "dft_vs", "inv_v")], axis=1).astype(np.float32)


def correlation_stage(c, ctx_in, tables):
    nc = c.nc
    with Stage(nc, "corr") as s:
        m = s.sb("m", [P, 8, P])
        cin = s.sb("cin", [P, 2, 2, D])
        xn = s.sb("xn", [P, 2, D])
        kf = s.sb("kf", [P, D])
        pa = s.sb("pa", [P, 2, 2, D])
        top = s.sb("top", [P, 8, TOP])
        z = s.sb("z", [P, 8, S])
        cor = s.sb("cor", [P, 8, S])
        e = s.sb("e", [P, 8, S])
        te = s.sb("te", [P, 8, TOP])
        sm = s.sb("sm", [P, 8])
        wT = s.sb("wT", [P, D])
        wf = s.sb("wf", [P, 2, D])
        pv = s.sb("pv", [P, 2, 2, D])
        qf_ps = s.ps("qf", [P, 2, D])
        kf_ps = s.ps("kf_ps", [P, D])
        cor_ps = s.ps("cor_ps", [P, 8, S])
        wT_ps = s.ps("wT_ps", [P, D])
        vf_ps = s.ps("vf_ps", [P, 2, D])
        y_ps = s.ps("y_ps", [P, D])
        m_in, k_in, v_in, xn_ready = s.sem("m_in"), s.sems("k_in"), s.sems("v_in"), s.sem("xn")
        kf_made, kf_out, qf_made, qf_used = s.sem("kf_made"), s.sem("kf_out"), s.sem("qf_made"), s.sem("qf_used")
        cor_made, cor_out, chain, shifted, exped = s.sem("cor_made"), s.sem("cor_out"), s.sem("chain"), s.sem("shifted"), s.sem("exped")
        w_ready, wT_made, wT_out = s.sem("w_ready"), s.sem("wT_made"), s.sem("wT_out")
        wf_made, wf_out, vf_made, vf_used, summed, x_new, stats = (s.sem(n) for n in ("wf_made", "wf_out", "vf_made", "vf_used", "summed", "x_new", "stats"))
        norm = Norm(c, s)
        with nc.Block() as block:
            @block.sync
            def _(sp):
                sp.dma_start(m[:, :, :], tables.rearrange("p (n f) -> p n f", n=8)).then_inc(m_in, 16)
                rows = rows_of(ctx_in)
                for u in range(2):
                    sp.dma_start(cin[:, 0, u, :], rows[:, u, :]).then_inc(k_in[u], 16)
                for u in range(2):
                    sp.dma_start(cin[:, 1, u, :], rows[:, u, :]).then_inc(v_in[u], 16)
                with sp.Fori(0, TURNS - 1) as j:
                    for u in range(2):
                        sp.wait_ge(kf_made, j * 2 + (u + 1))
                        sp.dma_start(cin[:, 0, u, :], rows[:, 2 * j + u + 2, :]).then_inc(k_in[u], 16)
                        sp.wait_ge(vf_made, j * 4 + (2 * u + 2))
                        sp.dma_start(cin[:, 1, u, :], rows[:, 2 * j + u + 2, :]).then_inc(v_in[u], 16)


            @block.tensor
            def _(pe):
                pe.wait_ge(m_in, 16)

                def values(p, par, b):
                    half = slice(S * b, S * b + S)
                    need(pe, v_in[par], (p - par) * 8 + 16)
                    need(pe, vf_used, p * 2 + b)
                    for n in range(2):
                        ins = pe.matmul(vf_ps[:, n, :], m[half, 5 + n, :], cin[half, 1, par, :], start=True, stop=True)
                    ins.then_inc(vf_made, 1)

                def weights(p, b, keys):
                    half = slice(S * b, S * b + S)
                    need(pe, wT_out, p + 1)
                    need(pe, kf_out, keys)
                    need(pe, wf_out, p * 2 + b)
                    pe.matmul(kf_ps[:, :], m[half, 4, :], wT[half, :], start=True, stop=True).then_inc(wf_made, 1)

                def step(i, par, has):
                    if has(0):
                        need(pe, w_ready, i + 1)
                        need(pe, wT_out, i)
                        for k in range(KT):
                            ins = pe.transpose(wT_ps[:, P * k:P * k + P], e[:, 2 * k:2 * k + 2, :].rearrange("p a b -> p (a b)"), c.ident[:, :])
                        ins.then_inc(wT_made, 1)
                    if has(1):
                        need(pe, qf_used, i * 2 + 4)
                        need(pe, cor_out, i + 1)
                        for k in range(KT):
                            for n in range(2):
                                ins = pe.matmul(cor_ps[:, 2 * k:2 * k + 2, :].rearrange("p a b -> p (a b)"), pa[:, 1 - par, n, P * k:P * k + P], m[:, 2 + n, :],
                                                start=(n == 0), stop=(n == 1))
                        ins.then_inc(cor_made, 1)
                    if has(0):
                        weights(i, 0, i + 2 if not isinstance(i, int) else min(i + 2, PAIRS))
                        values(i, par, 0)
                    if has(2):
                        p = i + 2
                        need(pe, k_in[par], (p - par) * 8 + 16)
                        need(pe, kf_out, p)
                        need(pe, wf_out, 2 * i + 1)
                        pe.matmul(kf_ps[:, :], m[:, 0, :], cin[:, 0, par, :], start=True, stop=True).then_inc(kf_made, 1)
                        need(pe, xn_ready, p + 1)
                        need(pe, qf_used, p * 2)
                        for n in range(2):
                            ins = pe.matmul(qf_ps[:, n, :], m[:, n, :], xn[:, par, :], start=True, stop=True)
                        ins.then_inc(qf_made, 1)
                    if has(0):
                        weights(i, 1, i + 3 if not isinstance(i, int) else min(i + 3, PAIRS))
                        values(i, par, 1)
                        for b in range(2):
                            need(pe, vf_used, i * 2 + b + 1)
                            need(pe, x_new, i)
                            for n in range(2):
                                ins = pe.matmul(y_ps[S * b:S * b + S, :], m[:, 7, S * n:S * n + S], pv[:, b, n, :], start=(n == 0), stop=(n == 1))
                        ins.then_inc(summed, 1)

                pipelined(pe, step, 0, 2)

            @block.scalar
            def _(act):
                norm.act(act)
                def weights(p, b):
                    need(act, wf_made, p * 2 + b + 1)
                    need(act, vf_used, p * 2)
                    act.copy(wf[:, b, :], kf_ps[:, :]).then_inc(wf_out, 1)

                def step(i, par, has):
                    if has(0):
                        need(act, wT_made, i + 1)
                        need(act, wf_made, i * 2)
                        act.copy(wT[:, :], wT_ps[:, :]).then_inc(wT_out, 1)
                    if has(1):
                        need(act, cor_made, i + 2)
                        need(act, w_ready, i + 1)
                        act.copy(cor[:, :, :], cor_ps[:, :, :]).then_inc(cor_out, 1)
                    if has(0):
                        weights(i, 0)
                    if has(2):
                        need(act, kf_made, i + 3)
                        need(act, qf_used, i * 2 + 4)
                        act.copy(kf[:, :], kf_ps[:, :]).then_inc(kf_out, 1)
                    if has(1):
                        need(act, shifted, i + 2)
                        act.activation(te[:, :, :], te[:, :, :], ACT.Exp).then_inc(exped, 1)
                        act.activation(e[:, :, :], e[:, :, :], ACT.Exp).then_inc(exped, 1)
                    if has(0):
                        weights(i, 1)

                pipelined(act, step, 0, 2)

            @block.vector
            def _(dve):
                norm.dve(dve)
                def values(p, b):
                    need(dve, vf_made, p * 2 + b + 1)
                    need(dve, wf_out, p * 2 + b + 1)
                    need(dve, summed, p)
                    dve.tensor_tensor(pv[:, b, :, :], vf_ps[:, :, :], wf[:, b:b + 1, :].to_broadcast([P, 2, D]), ALU.mult).then_inc(vf_used, 1)

                def step(i, par, has):
                    if has(2):
                        need(dve, qf_made, i + 1)
                        normalised(c, dve, xn[:, par, :], i + 2).then_inc(xn_ready, 1)
                    if has(1):
                        ch = Chain(dve, chain, i + 1, 6)
                        need(dve, cor_out, i + 2)
                        need(dve, wT_made, i + 1)
                        dve.tensor_copy(sm[:, 0:1], cor[:, 0, 0:1])
                        for g in range(8):
                            ins = dve.max(out=top[:, g, :], in_=cor[:, g, :])
                        ch.step(ins)
                        dve.tensor_tensor(te[:, :, :], top[:, :, :], spread(top[:, :, 0], TOP), ALU.subtract)
                        dve.tensor_tensor(e[:, :, :], cor[:, :, :], spread(top[:, :, 0], S), ALU.subtract).then_inc(shifted, 1)
                        for g in range(8):
                            ins = dve.match_replace(out=z[:, g, :], in_to_replace=top[:, g, :], in_values=cor[:, g, :], imm_value=LOW)
                        ch.step(ins)
                        ch.step(dve.tensor_tensor(z[:, :, :], cor[:, :, :], z[:, :, :], ALU.not_equal))
                    if has(0):
                        values(i, 0)
                    if has(2):
                        need(dve, qf_made, i + 3)
                        need(dve, kf_out, i + 3)
                        need(dve, cor_made, i + 1)
                        for n in range(2):
                            dve.tensor_tensor(pa[:, par, n, :], qf_ps[:, n, :], kf[:, :], ALU.mult).then_inc(qf_used, 1)
                    if has(1):
                        need(dve, exped, i * 2 + 4)
                        ch.step(dve.tensor_reduce(sm[:, :], te[:, :, :], X, ALU.add))
                        ch.step(dve.reciprocal(sm[:, :], sm[:, :]))
                        ch.step(dve.tensor_tensor(e[:, :, :], e[:, :, :], z[:, :, :], ALU.mult))
                        dve.tensor_tensor(e[:, :, :], e[:, :, :], spread(sm[:, :], S), ALU.mult).then_inc(w_ready, 1)
                        ch.end()
                    if has(0):
                        values(i, 1)
                        need(dve, summed, i + 1)
                        dve.scalar_tensor_tensor(out=c.x[:, i, :], in0=y_ps[:, :], scalar=c.gate[:, 2:3], in1=c.x[:, i, :],
                                                 op0=ALU.mult, op1=ALU.add).then_inc(x_new, 1)
                        need(dve, x_new, i + 1)
                        dve.bn_stats(c.stats[:, i, :], c.x[:, i, :]).then_inc(stats, 1)

                pipelined(dve, step, 0, 2)


FP8_MAX = 448.0
EXP_BITS = 0x7F800000


def fp8_linear_stage(c, w8T, w_scale, bias16):
    nc = c.nc
    with Stage(nc, "fp8") as s:
        xn = s.sb("xn", [P, PAIRS, D])
        mags = s.sb("mags", [P, PAIRS])
        amax, amax_all, sc = s.sb("amax", [P, 1]), s.sb("amax_all", [P, 1]), s.sb("sc", [P, 4])
        w_raw = s.sb("w_raw", [P, KT, D], U8)
        w_int = s.sb("w_int", [P, KT, D], I32)
        w_t = s.sb("w_t", [P, KT, D], I32)
        w_a = s.sb("w_a", [P, KT, D])
        w = s.sb("w", [P, KT, D], BF16)
        bias = s.sb("bias", [P, D], BF16)
        ws = s.sb("ws", [P, 1])
        y = s.sb("y", [P, 2, D])
        unit = s.sb("unit", [P, 2, D])
        q = s.sb("q", [P, 2, D], BF16)
        xT = s.sb("xT", [P, 2, KT, P], BF16)
        o16 = s.sb("o16", [P, 2, D], BF16)
        xT_ps = s.ps("xT_ps", [P, 2, 2 * KT, P], BF16)
        y_ps = s.ps("y_ps", [P, 2, D])
        w_in, b_in, chain, maxed, scaled = s.sem("w_in"), s.sem("b_in"), s.sem("chain"), s.sem("maxed"), s.sem("scaled")
        xn_made, w_made, reduced = s.sem("xn_made"), s.sem("w_made"), s.sem("reduced")
        x_scaled, stats = s.sem("x_scaled"), s.sem("stats")
        bounded, united, q_ready, lchain = s.sem("bounded"), s.sem("united"), s.sem("q_ready"), s.sem("lchain")
        xT_made, xT_out, summed, out_ready, x_new = (s.sem(n) for n in ("xT_made", "xT_out", "summed", "out_ready", "x_new"))
        norm = Norm(c, s)
        with nc.Block() as block:
            @block.sync
            def _(sp):
                sp.dma_start(w_raw[:, :, :], w8T.rearrange("(k p) n -> p k n", p=P)).then_inc(w_in, 16)
                sp.dma_start(bias[:, :], bias16.rearrange("(o n) -> o n", o=1).to_broadcast([P, D])).then_inc(b_in, 16)
                sp.dma_start(ws[:, :], w_scale.rearrange("(o n) -> o n", o=1).to_broadcast([P, 1])).then_inc(b_in, 16)

            @block.gpsimd
            def _(pool):
                pool.wait_ge(maxed, 1)
                pool.partition_all_reduce(amax_all[:, :], amax[:, :], P, RMAX).then_inc(reduced, 1)
                pool.wait_ge(scaled, 1)

                def step(v, par, has):
                    if has(0):
                        need(pool, out_ready, v + 1)
                        pool.tensor_tensor(o16[:, par, :], o16[:, par, :], bias[:, :], ALU.add).then_inc(bounded, 1)

                pipelined(pool, step, 0, 2)

            @block.vector
            def _(dve):
                norm.dve(dve)
                for t in range(PAIRS):
                    dve.wait_ge(xn_made, t + 1)
                    ins = dve.tensor_reduce(mags[:, t:t + 1], xn[:, t, :], X, ALU.max, apply_absolute_value=True)
                ch = Chain(dve, chain)
                ch.step(ins)
                dve.tensor_reduce(amax[:, :], mags[:, :], X, ALU.max).then_inc(maxed, 1)
                dve.wait_ge(w_in, 16)
                ch.step(dve.tensor_copy(w_int[:, :, :], w_raw[:, :, :]))
                ch.step(dve.tensor_scalar(w_t[:, :, :], w_int[:, :, :], 0x7F, 20, ALU.bitwise_and, ALU.logical_shift_left))
                ch.step(dve.tensor_scalar(w_t[:, :, :], w_t[:, :, :], 0x40000000, None, ALU.bitwise_or))
                ch.step(dve.tensor_scalar(w_a[:, :, :], w_t[:, :, :].bitcast(F32), 2.0 ** -7, -2.0 ** -6, ALU.mult, ALU.add))
                ch.step(dve.scalar_tensor_tensor(out=w_a[:, :, :], in0=w_t[:, :, :].bitcast(F32), scalar=2.0 ** -8, in1=w_a[:, :, :],
                                                 op0=ALU.mult, op1=ALU.min))
                ch.step(dve.tensor_scalar(w_int[:, :, :], w_int[:, :, :], 0x80, 24, ALU.bitwise_and, ALU.logical_shift_left))
                ch.step(dve.tensor_tensor(w_int[:, :, :], w_int[:, :, :], w_a[:, :, :].bitcast(I32), ALU.bitwise_or))
                ch.step(dve.tensor_copy(w[:, :, :], w_int[:, :, :].bitcast(F32)))
                dve.sem_inc(w_made, 1)
                dve.wait_ge(reduced, 1)
                dve.wait_ge(b_in, 32)
                ch.step(dve.tensor_scalar(sc[:, 0:1], amax_all[:, :], 1.0 / FP8_MAX, 1e-12, ALU.mult, ALU.max))
                ch.step(dve.reciprocal(sc[:, 1:2], sc[:, 0:1]))
                dve.tensor_tensor(sc[:, 2:3], sc[:, 0:1], ws[:, :], ALU.mult).then_inc(scaled, 1)
                dve.wait_ge(scaled, 1)

                def step(v, par, has):
                    if has(1):
                        u = 1 - par
                        need(dve, x_scaled, v + 2)
                        lc = Chain(dve, lchain, v + 1, 3)
                        lc.step(dve.tensor_scalar(y[:, u, :], y[:, u, :], FP8_MAX, -FP8_MAX, ALU.min, ALU.max))
                        lc.step(dve.tensor_scalar(unit[:, u, :].bitcast(I32), y[:, u, :].bitcast(I32), EXP_BITS, None, ALU.bitwise_and))
                        lc.step(dve.tensor_scalar(unit[:, u, :], unit[:, u, :], 2.0 ** -6, 1.5 * 2.0 ** 20, ALU.max, ALU.mult))
                        dve.tensor_tensor(y[:, u, :], y[:, u, :], unit[:, u, :], ALU.add).then_inc(united, 1)
                        need(dve, united, v + 2)
                        need(dve, xT_made, v)
                        dve.tensor_tensor(q[:, u, :], y[:, u, :], unit[:, u, :], ALU.subtract).then_inc(q_ready, 1)
                        lc.end()
                    if has(0):
                        need(dve, bounded, v + 1)
                        dve.scalar_tensor_tensor(out=c.x[:, v, :], in0=o16[:, par, :], scalar=c.gate[:, 6:7], in1=c.x[:, v, :],
                                                 op0=ALU.mult, op1=ALU.add).then_inc(x_new, 1)
                        need(dve, x_new, v + 1)
                        dve.bn_stats(c.stats[:, v, :], c.x[:, v, :]).then_inc(stats, 1)

                pipelined(dve, step, 0, 2)

            @block.tensor
            def _(pe):
                pe.wait_ge(w_made, 1)

                def step(v, par, has):
                    if has(1):
                        u = 1 - par
                        need(pe, q_ready, v + 2)
                        need(pe, xT_out, v)
                        for k in range(KT):
                            ins = pe.transpose(xT_ps[:, u, k, :], q[:, u, P * k:P * k + P], c.identb[:, :])
                        ins.then_inc(xT_made, 1)
                        need(pe, xT_out, v + 2)
                        need(pe, out_ready, v)
                        for k in range(KT):
                            ins = pe.matmul(y_ps[:, u, :], xT[:, u, k, :], w[:, k, :], start=(k == 0), stop=(k == KT - 1))
                        ins.then_inc(summed, 1)

                pipelined(pe, step, 0, 2)

            @block.scalar
            def _(act):
                norm.act(act)
                act.wait_ge(norm.chain, Norm.STEPS)
                for t in range(PAIRS):
                    act.activation(xn[:, t, :], c.x[:, t, :], ACT.Identity, bias=c.shift[:, t:t + 1], scale=c.rstd[:, t:t + 1]).then_inc(xn_made, 1)
                act.wait_ge(scaled, 1)

                def step(v, par, has):
                    if has(2):
                        need(act, q_ready, v + 1)
                        act.activation(y[:, par, :], xn[:, v + 2, :], ACT.Copy, scale=sc[:, 1:2]).then_inc(x_scaled, 1)
                    if has(1):
                        u = 1 - par
                        need(act, xT_made, v + 2)
                        need(act, summed, v)
                        act.copy(xT[:, u, :, :], xT_ps[:, u, 0:KT, :]).then_inc(xT_out, 1)
                        need(act, summed, v + 2)
                        need(act, x_new, v)
                        act.activation(o16[:, u, :], y_ps[:, u, :], ACT.Copy, scale=sc[:, 2:3]).then_inc(out_ready, 1)

                pipelined(act, step, 0, 2)


HEADS3, HD3, LQ, LKV = 16, 32, 64, 32


def latent_attention_stage(c, ctxT, wq_dT, w_qk, wkv_d4, wv_u):
    nc = c.nc
    with Stage(nc, "mla") as s:
        HT = HEADS3 * LKV // P
        wq = s.sb("wq", [P, KT, LQ])
        wqk = s.sb("wqk", [LQ, HEADS3 * LKV])
        wkv = s.sb("wkv", [P, KT, P])
        wv = s.sb("wv", [LKV, D])
        xn = s.sb("xn", [P, 2, D])
        xT = s.sb("xT", [P, 2, KT, P])
        cT = s.sb("cT", [P, 2, KT, P])
        cq = s.sb("cq", [LQ, 2, P])
        ql = s.sb("ql", [P, 2, HT, P])
        kl = s.sb("kl", [LKV, 2, P])
        kbd = s.sb("kbd", [P, 2, 2, 4, S])
        v = s.sb("v", [P, 2, D])
        d = s.sb("d", [P, HEADS3, S])
        mx = s.sb("mx", [P, HEADS3])
        e = s.sb("e", [P, 2, HEADS3, P])
        sm = s.sb("sm", [P, HEADS3])
        inv = s.sb("inv", [P, 2, HEADS3])
        oT = s.sb("oT", [P, HT, P])
        eT = s.sb("eT", [P, 2, 4, P])
        o = s.sb("o", [P, D])
        a_ps = s.ps("a_ps", [P, KT, P])
        b_ps = s.ps("b_ps", [P, 4, P])
        v_ps = s.ps("v_ps", [P, D])
        s_ps = s.ps("s_ps", [P, HEADS3, S])
        t_ps = s.ps("t_ps", [P, 2, 4, P])
        o_ps = s.ps("o_ps", [P, HT, P])
        w_in, c_in, zeros = s.sem("w_in"), s.sems("c_in"), s.sem("zeros")
        xn_ready, xT_made, xT_out, lat_made, lat_out = (s.sem(n) for n in ("xn", "xT_made", "xT_out", "lat_made", "lat_out"))
        ql_made, ql_out, v_made, v_out = (s.sem(n) for n in ("ql_made", "ql_out", "v_made", "v_out"))
        scored, maxed, shifted, exped, sums, chain = (s.sem(n) for n in ("scored", "maxed", "shifted", "exped", "sums", "chain"))
        turned, turned_out, summed, divided, x_new = (s.sem(n) for n in ("turned", "turned_out", "summed", "divided", "x_new"))
        oT_out, backed, stats = s.sem("oT_out"), s.sem("backed"), s.sem("stats")
        norm = Norm(c, s)
        with nc.Block() as block:
            @block.sync
            def _(sp):
                sp.dma_start(wq[:, :, :], wq_dT.rearrange("(k p) n -> p k n", p=P)).then_inc(w_in, 16)
                sp.dma_start(wqk[:, :], w_qk).then_inc(w_in, 16)
                sp.dma_start(wkv[:, :, :], wkv_d4.rearrange("(k p) n -> p k n", p=P)).then_inc(w_in, 16)
                sp.dma_start(wv[:, :], wv_u).then_inc(w_in, 16)
                cols = ctxT.rearrange("(k p) n -> p k n", p=P)
                for u in range(2):
                    sp.dma_start(cT[:, u, :, :], cols[:, :, P * u:P * u + P]).then_inc(c_in[u], 16)
                with sp.Fori(0, TURNS - 1) as j:
                    for u in range(2):
                        sp.wait_ge(lat_made, j * 2 + (u + 1))
                        sp.dma_start(cT[:, u, :, :], cols[:, :, bass.ds((2 * j + u + 2) * P, P)]).then_inc(c_in[u], 16)


            @block.tensor
            def _(pe):
                pe.wait_ge(w_in, 64)
                pe.wait_ge(zeros, 2)

                def turn(p, par, n):
                    if n == 0:
                        need(pe, exped, p + 1)
                    if n == 1:
                        need(pe, divided, p)
                    else:
                        need(pe, turned_out, p * 4 + max(0, n - 1))
                    for h in range(4):
                        ins = pe.transpose(t_ps[:, (n + 1) % 2, h, :], e[:, par, 4 * n + h, :], c.ident[:, :])
                    ins.then_inc(turned, 1)

                def weigh(p, par, n):
                    need(pe, turned_out, p * 4 + n + 1)
                    if n == 0:
                        need(pe, oT_out, p)
                        need(pe, v_out, p + 1)
                    for h in range(4):
                        cols = slice(HD3 * (4 * n + h), HD3 * (4 * n + h) + HD3)
                        ins = pe.matmul(o_ps[HD3 * h:HD3 * h + HD3, n, :], v[:, par, cols], eT[:, n % 2, h, :], start=True, stop=True)
                    ins.then_inc(summed, 1)

                def step(i, par, has):
                    p = i + 2
                    if has(1):
                        u = 1 - par
                        need(pe, ql_out, i + 2)
                        need(pe, shifted, i + 1)
                        for b in range(2):
                            for n in range(HT):
                                ins = pe.matmul(s_ps[S * b:S * b + S, 4 * n:4 * n + 4, :].rearrange("p h k -> p (h k)"), ql[:, u, n, S * b:S * b + S],
                                                kbd[:, u, b, :, :].rearrange("p h k -> p (h k)"), start=True, stop=True)
                        ins.then_inc(scored, 1)
                    if has(-1):
                        need(pe, oT_out, i)
                        need(pe, turned_out, 4 * i)
                        for n in range(HT):
                            ins = pe.transpose(t_ps[:, 0, n, :], oT[:, n, :], c.ident[:, :])
                        ins.then_inc(backed, 1)
                    if has(0):
                        turn(i, par, 0)
                    if has(2):
                        need(pe, xn_ready, p + 1)
                        need(pe, ql_out, p)
                        for k in range(KT):
                            ins = pe.transpose(a_ps[:, k, :], xn[:, par, P * k:P * k + P], c.ident[:, :])
                        ins.then_inc(xT_made, 1)
                    if has(0):
                        turn(i, par, 1)
                        weigh(i, par, 0)
                    if has(2):
                        need(pe, xT_out, p + 1)
                        need(pe, c_in[par], (p - par) * 8 + 16)
                        need(pe, lat_out, p)
                        for k in range(KT):
                            pe.matmul(b_ps[0:LQ, 0, :], wq[:, k, :], xT[:, par, k, :], start=(k == 0), stop=(k == KT - 1))
                        for k in range(KT):
                            ins = pe.matmul(b_ps[:, 1, :], wkv[:, k, :], cT[:, par, k, :], start=(k == 0), stop=(k == KT - 1))
                        ins.then_inc(lat_made, 1)
                    if has(0):
                        turn(i, par, 2)
                        weigh(i, par, 1)
                    if has(2):
                        need(pe, lat_out, p + 1)
                        for n in range(HT):
                            ins = pe.matmul(a_ps[:, n, :], wqk[:, P * n:P * n + P], cq[:, par, :], start=True, stop=True)
                        ins.then_inc(ql_made, 1)
                        need(pe, v_out, p)
                        pe.matmul(v_ps[:, :], kl[:, par, :], wv[:, :], start=True, stop=True).then_inc(v_made, 1)
                    if has(0):
                        turn(i, par, 3)
                        weigh(i, par, 2)
                        weigh(i, par, 3)

                pipelined(pe, step, -1, 2)

            @block.scalar
            def _(act):
                norm.act(act)
                act.wait_ge(zeros, 2)

                def turned_copy(p, n):
                    need(act, turned, p * 4 + n + 1)
                    need(act, summed, p * 4 + max(0, n - 1))
                    act.copy(eT[:, n % 2, :, :], t_ps[:, (n + 1) % 2, :, :]).then_inc(turned_out, 1)

                def step(i, par, has):
                    p = i + 2
                    if has(-1):
                        need(act, summed, 4 * i)
                        need(act, backed, i - 1)
                        act.copy(oT[:, :, :], o_ps[:, :, :]).then_inc(oT_out, 1)
                    if has(0):
                        turned_copy(i, 0)
                    if has(2):
                        need(act, xT_made, p + 1)
                        act.copy(xT[:, par, :, :], a_ps[:, :, :]).then_inc(xT_out, 1)
                    if has(0):
                        turned_copy(i, 1)
                    if has(2):
                        need(act, lat_made, p + 1)
                        need(act, v_made, p - 1)
                        need(act, scored, p - 1)
                        act.copy(cq[:, par, :], b_ps[0:LQ, 0, :])
                        act.copy(kl[:, par, :], b_ps[0:LKV, 1, :])
                        for h in range(4):
                            part = slice(LKV * h, LKV * h + LKV)
                            ins = act.copy(kbd[part, par, :, h, :], b_ps[part, 1, :].rearrange("p (b k) -> p b k", b=2))
                        ins.then_inc(lat_out, 1)
                    if has(0):
                        turned_copy(i, 2)
                    if has(2):
                        need(act, ql_made, p + 1)
                        act.copy(ql[:, par, :, :], a_ps[:, :, :]).then_inc(ql_out, 1)
                    if has(0):
                        turned_copy(i, 3)
                    if has(1):
                        u = 1 - par
                        need(act, shifted, i + 2)
                        need(act, sums, i)
                        need(act, turned, 4 * i)
                        for b in range(2):
                            half = slice(S * b, S * b + S)
                            ins = act.activation(e[half, u, :, half], d[half, :, :], ACT.Exp, scale=LKV ** -0.5)
                        ins.then_inc(exped, 1)
                    if has(2):
                        need(act, v_made, p + 1)
                        need(act, summed, 4 * (p - 1))
                        act.copy(v[:, par, :], v_ps[:, :]).then_inc(v_out, 1)

                pipelined(act, step, -1, 2)

            @block.vector
            def _(dve):
                norm.dve(dve)
                dve.memset(kbd[:, :, :, :, :], 0.0).then_inc(zeros, 1)
                dve.memset(e[:, :, :, :], 0.0).then_inc(zeros, 1)

                def step(i, par, has):
                    if has(2):
                        need(dve, xT_made, i + 1)
                        normalised(c, dve, xn[:, par, :], i + 2).then_inc(xn_ready, 1)
                    if has(-1):
                        q = i - 1
                        need(dve, backed, i)
                        dve.tensor_tensor(o[:, :].rearrange("p (h d) -> p h d", h=HEADS3), t_ps[:, 0, :, :].rearrange("p n (h d) -> p (n h) d", h=4),
                                          spread(inv[:, 1 - par, :], HD3), ALU.mult).then_inc(divided, 1)
                    if has(1):
                        need(dve, scored, i + 2)
                        dve.tensor_reduce(mx[:, :], s_ps[:, :, :], X, ALU.max).then_inc(maxed, 1)
                        need(dve, maxed, i + 2)
                        need(dve, exped, i + 1)
                        dve.tensor_tensor(d[:, :, :], s_ps[:, :, :], spread(mx[:, :], S), ALU.subtract).then_inc(shifted, 1)
                    if has(-1):
                        need(dve, divided, i)
                        dve.scalar_tensor_tensor(out=c.x[:, q, :], in0=o[:, :], scalar=c.gate[:, 3:4], in1=c.x[:, q, :],
                                                 op0=ALU.mult, op1=ALU.add).then_inc(x_new, 1)
                        need(dve, x_new, i)
                        dve.bn_stats(c.stats[:, q, :], c.x[:, q, :]).then_inc(stats, 1)
                    if has(0):
                        need(dve, exped, i + 1)
                        for b in range(2):
                            half = slice(S * b, S * b + S)
                            ins = dve.tensor_reduce(sm[half, :], e[half, par, :, half], X, ALU.add)
                        ins.then_inc(sums, 1)
                        need(dve, sums, i + 1)
                        dve.reciprocal(inv[:, par, :], sm[:, :]).then_inc(chain, 1)
                        need(dve, chain, i + 1)

                pipelined(dve, step, -1, 2)


HIDDEN, RANK3 = 1376, 16
H_TILES = [(P * n, min(P, HIDDEN - P * n)) for n in range(-(-HIDDEN // P))]


def swiglu_stage(c, gate_wT, up_wT, down_wT, gate_a, gate_bT, up_a, up_bT, down_a, down_bT, out):
    nc = c.nc
    with Stage(nc, "glu") as s:
        NH = len(H_TILES)
        w = s.sb("w", [P, 2, KT, HIDDEN])
        w16 = s.sb("w16", [P, 2, 2, KT, HIDDEN], F16)
        mags = s.sb("mags", [P, 2, KT + 2])
        scale = s.sb("scale", [P, 2])
        unit = s.sb("unit", [P, 2])
        wd = s.sb("wd", [P, NH, D])
        a = s.sb("a", [RANK3, 2, D])
        b = s.sb("b", [RANK3, 2, HIDDEN])
        da = s.sb("da", [RANK3, HIDDEN])
        db = s.sb("db", [RANK3, D])
        xn = s.sb("xn", [P, 2, D])
        xT16 = s.sb("xT16", [P, 2, KT, STEP], F16)
        g = s.sb("g", [P, 2, STEP])
        h = s.sb("h", [P, 2, STEP])
        p_ps = s.ps("p_ps", [P, 4, STEP])
        y_ps = s.ps("y_ps", [P, 4, D])
        w_in, lora_in = s.sems("w_in", 3), s.sem("lora_in")
        fold_made, folded = s.sem("fold_made"), s.sem("folded")
        xn_ready, xT_made, xT_out = (s.sem(n) for n in ("xn", "xT_made", "xT_out"))
        projected, silued, h_ready, downed, x_new, stored = (s.sem(n) for n in ("projected", "silued", "h_ready", "downed", "x_new", "stored"))
        maxed, reduced, scaled, w_chain = s.sem("maxed"), s.sem("reduced"), s.sem("scaled"), s.sem("w_chain")
        w_hi, w_lo, xT_lo = s.sem("w_hi"), s.sem("w_lo"), s.sem("xT_lo")
        pieces = [(n, k, c0, min(512, HIDDEN - c0)) for n in range(2) for k in range(KT) for c0 in range(0, HIDDEN, 512)]
        FOLDS = len(pieces) + NH

        def fold_ps(f):
            return p_ps[:, f % 8, :] if f % 8 < 4 else y_ps[:, f % 8 - 4, :]

        def xT_in_ps(i):
            return p_ps[:, 2 + i % 2, :].rearrange("p (k r) -> p k r", k=KT)

        norm = Norm(c, s)
        with nc.Block() as block:
            @block.sync
            def _(sp):
                for n, (x_a, x_b) in enumerate(((gate_a, gate_bT), (up_a, up_bT))):
                    sp.dma_start(a[:, n, :], x_a).then_inc(lora_in, 16)
                    sp.dma_start(b[:, n, :], x_b).then_inc(lora_in, 16)
                sp.dma_start(da[:, :], down_a).then_inc(lora_in, 16)
                sp.dma_start(db[:, :], down_bT).then_inc(lora_in, 16)
                for n, m in enumerate((gate_wT, up_wT)):
                    sp.dma_start(w[:, n, :, :], m.rearrange("(k p) n -> p k n", p=P)).then_inc(w_in[n], 16)
                full = (NH - 1) * P
                sp.dma_start(wd[:, 0:NH - 1, :], down_wT[0:full, :].rearrange("(n p) d -> p n d", p=P)).then_inc(w_in[2], 16)
                sp.dma_start(wd[0:HIDDEN - full, NH - 1, :], down_wT[full:HIDDEN, :]).then_inc(w_in[2], 16)
                rows = rows_of(out)
                with sp.Fori(0, STEPS) as j:
                    for i in range(4):
                        sp.wait_ge(x_new, j * 4 + i + 1)
                        sp.dma_start(rows[:, 4 * j + i, :], c.x[:, 4 * j + i, :]).then_inc(stored, 16)
                sp.wait_ge(stored, 16 * PAIRS)

            @block.vector
            def _(dve):
                norm.dve(dve)
                ch = Chain(dve, w_chain)

                def fold(f):
                    dve.wait_ge(fold_made, f + 1)
                    if f < len(pieces):
                        n, k, c0, wid = pieces[f]
                        dve.wait_ge(w_in[n], 16)
                        dst, rows = w[:, n, k, c0:c0 + wid], P
                    else:
                        t = f - len(pieces)
                        dve.wait_ge(w_in[2], 32)
                        rows, wid = H_TILES[t][1], D
                        dst = wd[0:rows, t, :]
                    dve.tensor_tensor(dst, dst, fold_ps(f)[0:rows, 0:wid], ALU.add).then_inc(folded, 1)

                def magnitude(n):
                    dve.wait_ge(folded, (n + 1) * len(pieces) // 2)
                    for k in range(KT):
                        ins = dve.tensor_reduce(mags[:, n, k:k + 1], w[:, n, k, :], X, ALU.max, apply_absolute_value=True)
                    ch.step(ins)
                    dve.tensor_reduce(mags[:, n, KT:KT + 1], mags[:, n, 0:KT], X, ALU.max).then_inc(maxed, 1)

                def scales(n):
                    dve.wait_ge(reduced, n + 1)
                    ch.step(dve.tensor_scalar(unit[:, n:n + 1], mags[:, n, KT + 1:KT + 2], TINY, 1 / TOP16, ALU.max, ALU.mult))
                    ch.step(dve.reciprocal(scale[:, n:n + 1], unit[:, n:n + 1]))
                    dve.tensor_scalar(unit[:, n:n + 1], unit[:, n:n + 1], 1 / XS, None, ALU.mult).then_inc(scaled, 1)

                def low(n):
                    for k in range(KT):
                        dve.wait_ge(w_hi, n * KT + k + 1)
                        dve.scalar_tensor_tensor(out=w16[:, n, 1, k, :], in0=w[:, n, k, :], scalar=scale[:, n:n + 1], in1=w16[:, n, 0, k, :],
                                                 op0=ALU.mult, op1=ALU.subtract).then_inc(w_lo, 1)

                def norm_rows(g, i):
                    need(dve, xT_made, 4 * g + max(0, i - 1))
                    normalised(c, dve, xn[:, i % 2, :], 4 * g + i).then_inc(xn_ready, 1)

                def xT_low(g, i):
                    need(dve, xT_out, 4 * g + i + 1)
                    rows = slice(P * i, P * i + P)
                    dve.scalar_tensor_tensor(out=xT16[:, 1, :, rows], in0=xT_in_ps(i), scalar=XS, in1=xT16[:, 0, :, rows],
                                             op0=ALU.mult, op1=ALU.subtract).then_inc(xT_lo, 1)

                norm_rows(0, 0)
                norm_rows(0, 1)
                for i in range(4):
                    xT_low(0, i)
                    if i < 2:
                        norm_rows(0, i + 2)
                half = len(pieces) // 2
                for f in range(half):
                    fold(f)
                magnitude(0)
                for f in range(half, 2 * half):
                    fold(f)
                scales(0)
                magnitude(1)
                low(0)
                scales(1)
                low(1)
                for f in range(2 * half, FOLDS):
                    fold(f)
                dve.wait_ge(scaled, 2)

                def body(j, more):
                    for n in range(NH):
                        rows = H_TILES[n][1]
                        dve.wait_ge(silued, j * NH + n + 1)
                        need(dve, downed, j * NH + max(0, n - 1))
                        dve.scalar_tensor_tensor(out=h[0:rows, n % 2, :], in0=p_ps[0:rows, 2 * (n % 2) + 1, :], scalar=unit[0:rows, 1:2], in1=g[0:rows, n % 2, :],
                                                 op0=ALU.mult, op1=ALU.mult).then_inc(h_ready, 1)
                        if more and n in (4, 5):
                            norm_rows(j + 1, n - 4)
                    for i in range(4):
                        if more:
                            xT_low(j + 1, i)
                            if i < 2:
                                norm_rows(j + 1, i + 2)
                    for i in range(4):
                        t = 4 * j + i
                        dve.wait_ge(downed, j * NH + NH)
                        dve.scalar_tensor_tensor(out=c.x[:, t, :], in0=y_ps[:, i, :], scalar=c.gate[:, 7:8], in1=c.x[:, t, :],
                                                 op0=ALU.mult, op1=ALU.add).then_inc(x_new, 1)

                with dve.Fori(0, STEPS - 1) as j:
                    body(j, True)
                body(STEPS - 1, False)

            @block.gpsimd
            def _(pool):
                for n in range(2):
                    pool.wait_ge(maxed, n + 1)
                    pool.partition_all_reduce(mags[:, n, KT + 1:KT + 2], mags[:, n, KT:KT + 1], P, RMAX).then_inc(reduced, 1)

            @block.scalar
            def _(act):
                norm.act(act)
                def xT_high(g, i):
                    need(act, xT_made, 4 * g + i + 1)
                    act.activation(xT16[:, 0, :, P * i:P * i + P], xT_in_ps(i), ACT.Copy, scale=XS).then_inc(xT_out, 1)

                for i in range(4):
                    xT_high(0, i)
                for n in range(2):
                    act.wait_ge(scaled, n + 1)
                    for k in range(KT):
                        act.activation(w16[:, n, 0, k, :], w[:, n, k, :], ACT.Copy, scale=scale[:, n:n + 1]).then_inc(w_hi, 1)

                def body(j, more):
                    for n in range(NH):
                        rows = H_TILES[n][1]
                        act.wait_ge(projected, j * NH + n + 1)
                        need(act, h_ready, j * NH + max(0, n - 1))
                        act.activation(g[0:rows, n % 2, :], p_ps[0:rows, 2 * (n % 2), :], ACT.Silu, scale=unit[0:rows, 0:1]).then_inc(silued, 1)
                    if more:
                        for i in range(4):
                            xT_high(j + 1, i)

                with act.Fori(0, STEPS - 1) as j:
                    body(j, True)
                body(STEPS - 1, False)

            @block.tensor
            def _(pe):
                def turn(g, i):
                    need(pe, xn_ready, 4 * g + i + 1)
                    need(pe, xT_lo, 4 * g + max(0, i - 1))
                    for k in range(KT):
                        ins = pe.transpose(p_ps[:, 2 + i % 2, P * k:P * k + P], xn[:, i % 2, P * k:P * k + P], c.ident[:, :])
                    ins.then_inc(xT_made, 1)

                def project(j, n):
                    c0, rows = H_TILES[n]
                    need(pe, h_ready, j * NH + max(0, n - 1))
                    if n == 0:
                        need(pe, xT_lo, 4 * j + 4)
                    for m in range(2):
                        for k in range(KT):
                            for pw, px in SPLIT:
                                ins = pe.matmul(p_ps[0:rows, 2 * (n % 2) + m, :], w16[:, m, pw, k, c0:c0 + rows], xT16[:, px, k, :],
                                                start=(k == 0 and (pw, px) == SPLIT[0]), stop=(k == KT - 1 and (pw, px) == SPLIT[-1]))
                    ins.then_inc(projected, 1)

                def down(j, n):
                    rows = H_TILES[n][1]
                    pe.wait_ge(h_ready, j * NH + n + 1)
                    if n == 0:
                        need(pe, x_new, 4 * j)
                    for i in range(4):
                        ins = pe.matmul(y_ps[:, i, :], h[0:rows, n % 2, P * i:P * i + P], wd[0:rows, n, :], start=(n == 0), stop=(n == NH - 1))
                    ins.then_inc(downed, 1)

                def body(j, more):
                    project(j, 0)
                    for n in range(1, NH):
                        project(j, n)
                        down(j, n - 1)
                    if more:
                        for i in range(4):
                            turn(j + 1, i)
                    down(j, NH - 1)

                for i in range(4):
                    turn(0, i)
                pe.wait_ge(lora_in, 96)
                pe.wait_ge(xT_lo, 4)
                for f in range(FOLDS):
                    if f >= 8:
                        pe.wait_ge(folded, f - 7)
                    if f < len(pieces):
                        n, k, c0, wid = pieces[f]
                        ins = pe.matmul(fold_ps(f)[:, 0:wid], a[:, n, P * k:P * k + P], b[:, n, c0:c0 + wid], start=True, stop=True)
                    else:
                        c0, rows = H_TILES[f - len(pieces)]
                        ins = pe.matmul(fold_ps(f)[0:rows, :], da[:, c0:c0 + rows], db[:, :], start=True, stop=True)
                    ins.then_inc(fold_made, 1)
                pe.wait_ge(folded, FOLDS)
                pe.wait_ge(w_lo, 2 * KT)
                with pe.Fori(0, STEPS - 1) as j:
                    body(j, True)
                body(STEPS - 1, False)


def store_stage(c, out):
    nc = c.nc
    with Stage(nc, "store") as s:
        stored = s.sem("stored")
        with nc.Block() as block:
            @block.sync
            def _(sp):
                for q in range(4):
                    sp.dma_start(rows_of(out)[:, 4 * q:4 * q + 4, :], c.x[:, 4 * q:4 * q + 4, :]).then_inc(stored, 16)
                sp.wait_ge(stored, 64)


def program(nc, a, out, first=0, last=7):
    with ExitStack() as ctx:
        c = Core(nc, ctx)
        load_stage(c, a["x"], a["g_xattn"], a["g_ffn"])
        for n in range(first, last + 1):
            STAGES[n](c, {**a, "out": out})
        if last < 7:
            store_stage(c, out)


def _window(c, a):
    window_attention_stage(c, a["ctx"], a["w0T"], a["b0"], a["sum_heads"], a["expand_heads"])


def _moe(c, a):
    lora_mixture_stage(c, a["a0T"], a["b0T"], a["router_b"])


def _gqa(c, a):
    with Stage(c.nc, "gqa_in") as s:
        cosT, sinT = s.sb("cosT", [P, B * S]), s.sb("sinT", [P, B * S])
        limit = s.sb("limit", [P, PAIRS, S])
        xT16, cT16 = s.sb("xT16", [P, 2, KT, B * S], F16), s.sb("cT16", [P, 2, KT, B * S], F16)
        unit = s.sb("c_unit", [P, 1])
        prepare_stage(c, a["pos"], a["mask"], a["rope"], cosT, sinT, limit, a["ctxT"], cT16, unit[:, :], xT16)
        grouped_attention_stage(c, a["w1q"], a["w1k"], a["w1v"], a["w1o"], cosT, sinT, limit, xT16, cT16, unit[:, :])


def _lora(c, a):
    lora_linear_stage(c, a["w1"], a["b1"], a["gate1"], a["eye32"], a["a1"], a["b1T"], a["a1sT"], a["b1sT"])


def _corr(c, a):
    correlation_stage(c, a["ctx"], a["dfts"])


def _fp8(c, a):
    fp8_linear_stage(c, a["w8T"], a["w8_scale"], a["b8"])


def _mla(c, a):
    latent_attention_stage(c, a["ctxT"], a["wq_d"], a["w_qk"], a["wkv_d4"], a["wv_u"])


def _glu(c, a):
    swiglu_stage(c, *[a[k] for k in ("gate_wT", "up_wT", "down_wT", "gate_a", "gate_bT", "up_a", "up_bT", "down_a", "down_bT")], a["out"])


STAGES = (_window, _moe, _gqa, _lora, _corr, _fp8, _mla, _glu)


def layouts(i):
    t = lambda w: np.ascontiguousarray(np.asarray(w).T)
    m = {"x": np.asarray(i["x"]), "ctx": np.asarray(i["ctx_4096"]), "g_xattn": np.asarray(i["g_xattn"]), "g_ffn": np.asarray(i["g_ffn"])}
    m["w0T"] = np.ascontiguousarray(np.stack([t(i[f"L0_xattn_W{k}"]) for k in "qkvo"], axis=1))
    m["b0"] = np.tile(np.stack([np.asarray(i[f"L0_xattn_b{k}"]) for k in "qkvo"], axis=1), (2, 1))
    m["a0T"] = t(np.concatenate([np.asarray(i["L0_ffn_A"]).reshape(ER, D), np.asarray(i["L0_ffn_router_w"])]))
    m["b0T"] = np.ascontiguousarray(np.asarray(i["L0_ffn_Bm"]).transpose(0, 2, 1).reshape(ER, D))
    m["pos"], m["mask"] = np.asarray(i["pos_BxS2"]), np.asarray(i["mask_BxSxS2_ik0"])
    m["rope"] = rope_tables()
    m["ctxT"] = t(np.asarray(i["ctx_4096"]).reshape(B * S, D))
    for k in "qkvo":
        m[f"w1{k}"] = np.asarray(i[f"L1_xattn_W{k}"])
    m["w1"], m["b1"] = np.asarray(i["L1_ffn_kernel"]), np.asarray(i["L1_ffn_bias"])
    m["gate1"] = np.ascontiguousarray(np.repeat(np.asarray(i["L1_ffn_gate"]).T, RANK1, axis=0).reshape(4, P, GROUPS1).transpose(1, 0, 2))
    m["eye32"] = np.tile(np.eye(RANK1, dtype=np.float32), (4, 1))
    m["a1"] = np.asarray(i["L1_ffn_lora_A"]).reshape(NR, D)
    m["b1T"] = np.ascontiguousarray(np.asarray(i["L1_ffn_lora_B"]).transpose(0, 2, 1).reshape(NR, D))
    m["a1sT"], m["b1sT"] = t(i["L1_ffn_lora_A_shared"]), t(i["L1_ffn_lora_B_shared"])
    m["dfts"] = correlation_tables()
    m["w8T"] = t(np.asarray(i["L2_ffn_weight_fp8"]).view(np.uint8))
    m["w8_scale"] = np.asarray(i["L2_ffn_weight_scale"]).reshape(1)
    m["b8"] = np.asarray(i["L2_ffn_bias"])
    m["wq_d"], m["w_qk"], m["wv_u"] = (np.asarray(i[f"L3_xattn_{k}"]) for k in ("Wq_d", "W_qk", "Wv_u"))
    m["wkv_d4"] = np.tile(np.asarray(i["L3_xattn_Wkv_d"]), (1, 4))
    for k in ("gate_w", "up_w", "down_w", "gate_b", "up_b", "down_b"):
        m[f"{k}T"] = t(i[f"L3_ffn_{k}"])
    for k in ("gate_a", "up_a", "down_a"):
        m[k] = np.asarray(i[f"L3_ffn_{k}"])
    m["router_b"] = np.asarray(i["L0_ffn_router_b"])
    m.update(window_tables())
    return m


def window_tables():
    p = np.arange(P)
    head = p // HD0
    sums = np.zeros((P, 2, 32), np.float32)
    expand = np.zeros((BLOCK, PARTS, BH, BLOCK, P), np.float32)
    for par in range(2):
        sums[p, par, BH * par + head] = 1
    for shift in range(BLOCK):
        for part in range(PARTS):
            expand[shift, part, head, shift, p] = 1 / PROB_SCALE
    return {"sum_heads": sums, "expand_heads": expand.reshape(P, BLOCK, P)}


def kernel(**inputs):
    import concourse.bacc as bacc
    from concourse.bass_utils import run_bass_kernel_spmd

    nc = bacc.Bacc("TRN2", target_bir_lowering=False, num_devices=1)
    arrays = layouts(inputs)
    aps = {name: nc.dram_tensor(name, v.shape, mybir.dt.from_np(v.dtype), kind="ExternalInput").ap() for name, v in arrays.items()}
    out = nc.dram_tensor("y", (B, S, D), F32, kind="ExternalOutput").ap()
    program(nc, aps, out)
    return run_bass_kernel_spmd(nc, [arrays], core_ids=[0]).results[0]["y"]
```
